# Optimizing a Trainium2 kernel written in Bass

```python
import numpy as np
import jax
import jax.numpy as jnp

def _softmax(x, axis=-1):
    return jax.nn.softmax(x, axis=axis)

def _gelu(x):
    return jax.nn.gelu(x, approximate=True)

def _silu(x):
    return jax.nn.silu(x)

def _sigmoid(x):
    return jax.nn.sigmoid(x)

def _layernorm(x, axis=-1, eps=1e-05):
    m = jnp.mean(x, axis=axis, keepdims=True)
    v = jnp.var(x, axis=axis, keepdims=True)
    return (x - m) / jnp.sqrt(v + eps)

def _scatter_add(tgt, idx, src, axis=0):
    return tgt.at[idx].add(src)

def _segment_sum(src, seg, n):
    return jax.ops.segment_sum(src, seg, n)
kernel_name = 'mk_gnn_resnorm_d2_gnn_r32_7b82ed'

def setup_inputs(seed: int=0):
    np.random.seed(seed)
    _w = jnp.asarray

    def _rec_inputs():
        import jax
        import jax.numpy as jnp
        _gk = jax.random.key(seed)
        x = -0.0005121 + 1.001 * jax.random.normal(jax.random.fold_in(_gk, 1), (3125, 64), jnp.float32)
        src = jax.random.randint(jax.random.fold_in(_gk, 2), (100000,), 0, 3125, jnp.int32)
        dst = jax.random.randint(jax.random.fold_in(_gk, 3), (100000,), 0, 3125, jnp.int32)
        _o = jnp.argsort(dst, stable=True)
        src = src[_o]
        dst = dst[_o]
        edge_attr_64 = 0.000189758 + 1.00013 * jax.random.normal(jax.random.fold_in(_gk, 12), (100000, 64), jnp.float32)
        edge_attr_9 = 0.000739051 + 0.999958 * jax.random.normal(jax.random.fold_in(_gk, 13), (100000, 9), jnp.float32)
        return (x, src, dst, edge_attr_64, edge_attr_9)
    x, src, dst, edge_attr_64, edge_attr_9 = _rec_inputs()

    def _L0_gnn_setup():
        import jax, jax.numpy as jnp
        import numpy as np
        N_NODES = 50000
        N_EDGES = 25000
        D = 64
        NUM_GRAPHS = 64
        IN_DIM = 3 * D
        K = 64

        def swish(x):
            return x * jax.nn.sigmoid(x)
        key = jax.random.key(seed)
        ks = jax.random.split(key, 9)
        x = jax.random.normal(ks[0], (N_NODES, D), dtype=jnp.float32)
        edge_index = jax.random.randint(ks[1], (2, N_EDGES), 0, N_NODES, dtype=jnp.int64)
        edge_attr = jax.random.normal(ks[2], (N_EDGES, D), dtype=jnp.float32)
        u = jax.random.normal(ks[3], (NUM_GRAPHS, D), dtype=jnp.float32)
        batch = jnp.sort(jax.random.randint(ks[4], (N_NODES,), 0, NUM_GRAPHS, dtype=jnp.int64))
        s1 = 1.0 / np.sqrt(IN_DIM)
        s2 = 1.0 / np.sqrt(K)
        W1 = jax.random.uniform(ks[5], (IN_DIM, K), minval=-s1, maxval=s1, dtype=jnp.float32)
        b1 = jax.random.uniform(ks[6], (K,), minval=-s1, maxval=s1, dtype=jnp.float32)
        W2 = jax.random.uniform(ks[7], (K, K), minval=-s2, maxval=s2, dtype=jnp.float32)
        b2 = jax.random.uniform(ks[8], (K,), minval=-s2, maxval=s2, dtype=jnp.float32)
        return {'x': x, 'edge_index': edge_index, 'edge_attr': edge_attr, 'u': u, 'batch': batch, 'W1': W1, 'b1': b1, 'W2': W2, 'b2': b2}
    _L0_gnn_all = _L0_gnn_setup()
    _L0_gnn_in = {k: v for k, v in _L0_gnn_all.items() if k in ('u', 'W1', 'b1', 'W2', 'b2')}
    del _L0_gnn_all

    def _L1_gnn_setup():
        import jax, jax.numpy as jnp
        import numpy as np
        N, E = (10000, 10000)
        D, S, HE = (64, 9, 64)
        H, DQK, DV = (8, 16, 16)
        OK, OV = (H * DQK, H * DV)
        EPS_BN = 1e-05

        def tensor_product(x_e, sh, w, C):
            acc = sh[:, 0:1] * (x_e @ C[:, 0, :])
            for s in range(1, S):
                acc = acc + sh[:, s:s + 1] * (x_e @ C[:, s, :])
            return acc * w

        def mlp2(x, w1, b1, w2, b2):
            return jax.nn.relu(x @ w1 + b1) @ w2 + b2
        key = jax.random.key(seed)
        ks = jax.random.split(key, 20)
        g = lambda k, shape, fan: jax.random.normal(k, shape, jnp.float32) / np.float32(np.sqrt(fan))
        return {'tfn_features': jax.random.normal(ks[0], (N, D), jnp.float32), 'edge_features': jax.random.normal(ks[1], (E, HE), jnp.float32), 'edge_sh': jax.random.normal(ks[2], (E, S), jnp.float32), 'Wq': g(ks[3], (D, OK), D), 'Cqk': g(ks[4], (D, S, OK), D * S), 'Cv': g(ks[5], (D, S, OV), D * S), 'k_w1': g(ks[6], (HE, HE), HE), 'k_b1': jnp.zeros((HE,), jnp.float32), 'k_w2': g(ks[7], (HE, OK), HE), 'k_b2': jnp.zeros((OK,), jnp.float32), 'v_w1': g(ks[8], (HE, HE), HE), 'v_b1': jnp.zeros((HE,), jnp.float32), 'v_w2': g(ks[9], (HE, OV), HE), 'v_b2': jnp.zeros((OV,), jnp.float32), 'W_out': g(ks[10], (OV, D), OV), 'W_self': g(ks[11], (D, D), D), 'gamma': jnp.ones((D,), jnp.float32), 'beta': jnp.zeros((D,), jnp.float32), 'edge_index': jax.random.randint(ks[12], (2, E), 0, N, dtype=jnp.int32)}
    _L1_gnn_all = _L1_gnn_setup()
    _L1_gnn_in = {k: v for k, v in _L1_gnn_all.items() if k in ('Wq', 'Cqk', 'Cv', 'k_w1', 'k_b1', 'k_w2', 'k_b2', 'v_w1', 'v_b1', 'v_w2', 'v_b2', 'W_out', 'W_self', 'gamma', 'beta')}
    del _L1_gnn_all
    return {'x': x, 'src': src, 'dst': dst, 'edge_attr_64': edge_attr_64, 'edge_attr_9': edge_attr_9, 'L0_gnn_u': _L0_gnn_in['u'], 'L0_gnn_W1': _L0_gnn_in['W1'], 'L0_gnn_b1': _L0_gnn_in['b1'], 'L0_gnn_W2': _L0_gnn_in['W2'], 'L0_gnn_b2': _L0_gnn_in['b2'], 'L1_gnn_Wq': _L1_gnn_in['Wq'], 'L1_gnn_Cqk': _L1_gnn_in['Cqk'], 'L1_gnn_Cv': _L1_gnn_in['Cv'], 'L1_gnn_k_w1': _L1_gnn_in['k_w1'], 'L1_gnn_k_b1': _L1_gnn_in['k_b1'], 'L1_gnn_k_w2': _L1_gnn_in['k_w2'], 'L1_gnn_k_b2': _L1_gnn_in['k_b2'], 'L1_gnn_v_w1': _L1_gnn_in['v_w1'], 'L1_gnn_v_b1': _L1_gnn_in['v_b1'], 'L1_gnn_v_w2': _L1_gnn_in['v_w2'], 'L1_gnn_v_b2': _L1_gnn_in['v_b2'], 'L1_gnn_W_out': _L1_gnn_in['W_out'], 'L1_gnn_W_self': _L1_gnn_in['W_self'], 'L1_gnn_gamma': _L1_gnn_in['gamma'], 'L1_gnn_beta': _L1_gnn_in['beta']}

def reference(x, src, dst, edge_attr_64, edge_attr_9, L0_gnn_u, L0_gnn_W1, L0_gnn_b1, L0_gnn_W2, L0_gnn_b2, L1_gnn_Wq, L1_gnn_Cqk, L1_gnn_Cv, L1_gnn_k_w1, L1_gnn_k_b1, L1_gnn_k_w2, L1_gnn_k_b2, L1_gnn_v_w1, L1_gnn_v_b1, L1_gnn_v_w2, L1_gnn_v_b2, L1_gnn_W_out, L1_gnn_W_self, L1_gnn_gamma, L1_gnn_beta):
    import jax
    import jax.numpy as jnp

    def _L0_gnn_ref(x, edge_index, edge_attr, u, batch, W1, b1, W2, b2):
        import jax, jax.numpy as jnp
        import numpy as np
        N_NODES = 50000
        N_EDGES = 25000
        D = 64
        NUM_GRAPHS = 64
        IN_DIM = 3 * D
        K = 64

        def swish(x):
            return x * jax.nn.sigmoid(x)
        col = edge_index[1]
        aggregated = jax.ops.segment_sum(edge_attr, col, num_segments=x.shape[0])
        inputs = jnp.concatenate([x, aggregated, u[batch]], axis=1)
        h = swish(inputs @ W1 + b1)
        return swish(h @ W2 + b2)

    def _L1_gnn_ref(tfn_features, edge_features, edge_sh, Wq, Cqk, Cv, k_w1, k_b1, k_w2, k_b2, v_w1, v_b1, v_w2, v_b2, W_out, W_self, gamma, beta, edge_index):
        import jax, jax.numpy as jnp
        import numpy as np
        N, E = (10000, 10000)
        D, S, HE = (64, 9, 64)
        H, DQK, DV = (8, 16, 16)
        OK, OV = (H * DQK, H * DV)
        EPS_BN = 1e-05

        def tensor_product(x_e, sh, w, C):
            acc = sh[:, 0:1] * (x_e @ C[:, 0, :])
            for s in range(1, S):
                acc = acc + sh[:, s:s + 1] * (x_e @ C[:, s, :])
            return acc * w

        def mlp2(x, w1, b1, w2, b2):
            return jax.nn.relu(x @ w1 + b1) @ w2 + b2
        edge_dst, edge_src = (edge_index[0], edge_index[1])
        n = tfn_features.shape[0]
        q = (tfn_features @ Wq).reshape(n, H, DQK)
        x_dst = tfn_features[edge_dst]
        wk = mlp2(edge_features, k_w1, k_b1, k_w2, k_b2)
        wv = mlp2(edge_features, v_w1, v_b1, v_w2, v_b2)
        k = tensor_product(x_dst, edge_sh, wk, Cqk).reshape(-1, H, DQK)
        v = tensor_product(x_dst, edge_sh, wv, Cv).reshape(-1, H, DV)
        attn = jnp.einsum('ehd,ehd->eh', q[edge_src], k)
        amax = jax.ops.segment_max(attn, edge_src, num_segments=n)
        ex = jnp.exp(attn - amax[edge_src])
        denom = jax.ops.segment_sum(ex, edge_src, num_segments=n)
        alpha = ex / (denom[edge_src] + 1e-16)
        upd = jax.ops.segment_sum(v * alpha[..., None], edge_src, num_segments=n)
        upd = upd.reshape(n, OV) @ W_out
        out = tfn_features @ W_self + upd
        mu = out.mean(axis=0)
        var = out.var(axis=0)
        return (out - mu) * jax.lax.rsqrt(var + EPS_BN) * gamma + beta
    edge_index = jnp.stack([src, dst])
    batch0 = jnp.zeros((3125,), jnp.int32)
    x = _layernorm(x + _L0_gnn_ref(x, edge_index, edge_attr_64, L0_gnn_u, batch0, L0_gnn_W1, L0_gnn_b1, L0_gnn_W2, L0_gnn_b2), axis=-1)
    x = _layernorm(x + _L1_gnn_ref(x, edge_attr_64, edge_attr_9, L1_gnn_Wq, L1_gnn_Cqk, L1_gnn_Cv, L1_gnn_k_w1, L1_gnn_k_b1, L1_gnn_k_w2, L1_gnn_k_b2, L1_gnn_v_w1, L1_gnn_v_b1, L1_gnn_v_w2, L1_gnn_v_b2, L1_gnn_W_out, L1_gnn_W_self, L1_gnn_gamma, L1_gnn_beta, edge_index), axis=-1)
    return x

_drawn_inputs = setup_inputs


def setup_inputs(seed=0):
    import zlib

    import numpy as np

    out = dict(_drawn_inputs(seed))
    spreads = {'L1_gnn_k_b1': (0.0, 0.1),
     'L1_gnn_k_b2': (0.0, 0.1),
     'L1_gnn_v_b1': (0.0, 0.1),
     'L1_gnn_v_b2': (0.0, 0.1),
     'L1_gnn_gamma': (1.0, 0.2),
     'L1_gnn_beta': (0.0, 0.1)}
    factors = {'L0_gnn_b1': 4.294}
    for name, (base, spread) in spreads.items():
        noise = np.random.default_rng([zlib.crc32(name.encode()), seed]).standard_normal(out[name].shape)
        drawn = base * np.exp(spread * noise) if base else spread * noise
        out[name] = jnp.asarray(drawn.astype(out[name].dtype))
    for name, factor in factors.items():
        out[name] = (out[name] * factor).astype(out[name].dtype)
    return out
```

```python
from contextlib import ExitStack

import concourse.bass as bass
from concourse import mybir

ALU = mybir.AluOpType
ACT = mybir.ActivationFunctionType
AX_X = mybir.AxisListType.X
F32 = mybir.dt.float32
BF16 = mybir.dt.bfloat16
I32 = mybir.dt.int32

P = 128
N = 3125
D = 64
NT = (N + P) // P
NP = NT * P
E = 100000
G = 512
NG = -(-E // G)
EP = NG * G
NK = EP // P
S = 9
SP3 = 3 * S
NJ = 5
H = 8
DH = 16
O = H * DH
RW = O + H
W = 2048
NC = EP // W
WJ = W // P
NODE_BLOCKS = [(b, min(G, NP - b)) for b in range(0, NP, G)]
OH = 8
NOH = NK // OH
LN_STEPS = 6
FAR = 3.0e38
EPS = 1e-5


def gnn_two_layers(nc, a, out):
    ctx = ExitStack()
    with ctx:
        def sb(name, shape, dt=F32):
            return ctx.enter_context(nc.sbuf_tensor(name, shape, dt))

        def sem(name):
            return ctx.enter_context(nc.semaphore(name))

        def dram(name, shape, dt=F32):
            return nc.dram_tensor(name, shape, dt, kind="Internal").ap()

        keep_d = dram("keep_d", [EP], BF16)
        reset_d = dram("reset_d", [EP], BF16)
        sh3_d = dram("sh3_d", [3, S, EP], BF16)
        aggrow_d = dram("aggrow_d", [EP, D])
        xtab_d = dram("xtab_d", [NP, 2 * D])
        qtab_d = dram("qtab_d", [NP, O])
        nrow_d = dram("nrow_d", [EP, RW])

        ident = sb("ident", [P, P])
        headones = sb("headones", [P, O])
        headpick = sb("headpick", [P, H])
        iota_row = sb("iota_row", [P, P])
        upper = sb("upper", [P, P])
        ones = sb("ones", [P, P])
        sel_f = sb("sel_f", [SP3, NJ * P])
        sel = sb("sel", [SP3, NJ, P], BF16)
        ck = sb("ck", [P, 4, O])
        cv = sb("cv", [P, 4, O])
        c8 = sb("c8", [P, O])
        w1kv = sb("w1kv", [D, P])
        w2kv = sb("w2kv", [P, O])
        b1kv = sb("b1kv", [P, 1])
        b2k = sb("b2k", [P, 1])
        b2v = sb("b2v", [P, 1])
        w1 = sb("w1", [P, D])
        w1u = sb("w1u", [D, D])
        b1 = sb("b1", [D, 1])
        u0 = sb("u0", [D, 1])
        w2 = sb("w2", [D, D])
        b2 = sb("b2", [D, 1])
        wq = sb("wq", [D, O])
        wout = sb("wout", [P, D])
        wself = sb("wself", [D, D])
        gamma = sb("gamma", [D, 1])
        beta = sb("beta", [D, 1])

        src_t = sb("src_t", [P, NK], I32)
        dst_t = sb("dst_t", [P, NK], I32)
        has = sb("has", [P, NT])
        end_i = sb("end_i", [P, NT], I32)

        x_r = sb("x_r", [P, NT, 2 * D])
        xa_t = sb("xa_t", [P, NP])
        h_t = sb("h_t", [D, NP])
        r_r = sb("r_r", [P, NT, D])
        x1_r = sb("x1_r", [P, NT, D])
        x1_t = sb("x1_t", [D, NP])
        q_r = sb("q_r", [P, NT, O])
        sq_r = q_r[:, :, 0:D]
        sg_t = x_r[0:D, :, :].rearrange("p t d -> p (t d)")
        mean = sb("mean", [P, NT])
        var = sb("var", [P, NT])
        rstd = sb("rstd", [P, NT])
        b1e = sb("b1e", [D, 1])
        epst = sb("epst", [P, 1])
        bnc = sb("bnc", [D, 8])

        early_ctx = ExitStack()

        def early(name, shape, dt=F32):
            return early_ctx.enter_context(nc.sbuf_tensor(name, shape, dt))

        d_prev = early("d_prev", [P, NK], I32)
        d_this = early("d_this", [P, NK], I32)
        keep = early("keep", [P, NK], BF16)
        reset = early("reset", [P, NK], BF16)
        lo_i = early("lo_i", [P, NK], I32)
        hi_i = early("hi_i", [P, NK], I32)
        lo_f = early("lo_f", [P, NK])
        hi_f = early("hi_f", [P, NK])
        oh_lo = early("oh_lo", [P, 2, OH, P], BF16)
        oh_hi = early("oh_hi", [P, 2, OH, NT], BF16)
        count = early("count", [NT, P])
        cum = early("cum", [NT, P])
        before = early("before", [NT, 1])
        count_t = early("count_t", [P, NT])
        end_f = early("end_f", [P, NT])

        SC = 14
        SW = EP // SC
        shf = early("shf", [S * SC, SW])
        shp = early("shp", [S * SC, SW], BF16)

        ea_c = early("ea_c", [D, 2, W])
        keep_c = early("keep_c", [D, 2, W], BF16)
        run_c = early("run_c", [D, 2, W])

        early_ctx.close()
        row_c = xa_t[:, 0:2 * WJ * D].rearrange("p (b w) -> p b w", b=2)

        ea = sb("ea", [D, 2, G])
        s3 = sb("s3", [SP3, 2, G], BF16)
        rs = sb("rs", [P, 2, G], BF16)
        xg = sb("xg", [P, 2, 4, 2 * D])
        qg = sb("qg", [P, 2, 4, O])
        src_g = sb("src_g", [P, 2, 4], I32)
        dst_g = sb("dst_g", [P, 2, 4], I32)
        xt = sb("xt", [P, 2, G])
        hid = sb("hid", [P, 2, G])
        qt = sb("qt", [P, 2, G])
        wkq = sb("wkq", [P, 2, G])
        wv = sb("wv", [P, 2, G])
        z = sb("z", [P, 2, NJ, G])
        kq = sb("kq", [P, 2, G])
        val = sb("val", [P, 2, G])
        mx = sb("mx", [P, 2, G])
        am = sb("am", [P, 2, G])
        ex = sb("ex", [P, 2, G])
        dm = sb("dm", [P, 2, G])
        dmr = sb("dmr", [P, 2, G])
        dec = sb("dec", [P, 2, G])
        num = sb("num", [P, 2, G])
        den = sb("den", [P, 2, G])
        row = sb("row", [P, 2, 4, RW])
        end_rows = z[:, :, :, :].rearrange("p b j g -> p (b j g)")[:, 0:NT * RW].rearrange("p (t w) -> p t w", t=NT)
        rden = sb("rden", [P, NT, H])

        bank = [ctx.enter_context(nc.psum_tensor(f"bank{i}", [P, G], F32)) for i in range(8)]
        ps_xw, ps_hw, ps_s0, ps_s1, ps_k, ps_v, ps_qa, ps_r = bank

        loaded = sem("loaded")
        dlin_in = sem("dlin_in")
        tabs_in = sem("tabs_in")
        sh_in = sem("sh_in")
        x_in = sem("x_in")
        flags_done = sem("flags_done")
        flags_out = sem("flags_out")
        split_done = sem("split_done")
        split_step = sem("split_step")
        split_out = [sem(f"split_out{i}") for i in range(3)]
        sel_done = sem("sel_done")
        hilo = sem("hilo")
        onehot = sem("onehot")
        counted = sem("counted")
        hist_ps = sem("hist_ps")
        hist_ok = sem("hist_ok")
        ends_ok = sem("ends_ok")
        chunk_in = [sem(f"chunk_in{i}") for i in range(2)]
        chunk_run = sem("chunk_run")
        chunk_ps = sem("chunk_ps")
        chunk_row = sem("chunk_row")
        chunk_out = [sem(f"chunk_out{i}") for i in range(2)]
        agg_in = sem("agg_in")
        masked = sem("masked")
        b1e_ps = sem("b1e_ps")
        b1e_ok = sem("b1e_ok")
        xat_ps = sem("xat_ps")
        xat_ok = sem("xat_ok")
        h1_ps = sem("h1_ps")
        h1_sig = sem("h1_sig")
        h1_ok = sem("h1_ok")
        h2_ps = sem("h2_ps")
        h2_sig = sem("h2_sig")
        h2_ok = sem("h2_ok")
        res_ok = sem("res_ok")
        rr_ps = sem("rr_ps")
        rr_ok = sem("rr_ok")
        ln = sem("ln")
        ln_sqrt = sem("ln_sqrt")
        x1_ok = sem("x1_ok")
        x1t_ps = sem("x1t_ps")
        x1t_ok = sem("x1t_ok")
        q_ps = sem("q_ps")
        q_ok = sem("q_ok")
        tab_out = sem("tab_out")
        ea_in = [sem(f"ea_in{i}") for i in range(2)]
        s3_in = [sem(f"s3_in{i}") for i in range(2)]
        rs_in = [sem(f"rs_in{i}") for i in range(2)]
        xg_in = [sem(f"xg_in{i}") for i in range(2)]
        qg_in = [sem(f"qg_in{i}") for i in range(2)]
        src_picked = sem("src_picked")
        dst_picked = sem("dst_picked")
        xt_ps = sem("xt_ps")
        xt_ok = sem("xt_ok")
        hid_ps = sem("hid_ps")
        hid_ok = sem("hid_ok")
        qt_ps = sem("qt_ps")
        qt_ok = sem("qt_ok")
        wk_ps = sem("wk_ps")
        wkq_ok = sem("wkq_ok")
        wv_ps = sem("wv_ps")
        wv_ok = sem("wv_ok")
        shb_ps = sem("shb_ps")
        z_ok = sem("z_ok")
        acc_ps = sem("acc_ps")
        kq_ok = sem("kq_ok")
        val_ok = sem("val_ok")
        att_ps = sem("att_ps")
        mx_ok = sem("mx_ok")
        am_ok = sem("am_ok")
        ex_ok = sem("ex_ok")
        dm_ok = sem("dm_ok")
        dmr_ok = sem("dmr_ok")
        dec_ok = sem("dec_ok")
        ev_ok = sem("ev_ok")
        num_ok = sem("num_ok")
        den_ok = sem("den_ok")
        row_ps = sem("row_ps")
        row_ok = sem("row_ok")
        row_out = [sem(f"row_out{i}") for i in range(2)]
        zeroed = sem("zeroed")
        nrow_in = sem("nrow_in")
        upd_step = sem("upd_step")
        upd_ps = sem("upd_ps")
        upd_ok = sem("upd_ok")
        o_ps = sem("o_ps")
        o_ok = sem("o_ok")
        bn = sem("bn")
        bn_sqrt = sem("bn_sqrt")
        y_ps = sem("y_ps")
        out_ok = sem("out_ok")
        stored = sem("stored")

        block = ctx.enter_context(nc.Block())

        WEIGHTS = [(ident, a["ident"]), (headones, a["headones"]), (headpick, a["headpick"]),
                   (iota_row, a["iota_row"]), (upper, a["upper"]), (sel_f, a["sel"]),
                   (ck, a["c_k"][0:8 * D, :].rearrange("(j p) o -> p j o", p=P)),
                   (cv, a["c_v"][0:8 * D, :].rearrange("(j p) o -> p j o", p=P)),
                   (c8[0:D, :], a["c_k"][8 * D:9 * D, :]), (c8[D:P, :], a["c_v"][8 * D:9 * D, :]),
                   (w1kv[:, 0:D], a["k_w1"]), (w1kv[:, D:P], a["v_w1"]),
                   (w2kv[0:D, :], a["k_w2"]), (w2kv[D:P, :], a["v_w2"]),
                   (b1kv[0:D, :], a["k_b1"]), (b1kv[D:P, :], a["v_b1"]), (b2k, a["k_b2"]), (b2v, a["v_b2"]),
                   (w1, a["w1"][0:P, :]), (w1u, a["w1"][P:P + D, :]), (b1, a["b1"]), (u0, a["u0"]),
                   (w2, a["w2"]), (b2, a["b2"]), (wq, a["wq"]), (wout, a["wout"]), (wself, a["wself"]),
                   (gamma, a["gamma"]), (beta, a["beta"])]
        ALL_WEIGHTS = 16 * len(WEIGHTS)

        def live(g):
            return not isinstance(g, int) or 0 <= g < NG

        def used(eng, s, g, per=1):
            if not isinstance(g, int) or g >= 2:
                eng.wait_ge(s, (g - 1) * per)

        def steps(eng, body):
            for t in range(-2, 4):
                body(t, t % 2)
            with eng.Fori(0, (NG - 6) // 2) as i:
                for r in range(2):
                    body(i * 2 + (4 + r), r)
            for t in range(NG - 2, NG + 2):
                body(t, t % 2)

        def carry(ins, s, n):
            return ins.wait_op(s, n, "sem-ge")

        def arrived(eng, ring, g, b, per=16):
            if isinstance(g, int):
                eng.wait_ge(ring[b], (g // 2 + 1) * per)
            else:
                eng.wait_ge(ring[b], (g - b + 2) * (per // 2))

        @block.sync
        def _(sp):
            sp.dma_start(d_prev[:, :], a["dst_lin"][0:EP].rearrange("(p c) -> p c", p=P)).then_inc(dlin_in, 16)
            sp.dma_start(d_this[:, :], a["dst_lin"][1:EP + 1].rearrange("(p c) -> p c", p=P)).then_inc(dlin_in, 16)
            sp.dma_start(dst_t[:, :], a["dst_t"]).then_inc(tabs_in, 16)
            sp.dma_start(src_t[:, :], a["src_t"]).then_inc(tabs_in, 16)
            for dst, src in WEIGHTS:
                sp.dma_start(dst[:] if not isinstance(dst, bass.AP) else dst, src).then_inc(loaded, 16)
            sp.dma_start(shf[:, :], a["sh_t"].rearrange("s (c w) -> (s c) w", c=SC)).then_inc(sh_in, 16)
            sp.dma_start(x_r[:, :, 0:D], a["x"].rearrange("(t p) d -> p t d", p=P)).then_inc(x_in, 16)
            sp.wait_ge(flags_done, 2)
            sp.dma_start(keep_d.rearrange("(p c) -> p c", p=P), keep[:, :]).then_inc(flags_out, 16)
            sp.dma_start(reset_d.rearrange("(p c) -> p c", p=P), reset[:, :]).then_inc(flags_out, 16)
            sp.wait_ge(flags_out, 32)

            def load_chunk(c, b):
                lo = c * W
                if not isinstance(c, int) or c >= 2:
                    sp.wait_ge(chunk_run, c - 1)
                sp.dma_start(ea_c[:, b, :], a["ea_t"][:, bass.ds(lo, W)]).then_inc(chunk_in[b], 16)
                sp.dma_start(keep_c[:, b, :],
                             keep_d[bass.ds(lo, W)].rearrange("(o w) -> o w", o=1).to_broadcast([D, W])
                             ).then_inc(chunk_in[b], 16)

            def store_chunk(c, b):
                sp.wait_ge(chunk_row, c * 2 + 2)
                sp.dma_start(aggrow_d[bass.ds(c * W, W), :].rearrange("(p j) d -> p (j d)", p=P),
                             row_c[:, b, :]).then_inc(chunk_out[b], 16)

            load_chunk(0, 0)
            load_chunk(1, 1)
            with sp.Fori(0, (NC - 3) // 2) as i:
                for r in range(2):
                    load_chunk(i * 2 + (2 + r), r)
                    store_chunk(i * 2 + r, r)
            load_chunk(NC - 1, 0)
            store_chunk(NC - 3, 0)
            store_chunk(NC - 2, 1)
            store_chunk(NC - 1, 0)

            sp.wait_ge(x1_ok, 1)
            for half in range(2):
                sp.dma_start(xtab_d[:, half * D:(half + 1) * D].rearrange("(t p) d -> p t d", p=P),
                             x1_r[:, :, :]).then_inc(tab_out, 16)
            sp.wait_ge(q_ok, len(NODE_BLOCKS))
            sp.dma_start(qtab_d.rearrange("(t p) d -> p t d", p=P), q_r[:, :, :]).then_inc(tab_out, 16)

            for part in range(3):
                sp.wait_ge(split_out[part], 16)

            def load_rs(g, b):
                used(sp, mx_ok, g)
                used(sp, dmr_ok, g)
                sp.dma_start(rs[:, b, :], reset_d[bass.ds(g * G, G)].rearrange("(o w) -> o w", o=1)
                             .to_broadcast([P, G])).then_inc(rs_in[b], 16)

            def load_edge(g, b):
                used(sp, shb_ps, g, NJ)
                used(sp, hid_ps, g)
                sp.dma_start(ea[:, b, :], a["ea_t"][:, bass.ds(g * G, G)]).then_inc(ea_in[b], 16)
                sp.dma_start(s3[:, b, :], sh3_d.rearrange("a s e -> (a s) e")[:, bass.ds(g * G, G)]
                             ).then_inc(s3_in[b], 16)

            def store_row(g, b):
                sp.wait_ge(row_ok, g * 2 + 2)
                sp.dma_start(nrow_d[bass.ds(g * G, G), :].rearrange("(p j) w -> p (j w)", p=P),
                             row[:, b, :, :].rearrange("p j w -> p (j w)")).then_inc(row_out[b], 16)

            def body(t, b):
                if live(t + 2):
                    load_edge(t + 2, b)
                if live(t):
                    load_rs(t, b)
                if live(t - 2):
                    store_row(t - 2, b)
            steps(sp, body)

            sp.wait_ge(out_ok, 1)
            sp.dma_start(out.rearrange("(t p) d -> p t d", p=P), r_r[:, :, :]).then_inc(stored, 16)
            sp.wait_ge(stored, 16)

        @block.gpsimd
        def _(pool):
            pool.memset(ones[:, :], 1.0).then_inc(zeroed, 1)
            pool.memset(epst[:, :], EPS).then_inc(zeroed, 1)
            pool.memset(run_c[:, 1, W - 1:W], 0.0).then_inc(zeroed, 1)

            pool.wait_ge(ends_ok, 2)
            pool.wait_ge(chunk_out[0], 16 * ((NC + 1) // 2))
            pool.wait_ge(chunk_out[1], 16 * (NC // 2))
            for t in range(NT):
                pool.indirect_dma_start(x_r[:, t, D:2 * D], None, aggrow_d[:, :],
                                        bass.IndirectOffsetOnAxis(ap=end_i[:, t:t + 1], axis=0)).then_inc(agg_in, 16)

            for part in range(3):
                pool.wait_ge(split_out[part], 16)
            for scanned in (mx, num, den):
                pool.memset(scanned[:, 1, G - 1:G], 0.0).then_inc(zeroed, 1)

            pool.wait_ge(tab_out, 48)
            pool.wait_ge(tabs_in, 32)

            def gather(g, b, rows, ring, table, index, picked, picks, read):
                if not isinstance(g, int) or g >= 2:
                    arrived(pool, ring, g - 2, b, 64)
                pool.tensor_copy(picked[:, b, :], index[:, bass.ds(g * 4, 4)]).then_inc(picks, 1)
                used(pool, read, g)
                pool.wait_ge(picks, g + 1)
                for k in range(4):
                    rows_in = pool.indirect_dma_start(rows[:, b, k, :], None, table,
                                                      bass.IndirectOffsetOnAxis(ap=picked[:, b, k:k + 1], axis=0))
                    if k == 0:
                        carry(rows_in, tab_out, 48)
                    rows_in.then_inc(ring[b], 16)

            def gather_x(g, b):
                gather(g, b, xg, xg_in, xtab_d[:, :], src_t, src_g, src_picked, xt_ps)

            def gather_q(g, b):
                gather(g, b, qg, qg_in, qtab_d[:, :], dst_t, dst_g, dst_picked, qt_ps)

            def shift(g, b):
                pool.wait_ge(mx_ok, g + 1)
                used(pool, dmr_ok, g)
                pool.tensor_tensor(dm[:, b, 1:G], mx[:, b, 0:G - 1], mx[:, b, 1:G], ALU.subtract).then_inc(dm_ok, 1)
                pool.tensor_tensor(dm[:, b, 0:1], mx[:, 1 - b, G - 1:G], mx[:, b, 0:1], ALU.subtract
                                   ).then_inc(dm_ok, 1)
                arrived(pool, rs_in, g, b)
                pool.wait_ge(dm_ok, g * 2 + 2)
                used(pool, dec_ok, g)
                pool.tensor_tensor(dmr[:, b, :], dm[:, b, :], rs[:, b, :], ALU.add).then_inc(dmr_ok, 1)

            def body(t, b):
                if live(t + 2):
                    gather_x(t + 2, b)
                if live(t + 1):
                    gather_q(t + 1, 1 - b)
                if live(t - 1):
                    shift(t - 1, 1 - b)
            steps(pool, body)

            pool.wait_ge(row_out[0], 16 * (NG // 2))
            pool.wait_ge(row_out[1], 16 * (NG // 2))
            for t in range(NT):
                pool.indirect_dma_start(end_rows[:, t, :], None, nrow_d[:, :],
                                        bass.IndirectOffsetOnAxis(ap=end_i[:, t:t + 1], axis=0)).then_inc(nrow_in, 16)


        ROW_TILES = [(b, list(range(8 * b, min(8 * b + 8, NT)))) for b in range(-(-NT // 8))]

        @block.scalar
        def _(act):
            act.wait_ge(loaded, ALL_WEIGHTS)
            act.activation(sel[:, :, :].rearrange("k j m -> k (j m)"), sel_f[:, :], ACT.Copy).then_inc(sel_done, 1)

            act.wait_ge(sh_in, 16)
            for part in range(3):
                if part > 0:
                    act.wait_ge(split_step, part)
                    act.wait_ge(split_out[part - 1], 16)
                act.activation(shp[:, :], shf[:, :], ACT.Copy).then_inc(split_done, 1)
                act.wait_ge(split_done, part + 1)
                act.dma_start(sh3_d[part].rearrange("s (c w) -> (s c) w", c=SC), shp[:, :]
                              ).then_inc(split_out[part], 16)

            def rows_out(c, b):
                if not isinstance(c, int) or c >= 2:
                    arrived(act, chunk_out, c - 2, b)
                for h in range(2):
                    act.wait_ge(chunk_ps, c * 2 + (h + 1))
                    act.activation(row_c[:, b, h * G:(h + 1) * G], bank[2 * b + h][:, :], ACT.Copy
                                   ).then_inc(chunk_row, 1)
            rows_out(0, 0)
            rows_out(1, 1)
            with act.Fori(0, (NC - 3) // 2) as i:
                for r in range(2):
                    rows_out(i * 2 + (2 + r), r)
            rows_out(NC - 1, 0)

            for n, (lo, w) in enumerate(NODE_BLOCKS):
                act.wait_ge(xat_ps, n + 1)
                act.activation(xa_t[:, lo:lo + w], bank[n][:, 0:w], ACT.Copy).then_inc(xat_ok, 1)
            act.wait_ge(b1e_ok, 1)
            for n, (lo, w) in enumerate(NODE_BLOCKS):
                act.wait_ge(h1_ps, n + 1)
                act.activation(sg_t[:, lo:lo + w], bank[n][0:D, 0:w], ACT.Sigmoid, bias=b1e[:, :]
                               ).then_inc(h1_sig, 1)
            for n, (lo, w) in enumerate(NODE_BLOCKS):
                act.wait_ge(h2_ps, n + 1)
                act.wait_ge(h1_ok, n + 1)
                act.activation(sg_t[:, lo:lo + w], bank[n][0:D, 0:w], ACT.Sigmoid, bias=b2[:, :]
                               ).then_inc(h2_sig, 1)
            act.wait_ge(ln, 5)
            act.activation(rstd[:, :], var[:, :], ACT.Sqrt, scale=1.0 / D, bias=epst[:, :]).then_inc(ln_sqrt, 1)
            for n, (lo, w) in enumerate(NODE_BLOCKS):
                act.wait_ge(x1t_ps, n + 1)
                act.activation(x1_t[:, lo:lo + w], bank[n][0:D, 0:w], ACT.Copy).then_inc(x1t_ok, 1)
            for n, (lo, w) in enumerate(NODE_BLOCKS):
                act.wait_ge(q_ps, n + 1)
                act.activation(q_r[:, lo // P:(lo + w) // P, :].rearrange("p t o -> p (t o)"),
                               bank[n][:, 0:w], ACT.Copy).then_inc(q_ok, 1)

            def front_x(g, b):
                act.wait_ge(xt_ps, g + 1)
                used(act, z_ok, g, NJ)
                act.activation(xt[:, b, :], ps_xw[:, :], ACT.Copy).then_inc(xt_ok, 1)

            def front_h(g, b):
                act.wait_ge(hid_ps, g + 1)
                used(act, wv_ps, g)
                act.activation(hid[:, b, :], ps_hw[:, :], ACT.Relu, bias=b1kv[:, :]).then_inc(hid_ok, 1)

            def front_q(g, b):
                act.wait_ge(qt_ps, g + 1)
                used(act, wkq_ok, g)
                act.activation(qt[:, b, :], ps_qa[:, :], ACT.Copy).then_inc(qt_ok, 1)

            def weights_v(g, b):
                act.wait_ge(wv_ps, g + 1)
                used(act, val_ok, g)
                act.activation(wv[:, b, :], ps_hw[:, :], ACT.Identity, bias=b2v[:, :]).then_inc(wv_ok, 1)

            def exponents(g, b):
                act.wait_ge(am_ok, g + 1)
                used(act, den_ok, g)
                act.activation(ex[:, b, :], am[:, b, :], ACT.Exp).then_inc(ex_ok, 1)
                act.wait_ge(dmr_ok, g + 1)
                act.activation(dec[:, b, :], dmr[:, b, :], ACT.Exp).then_inc(dec_ok, 1)

            def rows(g, b):
                if not isinstance(g, int) or g >= 2:
                    arrived(act, row_out, g - 2, b)
                for h in range(2):
                    act.wait_ge(row_ps, g * 2 + (h + 1))
                    act.activation(row[:, b, 2 * h:2 * h + 2, :].rearrange("p j w -> p (j w)"),
                                   ps_r[:, 0:2 * RW], ACT.Copy).then_inc(row_ok, 1)

            def body(t, b):
                if live(t + 2):
                    front_x(t + 2, b)
                if live(t + 1):
                    front_h(t + 1, 1 - b)
                    front_q(t + 1, 1 - b)
                    weights_v(t + 1, 1 - b)
                if live(t - 2):
                    rows(t - 2, b)
                if live(t - 1):
                    exponents(t - 1, 1 - b)
            steps(act, body)

            for n, (lo, w) in enumerate(NODE_BLOCKS):
                act.wait_ge(upd_ps, n + 1)
                act.activation(xa_t[:, lo:lo + w], bank[n][:, 0:w], ACT.Copy).then_inc(upd_ok, 1)
            act.wait_ge(bn, 5)
            act.activation(bnc[:, 3:4], bnc[:, 2:3], ACT.Sqrt, scale=1.0 / N, bias=epst[0:D, :]).then_inc(bn_sqrt, 1)
            act.wait_ge(ln, LN_STEPS + 5)
            act.activation(rstd[:, :], var[:, :], ACT.Sqrt, scale=1.0 / D, bias=epst[:, :]).then_inc(ln_sqrt, 1)

        @block.tensor
        def _(pe):
            pe.wait_ge(loaded, ALL_WEIGHTS)

            def count_tiles(n, b, first=False, last=False):
                pe.wait_ge(onehot, n * 2 + 2)
                for k in range(OH):
                    mm = pe.matmul(bank[7][0:NT, 0:P], oh_hi[:, b, k, :], oh_lo[:, b, k, :],
                                   start=first and k == 0, stop=last and k == OH - 1)
                mm.then_inc(counted, 1)

            def chunk_rows(c, b):
                pe.wait_ge(chunk_run, c + 1)
                for h in range(2):
                    used(pe, chunk_row, c, 2)
                    for j in range(8):
                        tr = pe.transpose(bank[2 * b + h][:, j * D:(j + 1) * D],
                                          run_c[:, b, bass.ds(8 * h + j, P, WJ)], ident[0:D, 0:D])
                        if j == 0:
                            carry(tr, loaded, ALL_WEIGHTS)
                    tr.then_inc(chunk_ps, 1)

            def chunk(c, b, first=False, last=False):
                count_tiles(c * 2, 0, first=first)
                count_tiles(c * 2 + 1, 1, last=last)
                chunk_rows(c, b)
            chunk(0, 0, first=True)
            chunk(1, 1)
            with pe.Fori(0, (NC - 3) // 2) as i:
                for r in range(2):
                    chunk(i * 2 + (2 + r), r)
            chunk(NC - 1, 0, last=True)

            pe.wait_ge(hist_ok, 2)
            pe.matmul(bank[7][0:D, 448:449], w1u[:, :], u0[:, :], start=True, stop=True).then_inc(b1e_ps, 1)
            pe.matmul(bank[7][0:NT, 256:257], upper[0:NT, 0:NT], cum[:, P - 1:P], start=True, stop=True
                      ).then_inc(hist_ps, 1)
            pe.wait_ge(hist_ok, 4)
            pe.transpose(bank[7][:, 320:320 + NT], cum[:, :], ident[0:NT, 0:NT])
            pe.transpose(bank[7][:, 352:352 + NT], count[:, :], ident[0:NT, 0:NT]).then_inc(hist_ps, 1)

            pe.wait_ge(masked, 1)
            pe.wait_ge(chunk_row, 2 * NC)
            for n, (lo, w) in enumerate(NODE_BLOCKS):
                for t in range(lo // P, (lo + w) // P):
                    tr = pe.transpose(bank[n][:, t * P - lo:(t + 1) * P - lo], x_r[:, t, :], ident[:, :])
                tr.then_inc(xat_ps, 1)
            for n, (lo, w) in enumerate(NODE_BLOCKS):
                pe.wait_ge(xat_ok, n + 1)
                pe.matmul(bank[n][0:D, 0:w], w1[:, :], xa_t[:, lo:lo + w], start=True, stop=True).then_inc(h1_ps, 1)
            for n, (lo, w) in enumerate(NODE_BLOCKS):
                pe.wait_ge(h1_ok, n + 1)
                pe.matmul(bank[n][0:D, 0:w], w2[:, :], h_t[:, lo:lo + w], start=True, stop=True).then_inc(h2_ps, 1)
            pe.wait_ge(res_ok, len(NODE_BLOCKS))
            for b, tiles in ROW_TILES:
                for j, t in enumerate(tiles):
                    tr = pe.transpose(bank[b][:, j * D:(j + 1) * D], h_t[:, t * P:(t + 1) * P], ident[0:D, 0:D])
                tr.then_inc(rr_ps, 1)
            pe.wait_ge(x1_ok, 1)
            for n, (lo, w) in enumerate(NODE_BLOCKS):
                for t in range(lo // P, (lo + w) // P):
                    tr = pe.transpose(bank[n][0:D, t * P - lo:(t + 1) * P - lo], x1_r[:, t, :], ident[:, :])
                tr.then_inc(x1t_ps, 1)
            for n, (lo, w) in enumerate(NODE_BLOCKS):
                pe.wait_ge(x1t_ok, n + 1)
                for t in range(lo // P, (lo + w) // P):
                    mm = pe.matmul(bank[n][:, t * P - lo:(t + 1) * P - lo], x1_t[:, t * P:(t + 1) * P], wq[:, :],
                                   start=True, stop=True)
                mm.then_inc(q_ps, 1)
            pe.wait_ge(q_ok, len(NODE_BLOCKS))
            pe.wait_ge(sel_done, 1)

            def x_turn(g, b):
                arrived(pe, xg_in, g, b, 64)
                used(pe, wkq_ok, g)
                if isinstance(g, int) and g == 1:
                    pe.wait_ge(xt_ok, 1)
                for k in range(4):
                    tr = pe.transpose(ps_xw[:, k * P:(k + 1) * P], xg[:, b, k, :], ident[:, :])
                tr.then_inc(xt_ps, 1)

            def hidden(g, b):
                arrived(pe, ea_in, g, b)
                if not isinstance(g, int) or g >= 1:
                    pe.wait_ge(wv_ok, g)
                pe.matmul(ps_hw[:, :], w1kv[:, :], ea[:, b, :], start=True, stop=True).then_inc(hid_ps, 1)

            def q_turn(g, b):
                arrived(pe, qg_in, g, b, 64)
                if not isinstance(g, int) or g >= 3:
                    pe.wait_ge(am_ok, g - 2)
                elif g >= 1:
                    pe.wait_ge(qt_ok, g)
                for k in range(4):
                    tr = pe.transpose(ps_qa[:, k * P:(k + 1) * P], qg[:, b, k, :], ident[:, :])
                tr.then_inc(qt_ps, 1)

            def weights(g, b):
                pe.wait_ge(hid_ok, g + 1)
                if not isinstance(g, int) or g + 1 < NG:
                    pe.wait_ge(xt_ok, g + 2)
                else:
                    pe.wait_ge(xt_ok, NG)
                pe.matmul(ps_xw[:, :], w2kv[0:D, :], hid[0:D, b, :], start=True, stop=True).then_inc(wk_ps, 1)
                pe.matmul(ps_hw[:, :], w2kv[D:P, :], hid[D:P, b, :], start=True, stop=True).then_inc(wv_ps, 1)

            def spread(g, b, j):
                if j == 0:
                    arrived(pe, s3_in, g, b)
                if not isinstance(g, int) or g * NJ + j >= 2:
                    pe.wait_ge(z_ok, g * NJ + (j - 1))
                pe.matmul(bank[2 + (NJ * b + j) % 2][:, :], sel[:, j, :], s3[:, b, :], start=True, stop=True
                          ).then_inc(shb_ps, 1)

            def products(g, b, j):
                pe.wait_ge(z_ok, g * NJ + (j + 1))
                if j == 0 and (not isinstance(g, int) or g >= 1):
                    pe.wait_ge(kq_ok, g)
                    pe.wait_ge(val_ok, g)
                if j < 4:
                    pe.matmul(ps_k[:, :], ck[:, j, :], z[:, b, j, :], start=j == 0, stop=False)
                    pe.matmul(ps_v[:, :], cv[:, j, :], z[:, b, j, :], start=j == 0, stop=False)
                else:
                    pe.matmul(ps_k[:, :], c8[0:D, :], z[0:D, b, j, :], start=False, stop=True)
                    pe.matmul(ps_v[:, :], c8[D:P, :], z[D:P, b, j, :], start=False, stop=True).then_inc(acc_ps, 1)

            def scores(g, b):
                pe.wait_ge(kq_ok, g + 1)
                pe.wait_ge(qt_ok, g + 3 if not isinstance(g, int) or g + 3 <= NG else NG)
                pe.matmul(ps_qa[:, :], headones[:, :], kq[:, b, :], start=True, stop=True).then_inc(att_ps, 1)

            def row_turn(g, b, h):
                pe.wait_ge(num_ok, g + 1)
                pe.wait_ge(den_ok, g + 1)
                if h == 1 or not isinstance(g, int) or g >= 1:
                    pe.wait_ge(row_ok, g * 2 + h)
                for i in range(2):
                    j = 2 * h + i
                    pe.transpose(ps_r[:, i * RW:i * RW + O], num[:, b, bass.ds(j, P, 4)], ident[:, :])
                    mm = pe.matmul(ps_r[:, i * RW + O:(i + 1) * RW], den[:, b, bass.ds(j, P, 4)], headpick[:, :],
                                   start=True, stop=True)
                mm.then_inc(row_ps, 1)

            def body(t, b):
                if live(t + 2):
                    x_turn(t + 2, b)
                if live(t + 1):
                    hidden(t + 1, 1 - b)
                    q_turn(t + 1, 1 - b)
                for j in range(NJ):
                    if live(t + 1):
                        spread(t + 1, 1 - b, j)
                    if live(t):
                        products(t, b, j)
                    if j == 0 and live(t + 1):
                        weights(t + 1, 1 - b)
                    if j == 1 and live(t - 1):
                        scores(t - 1, 1 - b)
                    if j == 3 and live(t - 2):
                        row_turn(t - 2, b, 0)
                    if j == 4 and live(t - 2):
                        row_turn(t - 2, b, 1)
            steps(pe, body)

            pe.wait_ge(upd_step, 4)
            pe.wait_ge(row_ok, 2 * NG)
            pe.wait_ge(am_ok, NG)
            pe.wait_ge(val_ok, NG)
            for n, (lo, w) in enumerate(NODE_BLOCKS):
                for t in range(lo // P, (lo + w) // P):
                    tr = pe.transpose(bank[n][:, t * P - lo:(t + 1) * P - lo], end_rows[:, t, 0:O], ident[:, :])
                tr.then_inc(upd_ps, 1)
            for n, (lo, w) in enumerate(NODE_BLOCKS):
                pe.wait_ge(upd_ok, n + 1)
                pe.matmul(bank[n][0:D, 0:w], wself[:, :], x1_t[:, lo:lo + w], start=True, stop=False)
                pe.matmul(bank[n][0:D, 0:w], wout[:, :], xa_t[:, lo:lo + w], start=False, stop=True).then_inc(o_ps, 1)
            pe.wait_ge(bn, 8)
            for b, tiles in ROW_TILES:
                for j, t in enumerate(tiles):
                    tr = pe.transpose(bank[b][:, j * D:(j + 1) * D], h_t[:, t * P:(t + 1) * P], ident[0:D, 0:D])
                tr.then_inc(y_ps, 1)

        @block.vector
        def _(dve):
            dve.wait_ge(dlin_in, 32)
            dve.tensor_tensor(keep[:, :], d_prev[:, :], d_this[:, :], ALU.is_equal).then_inc(flags_done, 1)
            dve.wait_ge(flags_done, 1)
            dve.tensor_scalar(reset[:, :], keep[:, :], -1.0, FAR, ALU.add, ALU.mult).then_inc(flags_done, 1)
            dve.wait_ge(tabs_in, 32)
            dve.tensor_scalar(lo_i[:, :], dst_t[:, :], P - 1, None, ALU.bitwise_and).then_inc(hilo, 1)
            dve.tensor_scalar(hi_i[:, :], dst_t[:, :], 7, None, ALU.logical_shift_right).then_inc(hilo, 1)
            dve.wait_ge(hilo, 2)
            dve.tensor_copy(lo_f[:, :], lo_i[:, :]).then_inc(hilo, 1)
            dve.tensor_copy(hi_f[:, :], hi_i[:, :]).then_inc(hilo, 1)
            for part in range(2):
                dve.wait_ge(split_done, part + 1)
                dve.tensor_tensor(shf[:, :], shf[:, :], shp[:, :], ALU.subtract).then_inc(split_step, 1)

            dve.wait_ge(zeroed, 3)

            def run(c, b):
                arrived(dve, chunk_in, c, b, 32)
                if not isinstance(c, int) or c >= 1:
                    dve.wait_ge(chunk_run, c)
                if not isinstance(c, int) or c >= 2:
                    dve.wait_ge(chunk_ps, c * 2 - 2)
                dve.tensor_tensor_scan(run_c[:, b, :], keep_c[:, b, :], ea_c[:, b, :], run_c[:, 1 - b, W - 1:W],
                                       ALU.mult, ALU.add).then_inc(chunk_run, 1)

            def one_hots(n, b):
                if not isinstance(n, int) or n >= 2:
                    dve.wait_ge(counted, n - 1)
                for f, oh, width in ((lo_f, oh_lo, P), (hi_f, oh_hi, NT)):
                    dve.tensor_tensor(oh[:, b, :, :],
                                      f[:, bass.ds(n * OH, OH)].rearrange("p (k o) -> p k o", o=1)
                                      .to_broadcast([P, OH, width]),
                                      iota_row[:, 0:width].rearrange("p (o w) -> p o w", o=1)
                                      .to_broadcast([P, OH, width]),
                                      ALU.is_equal).then_inc(onehot, 1)

            def chunk(c, b):
                run(c, b)
                one_hots(c * 2, 0)
                one_hots(c * 2 + 1, 1)
            dve.wait_ge(hilo, 4)
            dve.wait_ge(loaded, ALL_WEIGHTS)
            chunk(0, 0)
            chunk(1, 1)
            with dve.Fori(0, (NC - 3) // 2) as i:
                for r in range(2):
                    chunk(i * 2 + (2 + r), r)
            chunk(NC - 1, 0)

            dve.wait_ge(counted, NOH)
            dve.tensor_copy(count[:, :], bank[7][0:NT, 0:P]).then_inc(hist_ok, 1)
            dve.wait_ge(hist_ok, 1)
            dve.tensor_tensor_scan(cum[:, :], ones[0:NT, :], count[:, :], 0.0, ALU.mult, ALU.add).then_inc(hist_ok, 1)
            dve.wait_ge(hist_ps, 1)
            dve.tensor_copy(before[:, :], bank[7][0:NT, 256:257]).then_inc(hist_ok, 1)
            dve.wait_ge(hist_ok, 3)
            dve.tensor_scalar(cum[:, :], cum[:, :], before[:, :], None, ALU.add).then_inc(hist_ok, 1)
            dve.wait_ge(hist_ps, 2)
            dve.tensor_scalar(end_f[:, :], bank[7][:, 320:320 + NT], -1.0, 0.0, ALU.add, ALU.max).then_inc(hist_ok, 1)
            dve.tensor_scalar(has[:, :], bank[7][:, 352:352 + NT], 0.0, None, ALU.is_gt).then_inc(ends_ok, 1)
            dve.wait_ge(hist_ok, 5)
            dve.tensor_copy(end_i[:, :], end_f[:, :]).then_inc(ends_ok, 1)
            dve.wait_ge(b1e_ps, 1)
            dve.tensor_tensor(b1e[:, :], bank[7][0:D, 448:449], b1[:, :], ALU.add).then_inc(b1e_ok, 1)

            dve.wait_ge(agg_in, 16 * NT)
            dve.wait_ge(x_in, 16)
            dve.wait_ge(ends_ok, 2)
            dve.tensor_tensor(x_r[:, :, D:2 * D], x_r[:, :, D:2 * D],
                              has[:, :].rearrange("p (t o) -> p t o", o=1).to_broadcast([P, NT, D]), ALU.mult
                              ).then_inc(masked, 1)
            dve.wait_ge(b1e_ok, 1)
            for n, (lo, w) in enumerate(NODE_BLOCKS):
                dve.wait_ge(h1_sig, n + 1)
                dve.scalar_tensor_tensor(out=h_t[:, lo:lo + w], in0=bank[n][0:D, 0:w], scalar=b1e[:, :],
                                         in1=sg_t[:, lo:lo + w], op0=ALU.add, op1=ALU.mult).then_inc(h1_ok, 1)
            for n, (lo, w) in enumerate(NODE_BLOCKS):
                dve.wait_ge(h2_sig, n + 1)
                dve.scalar_tensor_tensor(out=h_t[:, lo:lo + w], in0=bank[n][0:D, 0:w], scalar=b2[:, :],
                                         in1=sg_t[:, lo:lo + w], op0=ALU.add, op1=ALU.mult).then_inc(h2_ok, 1)
            for n, (lo, w) in enumerate(NODE_BLOCKS):
                dve.wait_ge(h2_ok, n + 1)
                dve.tensor_tensor(h_t[:, lo:lo + w], h_t[:, lo:lo + w], xa_t[0:D, lo:lo + w], ALU.add
                                  ).then_inc(res_ok, 1)
            for b, tiles in ROW_TILES:
                dve.wait_ge(rr_ps, b + 1)
                dve.tensor_copy(r_r[:, tiles[0]:tiles[-1] + 1, :].rearrange("p t d -> p (t d)"),
                                bank[b][:, 0:len(tiles) * D]).then_inc(rr_ok, 1)

            def spread_cols(v):
                return v[:, :].rearrange("p (t o) -> p t o", o=1).to_broadcast([P, NT, D])

            def layer_norm(dst, ok, base):
                dve.tensor_reduce(mean[:, :], r_r[:, :, :], AX_X, ALU.add).then_inc(ln, 1)
                dve.wait_ge(ln, base + 1)
                dve.tensor_scalar(mean[:, :], mean[:, :], 1.0 / D, None, ALU.mult).then_inc(ln, 1)
                dve.wait_ge(ln, base + 2)
                dve.tensor_tensor(r_r[:, :, :], r_r[:, :, :], spread_cols(mean), ALU.subtract).then_inc(ln, 1)
                dve.wait_ge(ln, base + 3)
                dve.tensor_tensor(sq_r, r_r[:, :, :], r_r[:, :, :], ALU.mult).then_inc(ln, 1)
                dve.wait_ge(ln, base + 4)
                dve.tensor_reduce(var[:, :], sq_r, AX_X, ALU.add).then_inc(ln, 1)
                dve.wait_ge(ln_sqrt, base // LN_STEPS + 1)
                dve.reciprocal(rstd[:, :], rstd[:, :]).then_inc(ln, 1)
                dve.wait_ge(ln, base + LN_STEPS)
                dve.tensor_tensor(dst, r_r[:, :, :], spread_cols(rstd), ALU.mult).then_inc(ok, 1)
            dve.wait_ge(rr_ok, len(ROW_TILES))
            layer_norm(x1_r[:, :, :], x1_ok, 0)

            dve.wait_ge(zeroed, 6)

            def outer(g, b, j):
                dve.wait_ge(shb_ps, g * NJ + (j + 1))
                if j == 0:
                    dve.wait_ge(xt_ok, g + 1)
                    used(dve, acc_ps, g)
                dve.tensor_tensor(z[:, b, j, :], bank[2 + (NJ * b + j) % 2][:, :], xt[:, b, :], ALU.mult
                                  ).then_inc(z_ok, 1)

            def key_query(g, b):
                dve.wait_ge(wk_ps, g + 1)
                dve.wait_ge(qt_ok, g + 1)
                used(dve, kq_ok, g)
                dve.scalar_tensor_tensor(out=wkq[:, b, :], in0=ps_xw[:, :], scalar=b2k[:, :], in1=qt[:, b, :],
                                         op0=ALU.add, op1=ALU.mult).then_inc(wkq_ok, 1)

            def weigh(g, b):
                dve.wait_ge(acc_ps, g + 1)
                dve.wait_ge(wkq_ok, g + 1)
                used(dve, att_ps, g)
                dve.tensor_tensor(kq[:, b, :], ps_k[:, :], wkq[:, b, :], ALU.mult).then_inc(kq_ok, 1)
                dve.wait_ge(wv_ok, g + 1)
                dve.tensor_tensor(val[:, b, :], ps_v[:, :], wv[:, b, :], ALU.mult).then_inc(val_ok, 1)

            def maxima(g, b):
                dve.wait_ge(att_ps, g + 1)
                arrived(dve, rs_in, g, b)
                if not isinstance(g, int) or g >= 1:
                    dve.wait_ge(mx_ok, g)
                    dve.wait_ge(dm_ok, g * 2)
                dve.tensor_tensor_scan(mx[:, b, :], rs[:, b, :], ps_qa[:, :], mx[:, 1 - b, G - 1:G],
                                       ALU.add, ALU.max).then_inc(mx_ok, 1)

            def below(g, b):
                dve.wait_ge(mx_ok, g + 1)
                used(dve, ex_ok, g)
                dve.tensor_tensor(am[:, b, :], ps_qa[:, :], mx[:, b, :], ALU.subtract).then_inc(am_ok, 1)

            def weigh_values(g, b):
                dve.wait_ge(ex_ok, g + 1)
                dve.wait_ge(val_ok, g + 1)
                dve.tensor_tensor(val[:, b, :], val[:, b, :], ex[:, b, :], ALU.mult).then_inc(ev_ok, 1)

            def sum_values(g, b):
                dve.wait_ge(ev_ok, g + 1)
                dve.wait_ge(dec_ok, g + 1)
                if not isinstance(g, int) or g >= 1:
                    dve.wait_ge(num_ok, g)
                used(dve, row_ps, g, 2)
                dve.tensor_tensor_scan(num[:, b, :], dec[:, b, :], val[:, b, :], num[:, 1 - b, G - 1:G],
                                       ALU.mult, ALU.add).then_inc(num_ok, 1)

            def sum_exponents(g, b):
                if not isinstance(g, int) or g >= 1:
                    dve.wait_ge(den_ok, g)
                dve.tensor_tensor_scan(den[:, b, :], dec[:, b, :], ex[:, b, :], den[:, 1 - b, G - 1:G],
                                       ALU.mult, ALU.add).then_inc(den_ok, 1)

            def body(t, b):
                if live(t - 1):
                    weigh(t - 1, 1 - b)
                if live(t + 1):
                    outer(t + 1, 1 - b, 0)
                if live(t - 2):
                    weigh_values(t - 2, b)
                if live(t + 1):
                    outer(t + 1, 1 - b, 1)
                if live(t + 1):
                    key_query(t + 1, 1 - b)
                if live(t - 2):
                    sum_values(t - 2, b)
                if live(t + 1):
                    outer(t + 1, 1 - b, 2)
                if live(t - 2):
                    sum_exponents(t - 2, b)
                if live(t - 1):
                    maxima(t - 1, 1 - b)
                if live(t + 1):
                    outer(t + 1, 1 - b, 3)
                if live(t - 1):
                    below(t - 1, 1 - b)
                if live(t + 1):
                    outer(t + 1, 1 - b, 4)
            steps(dve, body)

            dve.wait_ge(nrow_in, 16 * NT)
            dve.tensor_tensor(end_rows[:, :, :], end_rows[:, :, :],
                              has[:, :].rearrange("p (t o) -> p t o", o=1).to_broadcast([P, NT, RW]), ALU.mult
                              ).then_inc(upd_step, 1)
            dve.wait_ge(upd_step, 1)
            dve.tensor_scalar(rden[:, :, :], end_rows[:, :, O:RW], 1e-16, None, ALU.add).then_inc(upd_step, 1)
            dve.wait_ge(upd_step, 2)
            dve.reciprocal(rden[:, :, :], rden[:, :, :]).then_inc(upd_step, 1)
            dve.wait_ge(upd_step, 3)
            heads = end_rows[:, :, 0:O].rearrange("p t (h d) -> p t h d", h=H)
            dve.tensor_tensor(heads, heads, rden[:, :, :].rearrange("p t (h o) -> p t h o", o=1)
                              .to_broadcast([P, NT, H, DH]), ALU.mult).then_inc(upd_step, 1)
            for n, (lo, w) in enumerate(NODE_BLOCKS):
                dve.wait_ge(o_ps, n + 1)
                dve.tensor_copy(h_t[:, lo:lo + w], bank[n][0:D, 0:w]).then_inc(o_ok, 1)
            dve.wait_ge(o_ok, len(NODE_BLOCKS))
            dve.tensor_reduce(bnc[:, 0:1], h_t[:, 0:N], AX_X, ALU.add).then_inc(bn, 1)
            dve.wait_ge(bn, 1)
            dve.tensor_scalar(bnc[:, 1:2], bnc[:, 0:1], 1.0 / N, None, ALU.mult).then_inc(bn, 1)
            dve.wait_ge(bn, 2)
            dve.tensor_scalar(h_t[:, :], h_t[:, :], bnc[:, 1:2], None, ALU.subtract).then_inc(bn, 1)
            dve.wait_ge(bn, 3)
            dve.tensor_tensor(sg_t[:, :], h_t[:, :], h_t[:, :], ALU.mult).then_inc(bn, 1)
            dve.wait_ge(bn, 4)
            dve.tensor_reduce(bnc[:, 2:3], sg_t[:, 0:N], AX_X, ALU.add).then_inc(bn, 1)
            dve.wait_ge(bn_sqrt, 1)
            dve.reciprocal(bnc[:, 4:5], bnc[:, 3:4]).then_inc(bn, 1)
            dve.wait_ge(bn, 6)
            dve.tensor_tensor(bnc[:, 5:6], bnc[:, 4:5], gamma[:, :], ALU.mult).then_inc(bn, 1)
            dve.wait_ge(bn, 7)
            dve.tensor_scalar(h_t[:, :], h_t[:, :], bnc[:, 5:6], beta[:, :], ALU.mult, ALU.add).then_inc(bn, 1)
            for b, tiles in ROW_TILES:
                dve.wait_ge(y_ps, b + 1)
                dve.tensor_tensor(r_r[:, tiles[0]:tiles[-1] + 1, :],
                                  bank[b][:, 0:len(tiles) * D].rearrange("p (t d) -> p t d", d=D),
                                  x1_r[:, tiles[0]:tiles[-1] + 1, :], ALU.add).then_inc(rr_ok, 1)
            dve.wait_ge(rr_ok, 2 * len(ROW_TILES))
            layer_norm(r_r[:, :, :], out_ok, LN_STEPS)


def kernel(**inputs):
    import numpy as _np
    import concourse.bacc as _bacc
    from concourse import mybir as _mybir
    from concourse.bass_utils import run_bass_kernel_spmd as _run

    v = {k: _np.asarray(x) for k, x in inputs.items()}
    l1 = lambda name: v["L1_gnn_" + name]
    pad = EP - E
    src = _np.pad(v["src"], (0, pad))
    dst = _np.pad(v["dst"], (0, pad), constant_values=N)
    ea = _np.pad(v["edge_attr_64"], ((0, pad), (0, 0)))
    sh = _np.pad(v["edge_attr_9"], ((0, pad), (0, 0)))
    k, m = _np.arange(P)[:, None], _np.arange(P)[None, :]
    s27 = _np.arange(SP3)[:, None] % S
    col = _np.arange(NJ * P)[None, :]
    arrays = {
        "x": _np.pad(v["x"], ((0, NP - N), (0, 0))),
        "src_t": src.reshape(NK, P).T, "dst_t": dst.reshape(NK, P).T,
        "dst_lin": _np.pad(dst, (1, 0), constant_values=-1),
        "ea_t": ea.T, "sh_t": sh.T,
        "c_k": l1("Cqk").transpose(1, 0, 2).reshape(S * D, O), "c_v": l1("Cv").transpose(1, 0, 2).reshape(S * D, O),
        "k_w1": l1("k_w1"), "v_w1": l1("v_w1"), "k_w2": l1("k_w2"), "v_w2": l1("v_w2"),
        "k_b1": l1("k_b1")[:, None], "v_b1": l1("v_b1")[:, None],
        "k_b2": l1("k_b2")[:, None], "v_b2": l1("v_b2")[:, None],
        "w1": v["L0_gnn_W1"], "b1": v["L0_gnn_b1"][:, None], "u0": v["L0_gnn_u"][0][:, None],
        "w2": v["L0_gnn_W2"], "b2": v["L0_gnn_b2"][:, None],
        "wq": l1("Wq"), "wout": l1("W_out"), "wself": l1("W_self"),
        "gamma": l1("gamma")[:, None], "beta": l1("beta")[:, None],
        "ident": (k == m).astype(_np.float32),
        "headones": (k // DH == m // DH).astype(_np.float32),
        "headpick": (k == DH * m[:, 0:H]).astype(_np.float32),
        "iota_row": (m + 0 * k).astype(_np.float32),
        "upper": (k < m).astype(_np.float32),
        "sel": (s27 == _np.minimum(2 * (col // P) + col % P // D, S - 1)).astype(_np.float32),
    }
    nc = _bacc.Bacc("TRN2", target_bir_lowering=False, num_devices=1)
    feed, aps = {}, {}
    for name, x in arrays.items():
        x = _np.ascontiguousarray(x)
        feed[f"in_{name}"] = x
        aps[name] = nc.dram_tensor(f"in_{name}", x.shape, _mybir.dt.from_np(x.dtype), kind="ExternalInput").ap()
    out = nc.dram_tensor("out_x", (NP, D), _mybir.dt.float32, kind="ExternalOutput").ap()
    gnn_two_layers(nc, aps, out)
    r = _run(nc, [feed], core_ids=[0])
    return r.results[0]["out_x"][0:N]
```

```python
from contextlib import ExitStack

import concourse.bass as bass
from concourse import mybir

ALU = mybir.AluOpType
ACT = mybir.ActivationFunctionType
AX_X = mybir.AxisListType.X
F32 = mybir.dt.float32
BF16 = mybir.dt.bfloat16
F32R = mybir.dt.float32r
I32 = mybir.dt.int32

P = 128
N = 3125
D = 64
NT = (N + P) // P
NP = NT * P
E = 100000
G = 512
NG = -(-E // G)
EP = NG * G
NK = EP // P
S = 9
SP3 = 3 * S
CK, CV, C8, W2KV = 0, 4, 8, 9
NW = 10
NJ = 5
H = 8
DH = 16
O = H * DH
RW = O + H
W = 2048
NC = EP // W
WJ = W // P
NODE_BLOCKS = [(b, min(G, NP - b)) for b in range(0, NP, G)]
OH = 8
NOH = NK // OH
LN_STEPS = 6
RS_SRC, RS_DST = D + S, D + S + 1
RSW = D + S + 2
SORT2 = 12
FAR = 3.0e38
EPS = 1e-5


def gnn_two_layers(nc, a, out):
    ctx = ExitStack()
    with ctx:
        def sb(name, shape, dt=F32):
            return ctx.enter_context(nc.sbuf_tensor(name, shape, dt))

        def sem(name):
            return ctx.enter_context(nc.semaphore(name))

        def dram(name, shape, dt=F32):
            return nc.dram_tensor(name, shape, dt, kind="Internal").ap()

        keep_d = dram("keep_d", [EP], BF16)
        reset_d = dram("reset_d", [EP], BF16)
        sh3_d = dram("sh3_d", [3, S, EP], BF16)
        aggrow_d = dram("aggrow_d", [EP, D])
        xtab_d = dram("xtab_d", [NP, 2 * D])
        qtab_d = dram("qtab_d", [NP, O])
        nrow_d = dram("nrow_d", [EP, RW])

        rows_s = dram("rows_s", [EP, RSW])
        ea_s = dram("ea_s", [D, EP])
        sh_s = dram("sh_s", [S, EP])
        dst_s = dram("dst_s", [EP + 1], I32)

        ident = sb("ident", [P, P])
        headones = sb("headones", [P, O])
        iota_row = sb("iota_row", [P, P])
        upper = sb("upper", [P, P])
        lower = sb("lower", [P, P])
        ones = sb("ones", [P, P])
        sel_f = sb("sel_f", [SP3, NJ * P])
        sel = sb("sel", [SP3, NJ, P], BF16)
        wt_h = sb("wt_h", [P, NW, O], F32R)
        wt_l = sb("wt_l", [P, NW, O], F32R)
        w1kv = sb("w1kv", [D, P])
        b1kv = sb("b1kv", [P, 1])
        b2k = sb("b2k", [P, 1])
        b2v = sb("b2v", [P, 1])
        w1 = sb("w1", [P, D])
        w1u = sb("w1u", [D, D])
        b1 = sb("b1", [D, 1])
        u0 = sb("u0", [D, 1])
        w2 = sb("w2", [D, D])
        b2 = sb("b2", [D, 1])
        wq = sb("wq", [D, O])
        wout = sb("wout", [P, D])
        wself = sb("wself", [D, D])
        gamma = sb("gamma", [D, 1])
        beta = sb("beta", [D, 1])

        src_t = sb("src_t", [P, NK], I32)
        dst_t = sb("dst_t", [P, NK], I32)
        has = sb("has", [P, NT])
        end_i = sb("end_i", [P, NT], I32)

        x_r = sb("x_r", [P, NT, 2 * D])
        xa_t = sb("xa_t", [P, NP])
        h_t = sb("h_t", [D, NP])
        r_r = sb("r_r", [P, NT, D])
        x1_r = sb("x1_r", [P, NT, D])
        x1_t = sb("x1_t", [D, NP])
        sq_r = x_r[:, :, 0:D]
        sg_t = x_r[0:D, :, :].rearrange("p t d -> p (t d)")
        free = x_r[:, :, :].rearrange("p t o -> p (t o)")
        so_lo, so_bc, so_prod = (free[:, i * P:(i + 1) * P] for i in range(3))
        so_hi = free[:, 3 * P:3 * P + NT]
        so_hit, so_count, so_cum = (free[0:NT, (4 + i) * P:(5 + i) * P] for i in range(3))
        so_row, so_turn = free[:, 7 * P:7 * P + RSW], free[0:D + S, 8 * P:9 * P]
        so_before = free[0:NT, 9 * P:9 * P + 1]
        so_dst, so_rank, so_base, so_posf = (free[:, 9 * P + 1 + i:9 * P + 2 + i] for i in range(4))
        so_pos = sb("so_pos", [P, 1], I32)
        bad_col = sb("bad_col", [P, 1])
        bad = sb("bad", [1, 1], I32)
        mean = sb("mean", [P, NT])
        var = sb("var", [P, NT])
        rstd = sb("rstd", [P, NT])
        b1e = sb("b1e", [D, 1])
        epst = sb("epst", [P, 1])
        bnc = sb("bnc", [D, 8])

        early_ctx = ExitStack()

        def early(name, shape, dt=F32):
            return early_ctx.enter_context(nc.sbuf_tensor(name, shape, dt))

        d_prev = early("d_prev", [P, NK], I32)
        d_this = early("d_this", [P, NK], I32)
        keep = early("keep", [P, NK], BF16)
        reset = early("reset", [P, NK], BF16)
        lo_i = early("lo_i", [P, NK], I32)
        hi_i = early("hi_i", [P, NK], I32)
        lo_f = early("lo_f", [P, NK])
        hi_f = early("hi_f", [P, NK])
        oh_lo = early("oh_lo", [P, 2, OH, P], BF16)
        oh_hi = early("oh_hi", [P, 2, OH, NT], BF16)
        count = early("count", [NT, P])
        cum = early("cum", [NT, P])
        before = early("before", [NT, 1])
        count_t = early("count_t", [P, NT])
        end_f = early("end_f", [P, NT])

        wt = early("wt", [P, NW, O])

        SC = 14
        SW = EP // SC
        shf = early("shf", [S * SC, SW])
        shp = early("shp", [S * SC, SW], BF16)

        ea_all = early("ea_all", [P, 2 * W])
        ea_c = ea_all[0:D, :].rearrange("d (b w) -> d b w", b=2)
        q_r = ea_all[:, 0:NT * O].rearrange("p (t o) -> p t o", t=NT)
        keep_c = early("keep_c", [D, 2, W], BF16)
        run_c = early("run_c", [D, 2, W])

        early_ctx.close()
        row_c = xa_t[:, 0:2 * WJ * D].rearrange("p (b w) -> p b w", b=2)

        ea = sb("ea", [D, 2, G])
        s3 = sb("s3", [SP3, 2, G], BF16)
        rs = sb("rs", [P, 2, G], BF16)
        gathered = sb("gathered", [P, 2 * 4 * 4 * P])
        rings = gathered[:, :].rearrange("p (r q k d) -> p r q k d", r=2, q=4, k=4)
        xg, qg = rings[:, 0], rings[:, 1]
        end_rows = gathered[:, 0:NT * RW].rearrange("p (t w) -> p t w", t=NT)
        src_g = sb("src_g", [P, 4, 4], I32)
        dst_g = sb("dst_g", [P, 4, 4], I32)
        xt = sb("xt", [P, 2, G])
        hid = sb("hid", [P, G])
        hid_h = sb("hid_h", [P, 2, G], F32R)
        hid_l = sb("hid_l", [P, 2, G], F32R)
        qt = sb("qt", [P, 2, G])
        wv = sb("wv", [P, 2, G])
        x_flat = x_r[:, :, :].rearrange("p t d -> p (t d)")
        z = xa_t[:, 0:NJ * G].rearrange("p (j g) -> p j g", j=NJ)
        num = x_flat[:, 0:2 * G].rearrange("p (b g) -> p b g", b=2)
        den = x_flat[:, 2 * G:4 * G].rearrange("p (b g) -> p b g", b=2)
        row = x_flat[:, 4 * G:4 * G + 8 * RW].rearrange("p (b j w) -> p b j w", b=2, j=4)
        z_h = sb("z_h", [P, 2, NJ, G], F32R)
        z_l = sb("z_l", [P, 2, NJ, G], F32R)
        kq = sb("kq", [P, 2, G])
        val = sb("val", [P, 2, G])
        mx = sb("mx", [P, 2, G])
        ex = sb("ex", [P, 2, G])
        dm = sb("dm", [P, 2, G])
        rden = sb("rden", [P, NT, H])

        bank = [ctx.enter_context(nc.psum_tensor(f"bank{i}", [P, G], F32)) for i in range(8)]
        ps_xw, ps_hw, ps_s0, ps_s1, ps_k, ps_v, ps_qa, ps_r = bank

        bad_step = sem("bad_step")
        bad_ps = sem("bad_ps")
        bad_ok = sem("bad_ok")
        so1 = sem("so1")
        so1_ps = sem("so1_ps")
        so_off = sem("so_off")
        so_off_ps = sem("so_off_ps")
        so2 = sem("so2")
        so2_turned = sem("so2_turned")
        so2_ps = sem("so2_ps")
        so_row_in = sem("so_row_in")
        so_placed = sem("so_placed")
        so3_in = sem("so3_in")
        so3_ps = sem("so3_ps")
        so3 = sem("so3")
        so3_out = sem("so3_out")
        so_first = sem("so_first")
        resorted = sem("resorted")
        hilo2 = sem("hilo2")
        loaded = sem("loaded")
        dlin_in = sem("dlin_in")
        tabs_in = sem("tabs_in")
        sh_in = sem("sh_in")
        x_in = sem("x_in")
        flags_done = sem("flags_done")
        flags_out = sem("flags_out")
        split_done = sem("split_done")
        split_step = sem("split_step")
        split_out = [sem(f"split_out{i}") for i in range(3)]
        sel_done = sem("sel_done")
        hilo = sem("hilo")
        onehot = sem("onehot")
        counted = sem("counted")
        hist_ps = sem("hist_ps")
        hist_ok = sem("hist_ok")
        ends_ok = sem("ends_ok")
        chunk_in = [sem(f"chunk_in{i}") for i in range(2)]
        chunk_run = sem("chunk_run")
        chunk_ps = sem("chunk_ps")
        chunk_row = sem("chunk_row")
        chunk_out = [sem(f"chunk_out{i}") for i in range(2)]
        agg_in = sem("agg_in")
        masked = sem("masked")
        b1e_ps = sem("b1e_ps")
        b1e_ok = sem("b1e_ok")
        xat_ps = sem("xat_ps")
        xat_ok = sem("xat_ok")
        h1_ps = sem("h1_ps")
        h1_sig = sem("h1_sig")
        h1_ok = sem("h1_ok")
        h2_ps = sem("h2_ps")
        h2_sig = sem("h2_sig")
        h2_ok = sem("h2_ok")
        res_ok = sem("res_ok")
        rr_ps = sem("rr_ps")
        rr_ok = sem("rr_ok")
        ln = sem("ln")
        ln_sqrt = sem("ln_sqrt")
        x1_ok = sem("x1_ok")
        x1t_ps = sem("x1t_ps")
        x1t_ok = sem("x1t_ok")
        q_ps = sem("q_ps")
        q_ok = sem("q_ok")
        tab_out = sem("tab_out")
        ea_in = [sem(f"ea_in{i}") for i in range(2)]
        s3_in = [sem(f"s3_in{i}") for i in range(2)]
        rs_in = [sem(f"rs_in{i}") for i in range(2)]
        xg_in = [sem(f"xg_in{i}") for i in range(4)]
        qg_in = [sem(f"qg_in{i}") for i in range(4)]
        src_picked = sem("src_picked")
        dst_picked = sem("dst_picked")
        xt_ps = sem("xt_ps")
        xt_ok = sem("xt_ok")
        hid_ps = sem("hid_ps")
        hid_ok = sem("hid_ok")
        qt_ps = sem("qt_ps")
        qt_ok = sem("qt_ok")
        wk_ps = sem("wk_ps")
        wkq_ok = sem("wkq_ok")
        wv_ps = sem("wv_ps")
        wv_ok = sem("wv_ok")
        shb_ps = sem("shb_ps")
        z_ok = sem("z_ok")
        zh_ok = sem("zh_ok")
        zl_ok = sem("zl_ok")
        hidl_ok = sem("hidl_ok")
        wth_ok = sem("wth_ok")
        wtl_ok = sem("wtl_ok")
        acc_ps = sem("acc_ps")
        kq_ok = sem("kq_ok")
        val_ok = sem("val_ok")
        att_ps = sem("att_ps")
        mx_ok = sem("mx_ok")
        am_ok = sem("am_ok")
        ex_ok = sem("ex_ok")
        dm_ok = sem("dm_ok")
        dmr_ok = sem("dmr_ok")
        dec_ok = sem("dec_ok")
        ev_ok = sem("ev_ok")
        num_ok = sem("num_ok")
        den_ok = sem("den_ok")
        row_ps = sem("row_ps")
        row_ok = sem("row_ok")
        row_out = [sem(f"row_out{i}") for i in range(2)]
        zeroed = sem("zeroed")
        nrow_in = sem("nrow_in")
        upd_step = sem("upd_step")
        upd_ps = sem("upd_ps")
        upd_ok = sem("upd_ok")
        o_ps = sem("o_ps")
        o_ok = sem("o_ok")
        bn = sem("bn")
        bn_sqrt = sem("bn_sqrt")
        y_ps = sem("y_ps")
        out_ok = sem("out_ok")
        stored = sem("stored")

        block = ctx.enter_context(nc.Block())

        WEIGHTS = [(ident, a["ident"]), (headones, a["headones"]),
                   (iota_row, a["iota_row"]), (upper, a["upper"]), (lower, a["lower"]), (sel_f, a["sel"]),
                   (wt[:, CK:CK + 4, :], a["c_k"][0:8 * D, :].rearrange("(j p) o -> p j o", p=P)),
                   (wt[:, CV:CV + 4, :], a["c_v"][0:8 * D, :].rearrange("(j p) o -> p j o", p=P)),
                   (wt[0:D, C8, :], a["c_k"][8 * D:9 * D, :]), (wt[D:P, C8, :], a["c_v"][8 * D:9 * D, :]),
                   (w1kv[:, 0:D], a["k_w1"]), (w1kv[:, D:P], a["v_w1"]),
                   (wt[0:D, W2KV, :], a["k_w2"]), (wt[D:P, W2KV, :], a["v_w2"]),
                   (b1kv[0:D, :], a["k_b1"]), (b1kv[D:P, :], a["v_b1"]), (b2k, a["k_b2"]), (b2v, a["v_b2"]),
                   (w1, a["w1"][0:P, :]), (w1u, a["w1"][P:P + D, :]), (b1, a["b1"]), (u0, a["u0"]),
                   (w2, a["w2"]), (b2, a["b2"]), (wq, a["wq"]), (wout, a["wout"]), (wself, a["wself"]),
                   (gamma, a["gamma"]), (beta, a["beta"])]
        ALL_WEIGHTS = 16 * len(WEIGHTS)

        def live(g):
            return not isinstance(g, int) or 0 <= g < NG

        def used(eng, s, g, per=1):
            if not isinstance(g, int) or g >= 2:
                eng.wait_ge(s, (g - 1) * per)

        def steps(eng, body):
            for t in range(-2, 4):
                body(t, t % 2, t % 4)
            with eng.Fori(0, (NG - 8) // 4) as i:
                for r in range(4):
                    body(i * 4 + (4 + r), r % 2, r)
            for t in range(NG - 4, NG + 2):
                body(t, t % 2, t % 4)

        def carry(ins, s, n):
            return ins.wait_op(s, n, "sem-ge")

        def arrived(eng, ring, g, b, per=16):
            n = len(ring)
            if isinstance(g, int):
                eng.wait_ge(ring[b], (g // n + 1) * per)
            else:
                eng.wait_ge(ring[b], (g - b + n) * (per // n))

        def loads_and_stores(sp, edges_t):
            sp.dma_start(x_r[:, :, 0:D], a["x"].rearrange("(t p) d -> p t d", p=P)).then_inc(x_in, 16)
            sp.wait_ge(flags_done, 2)
            sp.dma_start(keep_d.rearrange("(p c) -> p c", p=P), keep[:, :]).then_inc(flags_out, 16)
            sp.dma_start(reset_d.rearrange("(p c) -> p c", p=P), reset[:, :]).then_inc(flags_out, 16)
            sp.wait_ge(flags_out, 32)

            def load_chunk(c, b):
                lo = c * W
                if not isinstance(c, int) or c >= 2:
                    sp.wait_ge(chunk_run, c - 1)
                sp.dma_start(ea_c[:, b, :], edges_t[:, bass.ds(lo, W)]).then_inc(chunk_in[b], 16)
                sp.dma_start(keep_c[:, b, :],
                             keep_d[bass.ds(lo, W)].rearrange("(o w) -> o w", o=1).to_broadcast([D, W])
                             ).then_inc(chunk_in[b], 16)

            def store_chunk(c, b):
                sp.wait_ge(chunk_row, c * 2 + 2)
                sp.dma_start(aggrow_d[bass.ds(c * W, W), :].rearrange("(p j) d -> p (j d)", p=P),
                             row_c[:, b, :]).then_inc(chunk_out[b], 16)

            load_chunk(0, 0)
            load_chunk(1, 1)
            with sp.Fori(0, (NC - 3) // 2) as i:
                for r in range(2):
                    load_chunk(i * 2 + (2 + r), r)
                    store_chunk(i * 2 + r, r)
            load_chunk(NC - 1, 0)
            store_chunk(NC - 3, 0)
            store_chunk(NC - 2, 1)
            store_chunk(NC - 1, 0)

            sp.wait_ge(x1_ok, 1)
            for half in range(2):
                sp.dma_start(xtab_d[:, half * D:(half + 1) * D].rearrange("(t p) d -> p t d", p=P),
                             x1_r[:, :, :]).then_inc(tab_out, 16)
            sp.wait_ge(q_ok, len(NODE_BLOCKS))
            sp.dma_start(qtab_d.rearrange("(t p) d -> p t d", p=P), q_r[:, :, :]).then_inc(tab_out, 16)

            sp.wait_ge(tab_out, 48)
            for part in range(3):
                sp.wait_ge(split_out[part], 16)

            def load_rs(g, b):
                used(sp, mx_ok, g)
                used(sp, dmr_ok, g)
                sp.dma_start(rs[:, b, :], reset_d[bass.ds(g * G, G)].rearrange("(o w) -> o w", o=1)
                             .to_broadcast([P, G])).then_inc(rs_in[b], 16)

            def load_edge(g, b):
                used(sp, shb_ps, g, NJ)
                used(sp, hid_ps, g)
                sp.dma_start(ea[:, b, :], edges_t[:, bass.ds(g * G, G)]).then_inc(ea_in[b], 16)
                sp.dma_start(s3[:, b, :], sh3_d.rearrange("a s e -> (a s) e")[:, bass.ds(g * G, G)]
                             ).then_inc(s3_in[b], 16)

            def store_row(g, b):
                sp.wait_ge(row_ok, g * 4 + 4)
                sp.dma_start(nrow_d[bass.ds(g * G, G), :].rearrange("(p j) w -> p (j w)", p=P),
                             row[:, b, :, :].rearrange("p j w -> p (j w)")).then_inc(row_out[b], 16)

            def body(t, b, q):
                if live(t + 2):
                    load_edge(t + 2, b)
                if live(t):
                    load_rs(t, b)
                if live(t - 2):
                    store_row(t - 2, b)
            steps(sp, body)

        @block.sync
        def _(sp):
            sp.dma_start(d_prev[:, :], a["dst_lin"][0:EP].rearrange("(p c) -> p c", p=P)).then_inc(dlin_in, 16)
            sp.dma_start(d_this[:, :], a["dst_lin"][1:EP + 1].rearrange("(p c) -> p c", p=P)).then_inc(dlin_in, 16)
            sp.dma_start(dst_t[:, :], a["dst_t"]).then_inc(tabs_in, 16)
            sp.dma_start(src_t[:, :], a["src_t"]).then_inc(tabs_in, 16)
            for dst, src in WEIGHTS:
                sp.dma_start(dst[:] if not isinstance(dst, bass.AP) else dst, src).then_inc(loaded, 16)

            sp.wait_ge(bad_ok, 1)
            unsorted = sp.value_load(bad[0:1, 0:1], min_val=0, max_val=1)
            with sp.If(unsorted == 1):
                with sp.Fori(0, NK) as k:
                    sp.dma_start(so_row[:, 0:D], a["ea_rows"][bass.ds(k * P, P), :]).then_inc(so_row_in, 16)
                    sp.dma_start(so_row[:, D:D + S], a["sh_rows"][bass.ds(k * P, P), :]).then_inc(so_row_in, 16)
                    for col, name in ((RS_SRC, "src_col"), (RS_DST, "dst_col")):
                        sp.dma_start(so_row[:, col:col + 1].bitcast(I32), a[name][bass.ds(k * P, P), :]
                                     ).then_inc(so_row_in, 16)
                    sp.wait_ge(so_placed, k * 16 + 16)
                    carry(sp.nop(nofuse=True), bad_ok, 1)
                with sp.Fori(0, NK) as k:
                    sp.dma_start(so_row, rows_s[bass.ds(k * P, P), :]).then_inc(so3_in, 16)
                    sp.wait_ge(so3, k * 3 + 3)
                    carry(sp.nop(nofuse=True), bad_ok, 1)
                    sp.dma_start(ea_s[:, bass.ds(k * P, P)], so_turn[0:D, :]).then_inc(so3_out, 16)
                    sp.dma_start(sh_s[:, bass.ds(k * P, P)], so_turn[D:D + S, :]).then_inc(so3_out, 16)
                    sp.dma_start(dst_s[bass.ds(k * P + 1, P)].rearrange("(p o) -> p o", o=1),
                                 so_row[:, RS_DST:RS_DST + 1].bitcast(I32)).then_inc(so3_out, 16)
                    sp.wait_ge(so3_out, k * 48 + 48)
                    carry(sp.nop(nofuse=True), bad_ok, 1)
                sp.dma_start(dst_s[0:1], a["dst_lin"][0:1]).then_inc(so_first, 16)
                sp.wait_ge(so_first, 16)
                sp.dma_start(d_prev[:, :], dst_s[0:EP].rearrange("(p c) -> p c", p=P)).then_inc(resorted, 16)
                sp.dma_start(d_this[:, :], dst_s[1:EP + 1].rearrange("(p c) -> p c", p=P)).then_inc(resorted, 16)
                sp.dma_start(shf[:, :], sh_s.rearrange("s (c w) -> (s c) w", c=SC)).then_inc(sh_in, 16)
                loads_and_stores(sp, ea_s)
            with sp.Else():
                sp.dma_start(shf[:, :], a["sh_t"].rearrange("s (c w) -> (s c) w", c=SC)).then_inc(sh_in, 16)
                loads_and_stores(sp, a["ea_t"])
            sp.wait_ge(out_ok, 1)
            sp.dma_start(out.rearrange("(t p) d -> p t d", p=P), r_r[:, :, :]).then_inc(stored, 16)
            sp.wait_ge(stored, 16)

        @block.gpsimd
        def _(pool):
            pool.memset(ones[:, :], 1.0).then_inc(zeroed, 1)
            pool.memset(epst[:, :], EPS).then_inc(zeroed, 1)
            pool.memset(run_c[:, 1, W - 1:W], 0.0).then_inc(zeroed, 1)

            pool.wait_ge(bad_ok, 1)
            unsorted = pool.value_load(bad[0:1, 0:1], min_val=0, max_val=1)
            with pool.If(unsorted == 1):
                with pool.Fori(0, NK) as k:
                    pool.wait_ge(so2, k * SORT2 + (SORT2 - 1))
                    pool.wait_ge(so_row_in, k * 64 + 64)
                    carry(pool.indirect_dma_start(rows_s[:, :], bass.IndirectOffsetOnAxis(ap=so_pos[:, 0:1], axis=0),
                                                  so_row, None), bad_ok, 1).then_inc(so_placed, 16)
                pool.wait_ge(so3, 3 * NK)

            pool.wait_ge(ends_ok, 2)
            pool.wait_ge(chunk_out[0], 16 * ((NC + 1) // 2))
            pool.wait_ge(chunk_out[1], 16 * (NC // 2))
            for t in range(NT):
                pool.indirect_dma_start(x_r[:, t, D:2 * D], None, aggrow_d[:, :],
                                        bass.IndirectOffsetOnAxis(ap=end_i[:, t:t + 1], axis=0)).then_inc(agg_in, 16)

            pool.wait_ge(tab_out, 48)
            for part in range(3):
                pool.wait_ge(split_out[part], 16)
            for scanned in (mx, num, den):
                pool.memset(scanned[:, 1, G - 1:G], 0.0).then_inc(zeroed, 1)
            pool.wait_ge(tabs_in, 32)

            def gather(g, b, rows, ring, table, index, picked, picks, read):
                if not isinstance(g, int) or g >= 4:
                    arrived(pool, ring, g - 4, b, 64)
                pool.tensor_copy(picked[:, b, :], index[:, bass.ds(g * 4, 4)]).then_inc(picks, 1)
                if not isinstance(g, int) or g >= 4:
                    pool.wait_ge(read, g - 3)
                pool.wait_ge(picks, g + 1)
                for k in range(4):
                    rows_in = pool.indirect_dma_start(rows[:, b, k, :], None, table,
                                                      bass.IndirectOffsetOnAxis(ap=picked[:, b, k:k + 1], axis=0))
                    if k == 0:
                        carry(rows_in, tab_out, 48)
                    rows_in.then_inc(ring[b], 16)

            def gather_x(g, b):
                gather(g, b, xg, xg_in, xtab_d[:, :], src_t, src_g, src_picked, xt_ps)

            def gather_q(g, b):
                gather(g, b, qg, qg_in, qtab_d[:, :], dst_t, dst_g, dst_picked, qt_ps)

            def shift(g, b):
                pool.wait_ge(mx_ok, g + 1)
                used(pool, den_ok, g)
                pool.tensor_tensor(dm[:, b, 1:G], mx[:, b, 0:G - 1], mx[:, b, 1:G], ALU.subtract).then_inc(dm_ok, 1)
                pool.tensor_tensor(dm[:, b, 0:1], mx[:, 1 - b, G - 1:G], mx[:, b, 0:1], ALU.subtract
                                   ).then_inc(dm_ok, 1)
                arrived(pool, rs_in, g, b)
                pool.wait_ge(dm_ok, g * 2 + 2)
                pool.tensor_tensor(dm[:, b, :], dm[:, b, :], rs[:, b, :], ALU.add).then_inc(dmr_ok, 1)

            def body(t, b, q):
                if live(t + 4):
                    gather_x(t + 4, q)
                if live(t + 3):
                    gather_q(t + 3, (q + 3) % 4)
                if live(t - 1):
                    shift(t - 1, 1 - b)
            for g in range(2):
                gather_x(g, g)
            gather_q(0, 0)
            steps(pool, body)

            pool.wait_ge(row_out[0], 16 * (NG // 2))
            pool.wait_ge(row_out[1], 16 * (NG // 2))
            for t in range(NT):
                pool.indirect_dma_start(end_rows[:, t, :], None, nrow_d[:, :],
                                        bass.IndirectOffsetOnAxis(ap=end_i[:, t:t + 1], axis=0)).then_inc(nrow_in, 16)


        ROW_TILES = [(b, list(range(8 * b, min(8 * b + 8, NT)))) for b in range(-(-NT // 8))]

        @block.scalar
        def _(act):
            act.wait_ge(loaded, ALL_WEIGHTS)
            act.activation(sel[:, :, :].rearrange("k j m -> k (j m)"), sel_f[:, :], ACT.Copy).then_inc(sel_done, 1)

            act.activation(wt_h[:, :, :], wt[:, :, :], ACT.Copy).then_inc(wth_ok, 1)

            act.wait_ge(sh_in, 16)
            for part in range(3):
                if part > 0:
                    act.wait_ge(split_step, part)
                    act.wait_ge(split_out[part - 1], 16)
                act.activation(shp[:, :], shf[:, :], ACT.Copy).then_inc(split_done, 1)
                act.wait_ge(split_done, part + 1)
                act.dma_start(sh3_d[part].rearrange("s (c w) -> (s c) w", c=SC), shp[:, :]
                              ).then_inc(split_out[part], 16)

            def rows_out(c, b):
                if not isinstance(c, int) or c >= 2:
                    arrived(act, chunk_out, c - 2, b)
                for h in range(2):
                    act.wait_ge(chunk_ps, c * 2 + (h + 1))
                    act.activation(row_c[:, b, h * G:(h + 1) * G], bank[2 * b + h][:, :], ACT.Copy
                                   ).then_inc(chunk_row, 1)
            rows_out(0, 0)
            rows_out(1, 1)
            with act.Fori(0, (NC - 3) // 2) as i:
                for r in range(2):
                    rows_out(i * 2 + (2 + r), r)
            rows_out(NC - 1, 0)

            for n, (lo, w) in enumerate(NODE_BLOCKS):
                act.wait_ge(xat_ps, n + 1)
                act.activation(xa_t[:, lo:lo + w], bank[n][:, 0:w], ACT.Copy).then_inc(xat_ok, 1)
            act.wait_ge(b1e_ok, 1)
            for n, (lo, w) in enumerate(NODE_BLOCKS):
                act.wait_ge(h1_ps, n + 1)
                act.activation(sg_t[:, lo:lo + w], bank[n][0:D, 0:w], ACT.Sigmoid, bias=b1e[:, :]
                               ).then_inc(h1_sig, 1)
            for n, (lo, w) in enumerate(NODE_BLOCKS):
                act.wait_ge(h2_ps, n + 1)
                act.wait_ge(h1_ok, n + 1)
                act.activation(sg_t[:, lo:lo + w], bank[n][0:D, 0:w], ACT.Sigmoid, bias=b2[:, :]
                               ).then_inc(h2_sig, 1)
            act.wait_ge(ln, 5)
            act.activation(rstd[:, :], var[:, :], ACT.Sqrt, scale=1.0 / D, bias=epst[:, :]).then_inc(ln_sqrt, 1)
            for n, (lo, w) in enumerate(NODE_BLOCKS):
                act.wait_ge(x1t_ps, n + 1)
                act.activation(x1_t[:, lo:lo + w], bank[n][0:D, 0:w], ACT.Copy).then_inc(x1t_ok, 1)
            for n, (lo, w) in enumerate(NODE_BLOCKS):
                act.wait_ge(q_ps, n + 1)
                act.activation(q_r[:, lo // P:(lo + w) // P, :].rearrange("p t o -> p (t o)"),
                               bank[n][:, 0:w], ACT.Copy).then_inc(q_ok, 1)

            def front_x(g, b):
                act.wait_ge(xt_ps, g + 1)
                used(act, z_ok, g, NJ)
                act.activation(xt[:, b, :], ps_xw[:, :], ACT.Copy).then_inc(xt_ok, 1)

            def front_h(g, b):
                act.wait_ge(hid_ps, g + 1)
                if not isinstance(g, int) or g >= 1:
                    act.wait_ge(hidl_ok, g)
                act.activation(hid[:, :], ps_hw[:, :], ACT.Relu, bias=b1kv[:, :]).then_inc(hid_ok, 1)
                used(act, wv_ps, g)
                act.activation(hid_h[:, b, :], ps_hw[:, :], ACT.Relu, bias=b1kv[:, :]).then_inc(hid_ok, 1)

            def outer_high(g, b, j):
                if j == 0:
                    used(act, acc_ps, g)
                act.wait_ge(z_ok, g * NJ + (j + 1))
                act.activation(z_h[:, b, j, :], z[:, j, :], ACT.Copy).then_inc(zh_ok, 1)

            def front_q(g, b):
                act.wait_ge(qt_ps, g + 1)
                used(act, kq_ok, g)
                act.activation(qt[:, b, :], ps_qa[:, :], ACT.Copy).then_inc(qt_ok, 1)

            def weights_v(g, b):
                act.wait_ge(wv_ps, g + 1)
                used(act, val_ok, g)
                act.activation(wv[:, b, :], ps_hw[:, :], ACT.Identity, bias=b2v[:, :]).then_inc(wv_ok, 1)

            def exponents(g, b):
                act.wait_ge(am_ok, g + 1)
                used(act, den_ok, g)
                act.activation(ex[:, b, :], ex[:, b, :], ACT.Exp).then_inc(ex_ok, 1)
                act.wait_ge(dmr_ok, g + 1)
                act.activation(dm[:, b, :], dm[:, b, :], ACT.Exp).then_inc(dec_ok, 1)

            def rows(g, b, h):
                if h == 0 and (not isinstance(g, int) or g >= 2):
                    arrived(act, row_out, g - 2, b)
                act.wait_ge(row_ps, g * 2 + (h + 1))
                act.activation(row[:, b, 2 * h:2 * h + 2, 0:O],
                               ps_r[:, 0:2 * O].rearrange("p (j o) -> p j o", j=2), ACT.Copy).then_inc(row_ok, 1)
                act.activation(row[:, b, 2 * h:2 * h + 2, O:RW],
                               ps_r[:, 2 * O:4 * O].rearrange("p (j h d) -> p j h d", j=2, h=H)[:, :, :, 0],
                               ACT.Copy).then_inc(row_ok, 1)

            def body(t, b, q):
                if live(t + 2):
                    front_x(t + 2, b)
                if live(t + 1):
                    front_h(t + 1, 1 - b)
                    front_q(t + 1, 1 - b)
                    outer_high(t + 1, 1 - b, 0)
                    outer_high(t + 1, 1 - b, 1)
                    weights_v(t + 1, 1 - b)
                    outer_high(t + 1, 1 - b, 2)
                if live(t - 2):
                    rows(t - 2, b, 0)
                if live(t + 1):
                    outer_high(t + 1, 1 - b, 3)
                    outer_high(t + 1, 1 - b, 4)
                if live(t - 2):
                    rows(t - 2, b, 1)
                if live(t - 1):
                    exponents(t - 1, 1 - b)
            steps(act, body)

            for n, (lo, w) in enumerate(NODE_BLOCKS):
                act.wait_ge(upd_ps, n + 1)
                act.activation(xa_t[:, lo:lo + w], bank[n][:, 0:w], ACT.Copy).then_inc(upd_ok, 1)
            act.wait_ge(bn, 5)
            act.activation(bnc[:, 3:4], bnc[:, 2:3], ACT.Sqrt, scale=1.0 / N, bias=epst[0:D, :]).then_inc(bn_sqrt, 1)
            act.wait_ge(ln, LN_STEPS + 5)
            act.activation(rstd[:, :], var[:, :], ACT.Sqrt, scale=1.0 / D, bias=epst[:, :]).then_inc(ln_sqrt, 1)

        @block.tensor
        def _(pe):
            pe.wait_ge(loaded, ALL_WEIGHTS)
            pe.wait_ge(zeroed, 1)
            pe.wait_ge(bad_step, 2)
            pe.matmul(bank[6][0:1, 0:1], bad_col[:, :], ones[:, 0:1], start=True, stop=True).then_inc(bad_ps, 1)
            pe.wait_ge(bad_ok, 1)
            unsorted = pe.value_load(bad[0:1, 0:1], min_val=0, max_val=1)
            with pe.If(unsorted == 1):
                with pe.Fori(0, NK) as k:
                    pe.wait_ge(so1, k * 3 + 2)
                    pe.matmul(bank[0][0:NT, 0:P], so_hi, so_lo, start=True, stop=True).then_inc(so1_ps, 1)
                pe.wait_ge(so_off, 2)
                pe.matmul(bank[0][0:NT, 0:1], upper[0:NT, 0:NT], so_cum[:, P - 1:P], start=True, stop=True
                          ).then_inc(so_off_ps, 1)
                pe.wait_ge(so_off, 5)
                with pe.Fori(0, NK) as k:
                    pe.wait_ge(so2, k * SORT2 + 4)
                    pe.transpose(bank[0][0:NT, 0:P], so_hi, ident[:, :])
                    pe.transpose(bank[1][:, 0:P], so_bc, ident[:, :]).then_inc(so2_turned, 1)
                    pe.wait_ge(so2, k * SORT2 + 5)
                    pe.matmul(bank[2][:, 0:P], so_hit, so_cum, start=True, stop=True)
                    pe.matmul(bank[3][0:NT, 0:P], so_hi, so_lo, start=True, stop=True).then_inc(so2_ps, 1)
                with pe.Fori(0, NK) as k:
                    pe.wait_ge(so3_in, k * 16 + 16)
                    pe.transpose(bank[0][0:D + S, 0:P], so_row[:, 0:D + S], ident[:, :]).then_inc(so3_ps, 1)

            def count_tiles(n, b, first=False, last=False):
                pe.wait_ge(onehot, n * 2 + 2)
                for k in range(OH):
                    mm = pe.matmul(bank[7][0:NT, 0:P], oh_hi[:, b, k, :], oh_lo[:, b, k, :],
                                   start=first and k == 0, stop=last and k == OH - 1)
                mm.then_inc(counted, 1)

            def chunk_rows(c, b):
                pe.wait_ge(chunk_run, c + 1)
                for h in range(2):
                    used(pe, chunk_row, c, 2)
                    for j in range(8):
                        tr = pe.transpose(bank[2 * b + h][:, j * D:(j + 1) * D],
                                          run_c[:, b, bass.ds(8 * h + j, P, WJ)], ident[0:D, 0:D])
                        if j == 0:
                            carry(tr, loaded, ALL_WEIGHTS)
                    tr.then_inc(chunk_ps, 1)

            def chunk(c, b, first=False, last=False):
                count_tiles(c * 2, 0, first=first)
                count_tiles(c * 2 + 1, 1, last=last)
                chunk_rows(c, b)
            chunk(0, 0, first=True)
            chunk(1, 1)
            with pe.Fori(0, (NC - 3) // 2) as i:
                for r in range(2):
                    chunk(i * 2 + (2 + r), r)
            chunk(NC - 1, 0, last=True)

            pe.wait_ge(hist_ok, 2)
            pe.matmul(bank[7][0:D, 448:449], w1u[:, :], u0[:, :], start=True, stop=True).then_inc(b1e_ps, 1)
            pe.matmul(bank[7][0:NT, 256:257], upper[0:NT, 0:NT], cum[:, P - 1:P], start=True, stop=True
                      ).then_inc(hist_ps, 1)
            pe.wait_ge(hist_ok, 4)
            pe.transpose(bank[7][:, 320:320 + NT], cum[:, :], ident[0:NT, 0:NT])
            pe.transpose(bank[7][:, 352:352 + NT], count[:, :], ident[0:NT, 0:NT]).then_inc(hist_ps, 1)

            pe.wait_ge(masked, 1)
            pe.wait_ge(chunk_row, 2 * NC)
            for n, (lo, w) in enumerate(NODE_BLOCKS):
                for t in range(lo // P, (lo + w) // P):
                    tr = pe.transpose(bank[n][:, t * P - lo:(t + 1) * P - lo], x_r[:, t, :], ident[:, :])
                tr.then_inc(xat_ps, 1)
            for n, (lo, w) in enumerate(NODE_BLOCKS):
                pe.wait_ge(xat_ok, n + 1)
                pe.matmul(bank[n][0:D, 0:w], w1[:, :], xa_t[:, lo:lo + w], start=True, stop=True).then_inc(h1_ps, 1)
            for n, (lo, w) in enumerate(NODE_BLOCKS):
                pe.wait_ge(h1_ok, n + 1)
                pe.matmul(bank[n][0:D, 0:w], w2[:, :], h_t[:, lo:lo + w], start=True, stop=True).then_inc(h2_ps, 1)
            pe.wait_ge(res_ok, len(NODE_BLOCKS))
            for b, tiles in ROW_TILES:
                for j, t in enumerate(tiles):
                    tr = pe.transpose(bank[b][:, j * D:(j + 1) * D], h_t[:, t * P:(t + 1) * P], ident[0:D, 0:D])
                tr.then_inc(rr_ps, 1)
            pe.wait_ge(x1_ok, 1)
            for n, (lo, w) in enumerate(NODE_BLOCKS):
                for t in range(lo // P, (lo + w) // P):
                    tr = pe.transpose(bank[n][0:D, t * P - lo:(t + 1) * P - lo], x1_r[:, t, :], ident[:, :])
                tr.then_inc(x1t_ps, 1)
            for n, (lo, w) in enumerate(NODE_BLOCKS):
                pe.wait_ge(x1t_ok, n + 1)
                for t in range(lo // P, (lo + w) // P):
                    mm = pe.matmul(bank[n][:, t * P - lo:(t + 1) * P - lo], x1_t[:, t * P:(t + 1) * P], wq[:, :],
                                   start=True, stop=True)
                mm.then_inc(q_ps, 1)
            pe.wait_ge(q_ok, len(NODE_BLOCKS))
            pe.wait_ge(sel_done, 1)
            pe.wait_ge(wtl_ok, 1)

            def x_turn(g, q):
                arrived(pe, xg_in, g, q, 64)
                used(pe, wkq_ok, g)
                if isinstance(g, int) and g == 1:
                    pe.wait_ge(xt_ok, 1)
                for k in range(4):
                    tr = pe.transpose(ps_xw[:, k * P:(k + 1) * P], xg[:, q, k, :], ident[:, :])
                tr.then_inc(xt_ps, 1)

            def hidden(g, b):
                arrived(pe, ea_in, g, b)
                if not isinstance(g, int) or g >= 1:
                    pe.wait_ge(wv_ok, g)
                pe.matmul(ps_hw[:, :], w1kv[:, :], ea[:, b, :], start=True, stop=True).then_inc(hid_ps, 1)

            def q_turn(g, q):
                arrived(pe, qg_in, g, q, 64)
                if not isinstance(g, int) or g >= 3:
                    pe.wait_ge(am_ok, g - 2)
                elif g >= 1:
                    pe.wait_ge(qt_ok, g)
                for k in range(4):
                    tr = pe.transpose(ps_qa[:, k * P:(k + 1) * P], qg[:, q, k, :], ident[:, :])
                tr.then_inc(qt_ps, 1)

            def split_matmul(ps, w, rows, high, low, start, stop):
                pe.matmul(ps[:, :], wt_h[rows, w, :], high, start=start, stop=False)
                pe.matmul(ps[:, :], wt_h[rows, w, :], low, start=False, stop=False)
                return pe.matmul(ps[:, :], wt_l[rows, w, :], high, start=False, stop=stop)

            LOWER, UPPER, ALL = slice(0, D), slice(D, P), slice(0, P)

            def weights(g, b):
                pe.wait_ge(hidl_ok, g + 1)
                if not isinstance(g, int) or g + 1 < NG:
                    pe.wait_ge(xt_ok, g + 2)
                else:
                    pe.wait_ge(xt_ok, NG)
                split_matmul(ps_xw, W2KV, LOWER, hid_h[LOWER, b, :], hid_l[LOWER, b, :], True, True).then_inc(wk_ps, 1)
                split_matmul(ps_hw, W2KV, UPPER, hid_h[UPPER, b, :], hid_l[UPPER, b, :], True, True).then_inc(wv_ps, 1)

            def spread(g, b, j):
                if j == 0:
                    arrived(pe, s3_in, g, b)
                if not isinstance(g, int) or g * NJ + j >= 2:
                    pe.wait_ge(z_ok, g * NJ + (j - 1))
                pe.matmul(bank[2 + (NJ * b + j) % 2][:, :], sel[:, j, :], s3[:, b, :], start=True, stop=True
                          ).then_inc(shb_ps, 1)

            def products(g, b, j):
                pe.wait_ge(zl_ok, g * NJ + (j + 1))
                if j == 0 and (not isinstance(g, int) or g >= 1):
                    pe.wait_ge(kq_ok, g)
                    pe.wait_ge(val_ok, g)
                if j < 4:
                    split_matmul(ps_k, CK + j, ALL, z_h[:, b, j, :], z_l[:, b, j, :], j == 0, False)
                    split_matmul(ps_v, CV + j, ALL, z_h[:, b, j, :], z_l[:, b, j, :], j == 0, False)
                else:
                    split_matmul(ps_k, C8, LOWER, z_h[LOWER, b, j, :], z_l[LOWER, b, j, :], False, True)
                    split_matmul(ps_v, C8, UPPER, z_h[UPPER, b, j, :], z_l[UPPER, b, j, :], False, True
                                 ).then_inc(acc_ps, 1)

            def scores(g, b):
                pe.wait_ge(kq_ok, g + 1)
                pe.wait_ge(qt_ok, g + 3 if not isinstance(g, int) or g + 3 <= NG else NG)
                pe.matmul(ps_qa[:, :], headones[:, :], kq[:, b, :], start=True, stop=True).then_inc(att_ps, 1)

            def row_turn(g, b, h):
                pe.wait_ge(num_ok, g + 1)
                pe.wait_ge(den_ok, g + 1)
                if h == 1 or not isinstance(g, int) or g >= 1:
                    pe.wait_ge(row_ok, g * 4 + 2 * h)
                for i in range(2):
                    j = 2 * h + i
                    pe.transpose(ps_r[:, i * O:(i + 1) * O], num[:, b, bass.ds(j, P, 4)], ident[:, :])
                    mm = pe.transpose(ps_r[:, (2 + i) * O:(3 + i) * O], den[:, b, bass.ds(j, P, 4)], ident[:, :])
                mm.then_inc(row_ps, 1)

            def body(t, b, q):
                if live(t + 2):
                    x_turn(t + 2, (q + 2) % 4)
                if live(t + 1):
                    hidden(t + 1, 1 - b)
                    q_turn(t + 1, (q + 1) % 4)
                    spread(t + 1, 1 - b, 0)
                    spread(t + 1, 1 - b, 1)
                for j in range(NJ):
                    if live(t):
                        products(t, b, j)
                    if j + 2 < NJ and live(t + 1):
                        spread(t + 1, 1 - b, j + 2)
                    if j == 0 and live(t + 1):
                        weights(t + 1, 1 - b)
                    if j == 1 and live(t - 1):
                        scores(t - 1, 1 - b)
                    if j == 2 and live(t - 2):
                        row_turn(t - 2, b, 0)
                    if j == 4 and live(t - 2):
                        row_turn(t - 2, b, 1)
            steps(pe, body)

            pe.wait_ge(upd_step, 4)
            pe.wait_ge(row_ok, 4 * NG)
            pe.wait_ge(am_ok, NG)
            pe.wait_ge(val_ok, NG)
            for n, (lo, w) in enumerate(NODE_BLOCKS):
                for t in range(lo // P, (lo + w) // P):
                    tr = pe.transpose(bank[n][:, t * P - lo:(t + 1) * P - lo], end_rows[:, t, 0:O], ident[:, :])
                tr.then_inc(upd_ps, 1)
            for n, (lo, w) in enumerate(NODE_BLOCKS):
                pe.wait_ge(upd_ok, n + 1)
                pe.matmul(bank[n][0:D, 0:w], wself[:, :], x1_t[:, lo:lo + w], start=True, stop=False)
                pe.matmul(bank[n][0:D, 0:w], wout[:, :], xa_t[:, lo:lo + w], start=False, stop=True).then_inc(o_ps, 1)
            pe.wait_ge(bn, 8)
            for b, tiles in ROW_TILES:
                for j, t in enumerate(tiles):
                    tr = pe.transpose(bank[b][:, j * D:(j + 1) * D], h_t[:, t * P:(t + 1) * P], ident[0:D, 0:D])
                tr.then_inc(y_ps, 1)

        @block.vector
        def _(dve):
            def halves(step):
                dve.tensor_scalar(lo_i[:, :], dst_t[:, :], P - 1, None, ALU.bitwise_and).then_inc(step, 1)
                dve.tensor_scalar(hi_i[:, :], dst_t[:, :], 7, None, ALU.logical_shift_right).then_inc(step, 1)
                dve.wait_ge(step, 2)
                dve.tensor_copy(lo_f[:, :], lo_i[:, :]).then_inc(step, 1)
                dve.tensor_copy(hi_f[:, :], hi_i[:, :]).then_inc(step, 1)
            dve.wait_ge(tabs_in, 32)
            halves(hilo)

            dve.wait_ge(dlin_in, 32)
            falls = x1_r[:, :, :].rearrange("p t d -> p (t d)")[:, 0:NK]
            dve.tensor_tensor(falls, d_this[:, :], d_prev[:, :], ALU.is_lt).then_inc(bad_step, 1)
            dve.wait_ge(bad_step, 1)
            dve.tensor_reduce(bad_col[:, :], falls, AX_X, ALU.add).then_inc(bad_step, 1)
            dve.wait_ge(bad_ps, 1)
            dve.tensor_scalar(bad[:, :], bank[6][0:1, 0:1], 1.0, None, ALU.min).then_inc(bad_ok, 1)
            dve.wait_ge(bad_ok, 1)
            dve.wait_ge(hilo, 4)
            dve.wait_ge(loaded, ALL_WEIGHTS)
            unsorted = dve.value_load(bad[0:1, 0:1], min_val=0, max_val=1)
            with dve.If(unsorted == 1):
                dve.memset(so_count, 0.0).then_inc(so_off, 1)
                dve.wait_ge(so_off, 1)
                with dve.Fori(0, NK) as k:
                    dve.tensor_scalar(so_lo, iota_row[:, :], lo_f[:, bass.ds(k, 1)], None, ALU.is_equal
                                      ).then_inc(so1, 1)
                    dve.tensor_scalar(so_hi, iota_row[:, 0:NT], hi_f[:, bass.ds(k, 1)], None, ALU.is_equal
                                      ).then_inc(so1, 1)
                    dve.wait_ge(so1_ps, k + 1)
                    dve.tensor_tensor(so_count, so_count, bank[0][0:NT, 0:P], ALU.add).then_inc(so1, 1)
                    dve.wait_ge(so1, k * 3 + 3)
                dve.tensor_tensor_scan(so_cum, ones[0:NT, :], so_count, 0.0, ALU.mult, ALU.add).then_inc(so_off, 1)
                dve.wait_ge(so_off_ps, 1)
                dve.tensor_copy(so_before, bank[0][0:NT, 0:1]).then_inc(so_off, 1)
                dve.wait_ge(so_off, 3)
                dve.tensor_tensor(so_cum, so_cum, so_count, ALU.subtract).then_inc(so_off, 1)
                dve.wait_ge(so_off, 4)
                dve.tensor_scalar(so_cum, so_cum, so_before, None, ALU.add).then_inc(so_off, 1)
                dve.wait_ge(so_off, 5)
                with dve.Fori(0, NK) as k:
                    dve.tensor_scalar(so_lo, iota_row[:, :], lo_f[:, bass.ds(k, 1)], None, ALU.is_equal
                                      ).then_inc(so2, 1)
                    dve.tensor_scalar(so_hi, iota_row[:, 0:NT], hi_f[:, bass.ds(k, 1)], None, ALU.is_equal
                                      ).then_inc(so2, 1)
                    dve.tensor_copy(so_dst, dst_t[:, bass.ds(k, 1)]).then_inc(so2, 1)
                    dve.wait_ge(so2, k * SORT2 + 3)
                    dve.tensor_scalar(so_bc, ones[:, :], so_dst, None, ALU.mult).then_inc(so2, 1)
                    dve.wait_ge(so2_turned, k + 1)
                    dve.tensor_copy(so_hit, bank[0][0:NT, 0:P]).then_inc(so2, 1)
                    dve.scalar_tensor_tensor(out=so_bc, in0=bank[1][:, 0:P], scalar=so_dst, in1=lower[:, :],
                                             op0=ALU.is_equal, op1=ALU.mult).then_inc(so2, 1)
                    dve.wait_ge(so2, k * SORT2 + 6)
                    dve.tensor_reduce(so_rank, so_bc, AX_X, ALU.add).then_inc(so2, 1)
                    dve.wait_ge(so2_ps, k + 1)
                    dve.tensor_tensor(so_prod, bank[2][:, 0:P], so_lo, ALU.mult).then_inc(so2, 1)
                    dve.wait_ge(so2, k * SORT2 + 8)
                    dve.tensor_reduce(so_base, so_prod, AX_X, ALU.add).then_inc(so2, 1)
                    dve.wait_ge(so2, k * SORT2 + 9)
                    dve.tensor_tensor(so_posf, so_base, so_rank, ALU.add).then_inc(so2, 1)
                    dve.wait_ge(so2, k * SORT2 + 10)
                    dve.tensor_copy(so_pos[:, :], so_posf).then_inc(so2, 1)
                    dve.tensor_tensor(so_cum, so_cum, bank[3][0:NT, 0:P], ALU.add).then_inc(so2, 1)
                    dve.wait_ge(so2, k * SORT2 + SORT2)
                    dve.wait_ge(so_placed, k * 16 + 16)
                with dve.Fori(0, NK) as k:
                    dve.wait_ge(so3_ps, k + 1)
                    dve.tensor_copy(so_turn, bank[0][0:D + S, 0:P]).then_inc(so3, 1)
                    dve.tensor_copy(src_t[:, bass.ds(k, 1)], so_row[:, RS_SRC:RS_SRC + 1].bitcast(I32)
                                    ).then_inc(so3, 1)
                    dve.tensor_copy(dst_t[:, bass.ds(k, 1)], so_row[:, RS_DST:RS_DST + 1].bitcast(I32)
                                    ).then_inc(so3, 1)
                    dve.wait_ge(so3_out, k * 48 + 48)
                dve.wait_ge(so3, 3 * NK)
                halves(hilo2)
                dve.wait_ge(hilo2, 4)
                dve.wait_ge(resorted, 32)

            dve.tensor_tensor(keep[:, :], d_prev[:, :], d_this[:, :], ALU.is_equal).then_inc(flags_done, 1)
            dve.wait_ge(flags_done, 1)
            dve.tensor_scalar(reset[:, :], keep[:, :], -1.0, FAR, ALU.add, ALU.mult).then_inc(flags_done, 1)
            dve.wait_ge(wth_ok, 1)
            dve.tensor_tensor(wt_l[:, :, :], wt[:, :, :], wt_h[:, :, :].bitcast(F32), ALU.subtract).then_inc(wtl_ok, 1)
            for part in range(2):
                dve.wait_ge(split_done, part + 1)
                dve.tensor_tensor(shf[:, :], shf[:, :], shp[:, :], ALU.subtract).then_inc(split_step, 1)

            dve.wait_ge(zeroed, 3)

            def run(c, b):
                arrived(dve, chunk_in, c, b, 32)
                if not isinstance(c, int) or c >= 1:
                    dve.wait_ge(chunk_run, c)
                if not isinstance(c, int) or c >= 2:
                    dve.wait_ge(chunk_ps, c * 2 - 2)
                dve.tensor_tensor_scan(run_c[:, b, :], keep_c[:, b, :], ea_c[:, b, :], run_c[:, 1 - b, W - 1:W],
                                       ALU.mult, ALU.add).then_inc(chunk_run, 1)

            def one_hots(n, b):
                if not isinstance(n, int) or n >= 2:
                    dve.wait_ge(counted, n - 1)
                for f, oh, width in ((lo_f, oh_lo, P), (hi_f, oh_hi, NT)):
                    dve.tensor_tensor(oh[:, b, :, :],
                                      f[:, bass.ds(n * OH, OH)].rearrange("p (k o) -> p k o", o=1)
                                      .to_broadcast([P, OH, width]),
                                      iota_row[:, 0:width].rearrange("p (o w) -> p o w", o=1)
                                      .to_broadcast([P, OH, width]),
                                      ALU.is_equal).then_inc(onehot, 1)

            def chunk(c, b):
                run(c, b)
                one_hots(c * 2, 0)
                one_hots(c * 2 + 1, 1)
            chunk(0, 0)
            chunk(1, 1)
            with dve.Fori(0, (NC - 3) // 2) as i:
                for r in range(2):
                    chunk(i * 2 + (2 + r), r)
            chunk(NC - 1, 0)

            dve.wait_ge(counted, NOH)
            dve.tensor_copy(count[:, :], bank[7][0:NT, 0:P]).then_inc(hist_ok, 1)
            dve.wait_ge(hist_ok, 1)
            dve.tensor_tensor_scan(cum[:, :], ones[0:NT, :], count[:, :], 0.0, ALU.mult, ALU.add).then_inc(hist_ok, 1)
            dve.wait_ge(hist_ps, 1)
            dve.tensor_copy(before[:, :], bank[7][0:NT, 256:257]).then_inc(hist_ok, 1)
            dve.wait_ge(hist_ok, 3)
            dve.tensor_scalar(cum[:, :], cum[:, :], before[:, :], None, ALU.add).then_inc(hist_ok, 1)
            dve.wait_ge(hist_ps, 2)
            dve.tensor_scalar(end_f[:, :], bank[7][:, 320:320 + NT], -1.0, 0.0, ALU.add, ALU.max).then_inc(hist_ok, 1)
            dve.tensor_scalar(has[:, :], bank[7][:, 352:352 + NT], 0.0, None, ALU.is_gt).then_inc(ends_ok, 1)
            dve.wait_ge(hist_ok, 5)
            dve.tensor_copy(end_i[:, :], end_f[:, :]).then_inc(ends_ok, 1)
            dve.wait_ge(b1e_ps, 1)
            dve.tensor_tensor(b1e[:, :], bank[7][0:D, 448:449], b1[:, :], ALU.add).then_inc(b1e_ok, 1)

            dve.wait_ge(agg_in, 16 * NT)
            dve.wait_ge(x_in, 16)
            dve.wait_ge(ends_ok, 2)
            dve.tensor_tensor(x_r[:, :, D:2 * D], x_r[:, :, D:2 * D],
                              has[:, :].rearrange("p (t o) -> p t o", o=1).to_broadcast([P, NT, D]), ALU.mult
                              ).then_inc(masked, 1)
            dve.wait_ge(b1e_ok, 1)
            for n, (lo, w) in enumerate(NODE_BLOCKS):
                dve.wait_ge(h1_sig, n + 1)
                dve.scalar_tensor_tensor(out=h_t[:, lo:lo + w], in0=bank[n][0:D, 0:w], scalar=b1e[:, :],
                                         in1=sg_t[:, lo:lo + w], op0=ALU.add, op1=ALU.mult).then_inc(h1_ok, 1)
            for n, (lo, w) in enumerate(NODE_BLOCKS):
                dve.wait_ge(h2_sig, n + 1)
                dve.scalar_tensor_tensor(out=h_t[:, lo:lo + w], in0=bank[n][0:D, 0:w], scalar=b2[:, :],
                                         in1=sg_t[:, lo:lo + w], op0=ALU.add, op1=ALU.mult).then_inc(h2_ok, 1)
            for n, (lo, w) in enumerate(NODE_BLOCKS):
                dve.wait_ge(h2_ok, n + 1)
                dve.tensor_tensor(h_t[:, lo:lo + w], h_t[:, lo:lo + w], xa_t[0:D, lo:lo + w], ALU.add
                                  ).then_inc(res_ok, 1)
            for b, tiles in ROW_TILES:
                dve.wait_ge(rr_ps, b + 1)
                dve.tensor_copy(r_r[:, tiles[0]:tiles[-1] + 1, :].rearrange("p t d -> p (t d)"),
                                bank[b][:, 0:len(tiles) * D]).then_inc(rr_ok, 1)

            def spread_cols(v):
                return v[:, :].rearrange("p (t o) -> p t o", o=1).to_broadcast([P, NT, D])

            def layer_norm(dst, ok, base):
                dve.tensor_reduce(mean[:, :], r_r[:, :, :], AX_X, ALU.add).then_inc(ln, 1)
                dve.wait_ge(ln, base + 1)
                dve.tensor_scalar(mean[:, :], mean[:, :], 1.0 / D, None, ALU.mult).then_inc(ln, 1)
                dve.wait_ge(ln, base + 2)
                dve.tensor_tensor(r_r[:, :, :], r_r[:, :, :], spread_cols(mean), ALU.subtract).then_inc(ln, 1)
                dve.wait_ge(ln, base + 3)
                dve.tensor_tensor(sq_r, r_r[:, :, :], r_r[:, :, :], ALU.mult).then_inc(ln, 1)
                dve.wait_ge(ln, base + 4)
                dve.tensor_reduce(var[:, :], sq_r, AX_X, ALU.add).then_inc(ln, 1)
                dve.wait_ge(ln_sqrt, base // LN_STEPS + 1)
                dve.reciprocal(rstd[:, :], rstd[:, :]).then_inc(ln, 1)
                dve.wait_ge(ln, base + LN_STEPS)
                dve.tensor_tensor(dst, r_r[:, :, :], spread_cols(rstd), ALU.mult).then_inc(ok, 1)
            dve.wait_ge(rr_ok, len(ROW_TILES))
            layer_norm(x1_r[:, :, :], x1_ok, 0)

            dve.wait_ge(zeroed, 6)

            def outer(g, b, j):
                dve.wait_ge(shb_ps, g * NJ + (j + 1))
                if j == 0:
                    dve.wait_ge(xt_ok, g + 1)
                    used(dve, acc_ps, g)
                dve.tensor_tensor(z[:, j, :], bank[2 + (NJ * b + j) % 2][:, :], xt[:, b, :], ALU.mult
                                  ).then_inc(z_ok, 1)

            def outer_low(g, b, j):
                dve.wait_ge(zh_ok, g * NJ + (j + 1))
                dve.tensor_tensor(z_l[:, b, j, :], z[:, j, :], z_h[:, b, j, :].bitcast(F32), ALU.subtract
                                  ).then_inc(zl_ok, 1)

            def hidden_low(g, b):
                dve.wait_ge(hid_ok, g * 2 + 2)
                used(dve, wv_ps, g)
                dve.tensor_tensor(hid_l[:, b, :], hid[:, :], hid_h[:, b, :].bitcast(F32), ALU.subtract
                                  ).then_inc(hidl_ok, 1)

            def key_query(g, b):
                dve.wait_ge(wk_ps, g + 1)
                dve.wait_ge(qt_ok, g + 1)
                used(dve, kq_ok, g)
                dve.scalar_tensor_tensor(out=qt[:, b, :], in0=ps_xw[:, :], scalar=b2k[:, :], in1=qt[:, b, :],
                                         op0=ALU.add, op1=ALU.mult).then_inc(wkq_ok, 1)

            def weigh(g, b):
                dve.wait_ge(acc_ps, g + 1)
                dve.wait_ge(wkq_ok, g + 1)
                used(dve, att_ps, g)
                dve.tensor_tensor(kq[:, b, :], ps_k[:, :], qt[:, b, :], ALU.mult).then_inc(kq_ok, 1)
                dve.wait_ge(wv_ok, g + 1)
                dve.tensor_tensor(val[:, b, :], ps_v[:, :], wv[:, b, :], ALU.mult).then_inc(val_ok, 1)

            def maxima(g, b):
                dve.wait_ge(att_ps, g + 1)
                arrived(dve, rs_in, g, b)
                if not isinstance(g, int) or g >= 1:
                    dve.wait_ge(mx_ok, g)
                    dve.wait_ge(dm_ok, g * 2)
                dve.tensor_tensor_scan(mx[:, b, :], rs[:, b, :], ps_qa[:, :], mx[:, 1 - b, G - 1:G],
                                       ALU.add, ALU.max).then_inc(mx_ok, 1)

            def below(g, b):
                dve.wait_ge(mx_ok, g + 1)
                used(dve, ex_ok, g)
                dve.tensor_tensor(ex[:, b, :], ps_qa[:, :], mx[:, b, :], ALU.subtract).then_inc(am_ok, 1)

            def weigh_values(g, b):
                dve.wait_ge(ex_ok, g + 1)
                dve.wait_ge(val_ok, g + 1)
                dve.tensor_tensor(val[:, b, :], val[:, b, :], ex[:, b, :], ALU.mult).then_inc(ev_ok, 1)

            def sum_values(g, b):
                dve.wait_ge(ev_ok, g + 1)
                dve.wait_ge(dec_ok, g + 1)
                if not isinstance(g, int) or g >= 1:
                    dve.wait_ge(num_ok, g)
                used(dve, row_ps, g, 2)
                dve.tensor_tensor_scan(num[:, b, :], dm[:, b, :], val[:, b, :], num[:, 1 - b, G - 1:G],
                                       ALU.mult, ALU.add).then_inc(num_ok, 1)

            def sum_exponents(g, b):
                if not isinstance(g, int) or g >= 1:
                    dve.wait_ge(den_ok, g)
                dve.tensor_tensor_scan(den[:, b, :], dm[:, b, :], ex[:, b, :], den[:, 1 - b, G - 1:G],
                                       ALU.mult, ALU.add).then_inc(den_ok, 1)

            def body(t, b, q):
                if live(t - 1):
                    weigh(t - 1, 1 - b)
                if live(t + 1):
                    outer(t + 1, 1 - b, 0)
                if live(t - 2):
                    weigh_values(t - 2, b)
                if live(t + 1):
                    hidden_low(t + 1, 1 - b)
                    outer(t + 1, 1 - b, 1)
                    outer_low(t + 1, 1 - b, 0)
                if live(t - 2):
                    sum_values(t - 2, b)
                if live(t + 1):
                    outer_low(t + 1, 1 - b, 1)
                    outer(t + 1, 1 - b, 2)
                    key_query(t + 1, 1 - b)
                if live(t - 2):
                    sum_exponents(t - 2, b)
                if live(t + 1):
                    outer_low(t + 1, 1 - b, 2)
                    outer(t + 1, 1 - b, 3)
                if live(t - 1):
                    maxima(t - 1, 1 - b)
                if live(t + 1):
                    outer_low(t + 1, 1 - b, 3)
                    outer(t + 1, 1 - b, 4)
                if live(t - 1):
                    below(t - 1, 1 - b)
                if live(t + 1):
                    outer_low(t + 1, 1 - b, 4)
            steps(dve, body)

            dve.wait_ge(nrow_in, 16 * NT)
            dve.tensor_tensor(end_rows[:, :, :], end_rows[:, :, :],
                              has[:, :].rearrange("p (t o) -> p t o", o=1).to_broadcast([P, NT, RW]), ALU.mult
                              ).then_inc(upd_step, 1)
            dve.wait_ge(upd_step, 1)
            dve.tensor_scalar(rden[:, :, :], end_rows[:, :, O:RW], 1e-16, None, ALU.add).then_inc(upd_step, 1)
            dve.wait_ge(upd_step, 2)
            dve.reciprocal(rden[:, :, :], rden[:, :, :]).then_inc(upd_step, 1)
            dve.wait_ge(upd_step, 3)
            heads = end_rows[:, :, 0:O].rearrange("p t (h d) -> p t h d", h=H)
            dve.tensor_tensor(heads, heads, rden[:, :, :].rearrange("p t (h o) -> p t h o", o=1)
                              .to_broadcast([P, NT, H, DH]), ALU.mult).then_inc(upd_step, 1)
            for n, (lo, w) in enumerate(NODE_BLOCKS):
                dve.wait_ge(o_ps, n + 1)
                dve.tensor_copy(h_t[:, lo:lo + w], bank[n][0:D, 0:w]).then_inc(o_ok, 1)
            dve.wait_ge(o_ok, len(NODE_BLOCKS))
            dve.tensor_reduce(bnc[:, 0:1], h_t[:, 0:N], AX_X, ALU.add).then_inc(bn, 1)
            dve.wait_ge(bn, 1)
            dve.tensor_scalar(bnc[:, 1:2], bnc[:, 0:1], 1.0 / N, None, ALU.mult).then_inc(bn, 1)
            dve.wait_ge(bn, 2)
            dve.tensor_scalar(h_t[:, :], h_t[:, :], bnc[:, 1:2], None, ALU.subtract).then_inc(bn, 1)
            dve.wait_ge(bn, 3)
            dve.tensor_tensor(sg_t[:, :], h_t[:, :], h_t[:, :], ALU.mult).then_inc(bn, 1)
            dve.wait_ge(bn, 4)
            dve.tensor_reduce(bnc[:, 2:3], sg_t[:, 0:N], AX_X, ALU.add).then_inc(bn, 1)
            dve.wait_ge(bn_sqrt, 1)
            dve.reciprocal(bnc[:, 4:5], bnc[:, 3:4]).then_inc(bn, 1)
            dve.wait_ge(bn, 6)
            dve.tensor_tensor(bnc[:, 5:6], bnc[:, 4:5], gamma[:, :], ALU.mult).then_inc(bn, 1)
            dve.wait_ge(bn, 7)
            dve.tensor_scalar(h_t[:, :], h_t[:, :], bnc[:, 5:6], beta[:, :], ALU.mult, ALU.add).then_inc(bn, 1)
            for b, tiles in ROW_TILES:
                dve.wait_ge(y_ps, b + 1)
                dve.tensor_tensor(r_r[:, tiles[0]:tiles[-1] + 1, :],
                                  bank[b][:, 0:len(tiles) * D].rearrange("p (t d) -> p t d", d=D),
                                  x1_r[:, tiles[0]:tiles[-1] + 1, :], ALU.add).then_inc(rr_ok, 1)
            dve.wait_ge(rr_ok, 2 * len(ROW_TILES))
            layer_norm(r_r[:, :, :], out_ok, LN_STEPS)


def kernel(**inputs):
    import numpy as _np
    import concourse.bacc as _bacc
    from concourse import mybir as _mybir
    from concourse.bass_utils import run_bass_kernel_spmd as _run

    v = {k: _np.asarray(x) for k, x in inputs.items()}
    l1 = lambda name: v["L1_gnn_" + name]
    pad = EP - E
    src = _np.pad(v["src"], (0, pad))
    dst = _np.pad(v["dst"], (0, pad), constant_values=N)
    ea = _np.pad(v["edge_attr_64"], ((0, pad), (0, 0)))
    sh = _np.pad(v["edge_attr_9"], ((0, pad), (0, 0)))
    k, m = _np.arange(P)[:, None], _np.arange(P)[None, :]
    s27 = _np.arange(SP3)[:, None] % S
    col = _np.arange(NJ * P)[None, :]
    arrays = {
        "x": _np.pad(v["x"], ((0, NP - N), (0, 0))),
        "src_t": src.reshape(NK, P).T, "dst_t": dst.reshape(NK, P).T,
        "dst_lin": _np.pad(dst, (1, 0), constant_values=-1),
        "ea_rows": ea, "sh_rows": sh, "src_col": src[:, None], "dst_col": dst[:, None],
        "ea_t": ea.T, "sh_t": sh.T,
        "c_k": l1("Cqk").transpose(1, 0, 2).reshape(S * D, O), "c_v": l1("Cv").transpose(1, 0, 2).reshape(S * D, O),
        "k_w1": l1("k_w1"), "v_w1": l1("v_w1"), "k_w2": l1("k_w2"), "v_w2": l1("v_w2"),
        "k_b1": l1("k_b1")[:, None], "v_b1": l1("v_b1")[:, None],
        "k_b2": l1("k_b2")[:, None], "v_b2": l1("v_b2")[:, None],
        "w1": v["L0_gnn_W1"], "b1": v["L0_gnn_b1"][:, None], "u0": v["L0_gnn_u"][0][:, None],
        "w2": v["L0_gnn_W2"], "b2": v["L0_gnn_b2"][:, None],
        "wq": l1("Wq"), "wout": l1("W_out"), "wself": l1("W_self"),
        "gamma": l1("gamma")[:, None], "beta": l1("beta")[:, None],
        "ident": (k == m).astype(_np.float32),
        "headones": (k // DH == m // DH).astype(_np.float32),
        "iota_row": (m + 0 * k).astype(_np.float32),
        "upper": (k < m).astype(_np.float32), "lower": (m < k).astype(_np.float32),
        "sel": (s27 == _np.minimum(2 * (col // P) + col % P // D, S - 1)).astype(_np.float32),
    }
    nc = _bacc.Bacc("TRN2", target_bir_lowering=False, num_devices=1)
    feed, aps = {}, {}
    for name, x in arrays.items():
        x = _np.ascontiguousarray(x)
        feed[f"in_{name}"] = x
        aps[name] = nc.dram_tensor(f"in_{name}", x.shape, _mybir.dt.from_np(x.dtype), kind="ExternalInput").ap()
    out = nc.dram_tensor("out_x", (NP, D), _mybir.dt.float32, kind="ExternalOutput").ap()
    gnn_two_layers(nc, aps, out)
    r = _run(nc, [feed], core_ids=[0])
    return r.results[0]["out_x"][0:N]
```

```python
from contextlib import ExitStack

import concourse.bass as bass
from concourse import mybir

ALU = mybir.AluOpType
ACT = mybir.ActivationFunctionType
AX_X = mybir.AxisListType.X
F32 = mybir.dt.float32
BF16 = mybir.dt.bfloat16
F32R = mybir.dt.float32r
I32 = mybir.dt.int32
U8 = mybir.dt.uint8

P = 128
N = 3125
D = 64
NT = (N + P) // P
NP = NT * P
E = 100000
G = 512
NG = -(-E // G)
EP = NG * G
NK = EP // P
S = 9
SP3 = 3 * S
NJ = 5
CK, CV, W2KV = 0, NJ, 2 * NJ
NW = 2 * NJ + 1
H = 8
DH = 16
O = H * DH
RW = O + H
W = 2048
NC = EP // W
CR = 2
CL = (NC - 2) // CR
WJ = W // P
NODE_BLOCKS = [(b, min(G, NP - b)) for b in range(0, NP, G)]
RP = 7
RL = NK // RP
LN_STEPS = 6
RS_SRC, RS_DST = D + S, D + S + 1
RSW = D + S + 2
SORT2 = 12
FAR = 3.0e38
EPS = 1e-5


def gnn_two_layers(nc, a, out):
    ctx = ExitStack()
    with ctx:
        def sb(name, shape, dt=F32):
            return ctx.enter_context(nc.sbuf_tensor(name, shape, dt))

        def sem(name):
            return ctx.enter_context(nc.semaphore(name))

        def dram(name, shape, dt=F32):
            return nc.dram_tensor(name, shape, dt, kind="Internal").ap()

        keep_d = dram("keep_d", [EP], U8)
        reset_d = dram("reset_d", [EP], BF16)
        sh3_d = dram("sh3_d", [3, S, EP], BF16)
        aggrow_d = dram("aggrow_d", [EP, D])
        xtab_d = dram("xtab_d", [NP, 2 * D])
        qtab_d = dram("qtab_d", [NP, O])
        nrow_d = dram("nrow_d", [EP, RW])

        rows_s = dram("rows_s", [EP, RSW])
        ea_s = dram("ea_s", [D, EP])
        sh_s = dram("sh_s", [S, EP])
        dst_s = dram("dst_s", [EP + 1], I32)
        dst_d = dram("dst_d", [EP], I32)

        ident = sb("ident", [P, P])
        headones = sb("headones", [P, O])
        iota_row = sb("iota_row", [P, P])
        upper = sb("upper", [P, P])
        lower = sb("lower", [P, P])
        ones = sb("ones", [P, P])
        sel_f = sb("sel_f", [SP3, NJ * P])
        sel = sb("sel", [SP3, NJ, P], BF16)
        wt_h = sb("wt_h", [P, NW, O], F32R)
        wt_l = sb("wt_l", [P, NW, O], F32R)
        w1kv = sb("w1kv", [D, P])
        b1kv = sb("b1kv", [P, 1])
        b2k = sb("b2k", [P, 1])
        b2v = sb("b2v", [P, 1])
        w1 = sb("w1", [P, D])
        w1u = sb("w1u", [D, D])
        b1 = sb("b1", [D, 1])
        u0 = sb("u0", [D, 1])
        w2 = sb("w2", [D, D])
        b2 = sb("b2", [D, 1])
        wq = sb("wq", [D, O])
        wout = sb("wout", [P, D])
        wself = sb("wself", [D, D])
        gamma = sb("gamma", [D, 1])
        beta = sb("beta", [D, 1])

        src_t = sb("src_t", [P, NK], I32)
        dst_t = sb("dst_t", [P, NK], I32)
        node_i = sb("node_i", [P, NT], I32)
        has = sb("has", [P, NT])
        end_i = sb("end_i", [P, NT], I32)

        x_r = sb("x_r", [P, NT, 2 * D])
        xa_t = sb("xa_t", [P, NP])
        h_t = sb("h_t", [D, NP])
        r_r = sb("r_r", [P, NT, D])
        x1_r = sb("x1_r", [P, NT, D])
        x1_t = sb("x1_t", [D, NP])
        flags = [v[:, :, :].rearrange("p t d -> p (t d)").bitcast(BF16) for v in (r_r, x1_r)]
        q_r = x_r[:, :, :]
        sq_r = x_r[:, :, 0:D]
        sg_t = x_r[0:D, :, :].rearrange("p t d -> p (t d)")
        free = x_r[:, :, :].rearrange("p t o -> p (t o)")
        so_lo, so_bc, so_prod = (free[:, i * P:(i + 1) * P] for i in range(3))
        so_hi = free[:, 3 * P:3 * P + NT]
        so_hit, so_count, so_cum = (free[0:NT, (4 + i) * P:(5 + i) * P] for i in range(3))
        so_row, so_turn = free[:, 7 * P:7 * P + RSW], free[0:D + S, 8 * P:9 * P]
        so_before = free[0:NT, 9 * P:9 * P + 1]
        so_dst, so_rank, so_base, so_posf = (free[:, 9 * P + 1 + i:9 * P + 2 + i] for i in range(4))
        so_pos = sb("so_pos", [P, 1], I32)
        bad_col = sb("bad_col", [P, 1])
        bad = sb("bad", [1, 1], I32)
        mean = sb("mean", [P, NT])
        var = sb("var", [P, NT])
        rstd = sb("rstd", [P, NT])
        b1e = sb("b1e", [D, 1])
        epst = sb("epst", [P, 1])
        bnc = sb("bnc", [D, 8])

        early_ctx = ExitStack()

        def early(name, shape, dt=F32):
            return early_ctx.enter_context(nc.sbuf_tensor(name, shape, dt))

        d_prev = early("d_prev", [P, NK], I32)
        d_this = early("d_this", [P, NK], I32)
        keep = early("keep", [P, NK], U8)
        reset = early("reset", [P, NK], BF16)
        first_f = early("first_f", [P, RP])
        tile_f = early("tile_f", [P, NT])
        rel_f = early("rel_f", [P, RP, NT])
        row_f = early("row_f", [P, NT])
        row_i = early("row_i", [P, NT], I32)
        within = early("within", [P, NT])
        end_f = early("end_f", [P, NT])
        one_col = early("one_col", [P, 2 * NT - 1], BF16)
        count = early("count", [NT, P])
        wt = early("wt", [P, NW, O])
        with ExitStack() as sort_ctx:
            def sorting(name, dt):
                return sort_ctx.enter_context(nc.sbuf_tensor(name, [P, NK], dt))
            lo_i = sorting("lo_i", I32)
            hi_i = sorting("hi_i", I32)
            lo_f = sorting("lo_f", F32)
            hi_f = sorting("hi_f", F32)
        dst_rows = early("dst_rows", [P, NT, RL], I32)
        ea_c = early("ea_c", [D, CR, W])

        SC = 14
        SW = EP // SC
        shf = early("shf", [S * SC, SW])
        shp = early("shp", [S * SC, SW], BF16)

        keep_c = early("keep_c", [D, CR, W], U8)
        run_c = early("run_c", [D, 2, W])

        early_ctx.close()
        row_c = xa_t[:, 0:2 * WJ * D].rearrange("p (b w) -> p b w", b=2)

        ea = sb("ea", [D, 2, G])
        s3 = sb("s3", [SP3, 2, G], BF16)
        rs = sb("rs", [P, 2, G], BF16)
        gathered = sb("gathered", [P, 2 * 4 * 4 * P])
        rings = gathered[:, :].rearrange("p (r q k d) -> p r q k d", r=2, q=4, k=4)
        xg, qg = rings[:, 0], rings[:, 1]
        end_rows = gathered[:, 0:NT * RW].rearrange("p (t w) -> p t w", t=NT)
        src_g = sb("src_g", [P, 4, 4], I32)
        dst_g = sb("dst_g", [P, 4, 4], I32)
        xt = sb("xt", [P, 2, G])
        hid = sb("hid", [P, G])
        hid_h = sb("hid_h", [P, G], F32R)
        hid_l = sb("hid_l", [P, G], F32R)
        qt = sb("qt", [P, 2, G])
        wv = sb("wv", [P, 2, G])
        x_flat = x_r[:, :, :].rearrange("p t d -> p (t d)")
        z = xa_t[:, 0:NJ * G].rearrange("p (j g) -> p j g", j=NJ)
        num = x_flat[:, 0:2 * G].rearrange("p (b g) -> p b g", b=2)
        den = x_flat[:, 2 * G:4 * G].rearrange("p (b g) -> p b g", b=2)
        row = x_flat[:, 4 * G:4 * G + 8 * RW].rearrange("p (b j w) -> p b j w", b=2, j=4)
        z_h = sb("z_h", [P, 2, NJ, G], F32R)
        z_l = sb("z_l", [P, 2, NJ - 1, G], F32R)
        kq = sb("kq", [P, 2, G])
        val = sb("val", [P, 2, G])
        mx = sb("mx", [P, 2, G])
        ex = sb("ex", [P, 2, G])
        dm = sb("dm", [P, 2, G])
        rden = sb("rden", [P, NT, H])

        bank = [ctx.enter_context(nc.psum_tensor(f"bank{i}", [P, G], F32)) for i in range(8)]
        ps_xw, ps_hw, ps_s0, ps_s1, ps_k, ps_v, ps_qa, ps_r = bank

        bad_step = sem("bad_step")
        bad_ps = sem("bad_ps")
        bad_ok = sem("bad_ok")
        so1 = sem("so1")
        so1_ps = sem("so1_ps")
        so_off = sem("so_off")
        so_off_ps = sem("so_off_ps")
        so2 = sem("so2")
        so2_turned = sem("so2_turned")
        so2_ps = sem("so2_ps")
        so_row_in = sem("so_row_in")
        so_placed = sem("so_placed")
        so3_in = sem("so3_in")
        so3_ps = sem("so3_ps")
        so3 = sem("so3")
        so3_out = sem("so3_out")
        so_first = sem("so_first")
        resorted = sem("resorted")
        consts_in = sem("consts_in")
        loaded = sem("loaded")
        dlin_in = sem("dlin_in")
        tabs_in = sem("tabs_in")
        sh_in = sem("sh_in")
        x_in = sem("x_in")
        flags_done = sem("flags_done")
        flags_out = sem("flags_out")
        split_done = sem("split_done")
        split_step = sem("split_step")
        split_out = [sem(f"split_out{i}") for i in range(3)]
        sel_done = sem("sel_done")
        hilo = sem("hilo")
        find_step = sem("find_step")
        below_ok = sem("below_ok")
        below_ps = sem("below_ps")
        dst_out = sem("dst_out")
        dst_rows_in = sem("dst_rows_in")
        ends_ok = sem("ends_ok")
        chunk_in = [sem(f"chunk_in{i}") for i in range(CR)]
        chunk_run = sem("chunk_run")
        chunk_ps = sem("chunk_ps")
        chunk_row = sem("chunk_row")
        chunk_out = [sem(f"chunk_out{i}") for i in range(2)]
        agg_in = [sem(f"agg_in{i}") for i in range(len(NODE_BLOCKS))]
        masked = sem("masked")
        b1e_ps = sem("b1e_ps")
        b1e_ok = sem("b1e_ok")
        xat_ps = sem("xat_ps")
        xat_ok = sem("xat_ok")
        h1_ps = sem("h1_ps")
        h1_sig = sem("h1_sig")
        h1_ok = sem("h1_ok")
        h2_ps = sem("h2_ps")
        h2_sig = sem("h2_sig")
        h2_ok = sem("h2_ok")
        res_ok = sem("res_ok")
        rr_ps = sem("rr_ps")
        rr_ok = sem("rr_ok")
        ln = sem("ln")
        ln_sqrt = sem("ln_sqrt")
        x1_ok = sem("x1_ok")
        x1t_ps = sem("x1t_ps")
        x1t_ok = sem("x1t_ok")
        q_ps = sem("q_ps")
        q_ok = sem("q_ok")
        xtab_out = sem("xtab_out")
        qtab_out = sem("qtab_out")
        ea_in = [sem(f"ea_in{i}") for i in range(2)]
        s3_in = [sem(f"s3_in{i}") for i in range(2)]
        rs_in = [sem(f"rs_in{i}") for i in range(2)]
        xg_in = [sem(f"xg_in{i}") for i in range(4)]
        qg_in = [sem(f"qg_in{i}") for i in range(4)]
        src_picked = sem("src_picked")
        dst_picked = sem("dst_picked")
        xt_ps = sem("xt_ps")
        xt_ok = sem("xt_ok")
        hid_ps = sem("hid_ps")
        hid_ok = sem("hid_ok")
        qt_ps = sem("qt_ps")
        qt_ok = sem("qt_ok")
        wk_ps = sem("wk_ps")
        wkq_ok = sem("wkq_ok")
        wv_ps = sem("wv_ps")
        wv_ok = sem("wv_ok")
        shb_ps = sem("shb_ps")
        z_ok = sem("z_ok")
        zh_ok = sem("zh_ok")
        zl_ok = sem("zl_ok")
        hidl_ok = sem("hidl_ok")
        wth_ok = sem("wth_ok")
        wtl_ok = sem("wtl_ok")
        acc_ps = sem("acc_ps")
        kq_ok = sem("kq_ok")
        val_ok = sem("val_ok")
        att_ps = sem("att_ps")
        mx_ok = sem("mx_ok")
        am_ok = sem("am_ok")
        ex_ok = sem("ex_ok")
        dm_ok = sem("dm_ok")
        dmr_ok = sem("dmr_ok")
        dec_ok = sem("dec_ok")
        ev_ok = sem("ev_ok")
        num_ok = sem("num_ok")
        den_ok = sem("den_ok")
        row_ps = sem("row_ps")
        row_ok = sem("row_ok")
        row_out = [sem(f"row_out{i}") for i in range(2)]
        zeroed = sem("zeroed")
        nrow_in = [sem(f"nrow_in{i}") for i in range(len(NODE_BLOCKS))]
        upd_step = sem("upd_step")
        upd_ps = sem("upd_ps")
        upd_ok = sem("upd_ok")
        o_ps = sem("o_ps")
        o_ok = sem("o_ok")
        bn = sem("bn")
        bn_sqrt = sem("bn_sqrt")
        y_ps = sem("y_ps")
        out_ok = sem("out_ok")
        stored = sem("stored")

        block = ctx.enter_context(nc.Block())

        CONSTS = [(iota_row, a["iota_row"]), (ident, a["ident"]), (upper, a["upper"]), (lower, a["lower"]),
                  (node_i, a["node_id"])]
        ALL_CONSTS = 16 * len(CONSTS)
        WEIGHTS = [(sel_f, a["sel"]), (headones, a["headones"]),
                   (wt[:, CK:CK + 4, :], a["c_k"][0:8 * D, :].rearrange("(j p) o -> p j o", p=P)),
                   (wt[:, CV:CV + 4, :], a["c_v"][0:8 * D, :].rearrange("(j p) o -> p j o", p=P)),
                   (wt[0:D, CK + 4, :], a["c_k"][8 * D:9 * D, :]), (wt[D:P, CK + 4, :], a["c_k"][8 * D:9 * D, :]),
                   (wt[0:D, CV + 4, :], a["c_v"][8 * D:9 * D, :]), (wt[D:P, CV + 4, :], a["c_v"][8 * D:9 * D, :]),
                   (w1kv[:, 0:D], a["k_w1"]), (w1kv[:, D:P], a["v_w1"]),
                   (wt[0:D, W2KV, :], a["k_w2"]), (wt[D:P, W2KV, :], a["v_w2"]),
                   (b1kv[0:D, :], a["k_b1"]), (b1kv[D:P, :], a["v_b1"]), (b2k, a["k_b2"]), (b2v, a["v_b2"]),
                   (w1, a["w1"][0:P, :]), (w1u, a["w1"][P:P + D, :]), (b1, a["b1"]), (u0, a["u0"]),
                   (w2, a["w2"]), (b2, a["b2"]), (wq, a["wq"]), (wout, a["wout"]), (wself, a["wself"]),
                   (gamma, a["gamma"]), (beta, a["beta"])]
        ALL_WEIGHTS = 16 * len(WEIGHTS)

        def tiles_of(n):
            lo, w = NODE_BLOCKS[n]
            return range(lo // P, (lo + w) // P)

        def staggered(*stages):
            for step in range(len(NODE_BLOCKS) + len(stages) - 1):
                for i, stage in reversed(list(enumerate(stages))):
                    if stage is not None and 0 <= step - i < len(NODE_BLOCKS):
                        stage(step - i, *NODE_BLOCKS[step - i])

        def live(g):
            return not isinstance(g, int) or 0 <= g < NG

        def used(eng, s, g, per=1):
            if not isinstance(g, int) or g >= 2:
                eng.wait_ge(s, (g - 1) * per)

        def steps(eng, body):
            for t in range(-2, 4):
                body(t, t % 2, t % 4)
            with eng.Fori(0, (NG - 8) // 4) as i:
                for r in range(4):
                    body(i * 4 + (4 + r), r % 2, r)
            for t in range(NG - 4, NG + 2):
                body(t, t % 2, t % 4)

        def carry(ins, s, n):
            return ins.wait_op(s, n, "sem-ge")

        def arrived(eng, ring, g, b, per=16):
            n = len(ring)
            if isinstance(g, int):
                eng.wait_ge(ring[b], (g // n + 1) * per)
            else:
                eng.wait_ge(ring[b], (g - b + n) * (per // n))

        def loads_and_stores(sp, edges_t):
            sp.dma_start(x_r[:, :, 0:D], a["x"].rearrange("(t p) d -> p t d", p=P)).then_inc(x_in, 16)
            sp.wait_ge(flags_done, 2)
            sp.dma_start(keep_d.rearrange("(p c) -> p c", p=P), keep[:, :]).then_inc(flags_out, 16)
            sp.dma_start(reset_d.rearrange("(p c) -> p c", p=P), reset[:, :]).then_inc(flags_out, 16)
            sp.dma_start(dst_d.rearrange("(p c) -> p c", p=P), d_this[:, :]).then_inc(dst_out, 16)
            sp.wait_ge(flags_out, 32)

            def load_chunk(c, b):
                lo = c * W
                if not isinstance(c, int) or c >= CR:
                    sp.wait_ge(chunk_run, c - (CR - 1))
                sp.dma_start(ea_c[:, b, :], edges_t[:, bass.ds(lo, W)]).then_inc(chunk_in[b], 16)
                sp.dma_start(keep_c[:, b, :],
                             keep_d[bass.ds(lo, W)].rearrange("(o w) -> o w", o=1).to_broadcast([D, W])
                             ).then_inc(chunk_in[b], 16)

            def store_chunk(c, b):
                sp.wait_ge(chunk_row, c * 2 + 2)
                sp.dma_start(aggrow_d[bass.ds(c * W, W), :].rearrange("(p j) d -> p (j d)", p=P),
                             row_c[:, b, :]).then_inc(chunk_out[b], 16)

            load_chunk(0, 0)
            load_chunk(1, 1)
            with sp.Fori(0, CL) as i:
                for r in range(CR):
                    load_chunk(i * CR + (CR + r), r)
                    store_chunk(i * CR + r, r)
            for c in range(CL * CR, NC):
                if c + CR < NC:
                    load_chunk(c + CR, c % CR)
                store_chunk(c, c % CR)

            sp.wait_ge(x1_ok, 1)
            for half in range(2):
                sp.dma_start(xtab_d[:, half * D:(half + 1) * D].rearrange("(t p) d -> p t d", p=P),
                             x1_r[:, :, :]).then_inc(xtab_out, 16)

            for part in range(3):
                sp.wait_ge(split_out[part], 16)

            def load_rs(g, b):
                used(sp, mx_ok, g)
                used(sp, dmr_ok, g)
                sp.dma_start(rs[:, b, :], reset_d[bass.ds(g * G, G)].rearrange("(o w) -> o w", o=1)
                             .to_broadcast([P, G])).then_inc(rs_in[b], 16)

            def load_edge(g, b):
                used(sp, shb_ps, g, NJ)
                used(sp, hid_ps, g)
                sp.dma_start(ea[:, b, :], edges_t[:, bass.ds(g * G, G)]).then_inc(ea_in[b], 16)
                sp.dma_start(s3[:, b, :], sh3_d.rearrange("a s e -> (a s) e")[:, bass.ds(g * G, G)]
                             ).then_inc(s3_in[b], 16)

            def store_row(g, b):
                sp.wait_ge(row_ok, g * 4 + 4)
                sp.dma_start(nrow_d[bass.ds(g * G, G), :].rearrange("(p j) w -> p (j w)", p=P),
                             row[:, b, :, :].rearrange("p j w -> p (j w)")).then_inc(row_out[b], 16)

            def body(t, b, q):
                if live(t + 2):
                    load_edge(t + 2, b)
                if live(t):
                    load_rs(t, b)
                if live(t - 2):
                    store_row(t - 2, b)
            steps(sp, body)

        @block.sync
        def _(sp):
            sp.dma_start(d_prev[:, :], a["dst_lin"][0:EP].rearrange("(p c) -> p c", p=P)).then_inc(dlin_in, 16)
            sp.dma_start(d_this[:, :], a["dst_lin"][1:EP + 1].rearrange("(p c) -> p c", p=P)).then_inc(dlin_in, 16)
            sp.dma_start(dst_t[:, :], a["dst_t"]).then_inc(tabs_in, 16)
            sp.dma_start(src_t[:, :], a["src_t"]).then_inc(tabs_in, 16)
            for dst, src in CONSTS:
                sp.dma_start(dst[:, :], src).then_inc(consts_in, 16)

            sp.wait_ge(bad_ok, 1)
            unsorted = sp.value_load(bad[0:1, 0:1], min_val=0, max_val=1)
            with sp.If(unsorted == 1):
                with sp.Fori(0, NK) as k:
                    sp.dma_start(so_row[:, 0:D], a["ea_rows"][bass.ds(k * P, P), :]).then_inc(so_row_in, 16)
                    sp.dma_start(so_row[:, D:D + S], a["sh_rows"][bass.ds(k * P, P), :]).then_inc(so_row_in, 16)
                    for col, name in ((RS_SRC, "src_col"), (RS_DST, "dst_col")):
                        sp.dma_start(so_row[:, col:col + 1].bitcast(I32), a[name][bass.ds(k * P, P), :]
                                     ).then_inc(so_row_in, 16)
                    sp.wait_ge(so_placed, k * 16 + 16)
                    carry(sp.nop(nofuse=True), bad_ok, 1)
                with sp.Fori(0, NK) as k:
                    sp.dma_start(so_row, rows_s[bass.ds(k * P, P), :]).then_inc(so3_in, 16)
                    sp.wait_ge(so3, k * 3 + 3)
                    carry(sp.nop(nofuse=True), bad_ok, 1)
                    sp.dma_start(ea_s[:, bass.ds(k * P, P)], so_turn[0:D, :]).then_inc(so3_out, 16)
                    sp.dma_start(sh_s[:, bass.ds(k * P, P)], so_turn[D:D + S, :]).then_inc(so3_out, 16)
                    sp.dma_start(dst_s[bass.ds(k * P + 1, P)].rearrange("(p o) -> p o", o=1),
                                 so_row[:, RS_DST:RS_DST + 1].bitcast(I32)).then_inc(so3_out, 16)
                    sp.wait_ge(so3_out, k * 48 + 48)
                    carry(sp.nop(nofuse=True), bad_ok, 1)
                sp.dma_start(dst_s[0:1], a["dst_lin"][0:1]).then_inc(so_first, 16)
                sp.wait_ge(so_first, 16)
                sp.dma_start(d_prev[:, :], dst_s[0:EP].rearrange("(p c) -> p c", p=P)).then_inc(resorted, 16)
                sp.dma_start(d_this[:, :], dst_s[1:EP + 1].rearrange("(p c) -> p c", p=P)).then_inc(resorted, 16)
                sp.dma_start(shf[:, :], sh_s.rearrange("s (c w) -> (s c) w", c=SC)).then_inc(sh_in, 16)
                loads_and_stores(sp, ea_s)
            with sp.Else():
                sp.dma_start(shf[:, :], a["sh_t"].rearrange("s (c w) -> (s c) w", c=SC)).then_inc(sh_in, 16)
                loads_and_stores(sp, a["ea_t"])
            sp.wait_ge(out_ok, 1)
            sp.dma_start(out.rearrange("(t p) d -> p t d", p=P), r_r[:, :, :]).then_inc(stored, 16)
            sp.wait_ge(stored, 16)

        @block.gpsimd
        def _(pool):
            pool.memset(ones[:, :], 1.0).then_inc(zeroed, 1)
            pool.memset(epst[:, :], EPS).then_inc(zeroed, 1)
            pool.memset(one_col[:, :], 0.0).then_inc(zeroed, 1)
            pool.wait_ge(zeroed, 3)
            pool.memset(one_col[:, NT - 1:NT], 1.0).then_inc(zeroed, 1)
            pool.memset(run_c[:, 1, W - 1:W], 0.0).then_inc(zeroed, 1)

            pool.wait_ge(bad_ok, 1)
            unsorted = pool.value_load(bad[0:1, 0:1], min_val=0, max_val=1)
            with pool.If(unsorted == 1):
                with pool.Fori(0, NK) as k:
                    pool.wait_ge(so2, k * SORT2 + (SORT2 - 1))
                    pool.wait_ge(so_row_in, k * 64 + 64)
                    carry(pool.indirect_dma_start(rows_s[:, :], bass.IndirectOffsetOnAxis(ap=so_pos[:, 0:1], axis=0),
                                                  so_row, None), bad_ok, 1).then_inc(so_placed, 16)
                pool.wait_ge(so3, 3 * NK)

            pool.wait_ge(find_step, 6)
            pool.wait_ge(dst_out, 16)
            for t in range(NT):
                pool.indirect_dma_start(dst_rows[:, t, :], None, dst_d.rearrange("(r c) -> r c", c=RL),
                                        bass.IndirectOffsetOnAxis(ap=row_i[:, t:t + 1], axis=0)
                                        ).then_inc(dst_rows_in, 16)

            pool.wait_ge(ends_ok, 2)
            pool.wait_ge(chunk_out[0], 16 * ((NC + 1) // 2))
            pool.wait_ge(chunk_out[1], 16 * (NC // 2))
            for t in range(NT):
                pool.indirect_dma_start(x_r[:, t, D:2 * D], None, aggrow_d[:, :],
                                        bass.IndirectOffsetOnAxis(ap=end_i[:, t:t + 1], axis=0)).then_inc(agg_in[t * P // G], 16)

            for part in range(3):
                pool.wait_ge(split_out[part], 16)
            pool.wait_ge(tabs_in, 32)

            def gather(g, b, rows, ring, table, out, outs, index, picked, picks, read):
                if not isinstance(g, int) or g >= 4:
                    arrived(pool, ring, g - 4, b, 64)
                pool.tensor_copy(picked[:, b, :], index[:, bass.ds(g * 4, 4)]).then_inc(picks, 1)
                if not isinstance(g, int) or g >= 4:
                    pool.wait_ge(read, g - 3)
                pool.wait_ge(picks, g + 1)
                for k in range(4):
                    rows_in = pool.indirect_dma_start(rows[:, b, k, :], None, table,
                                                      bass.IndirectOffsetOnAxis(ap=picked[:, b, k:k + 1], axis=0))
                    if k == 0:
                        carry(rows_in, out, outs)
                    rows_in.then_inc(ring[b], 16)

            def gather_x(g, b):
                gather(g, b, xg, xg_in, xtab_d[:, :], xtab_out, 32, src_t, src_g, src_picked, xt_ps)

            def gather_q(g, b):
                gather(g, b, qg, qg_in, qtab_d[:, :], qtab_out, 16, dst_t, dst_g, dst_picked, qt_ps)

            def shift(g, b):
                pool.wait_ge(mx_ok, g + 1)
                used(pool, den_ok, g)
                pool.tensor_tensor(dm[:, b, 1:G], mx[:, b, 0:G - 1], mx[:, b, 1:G], ALU.subtract).then_inc(dm_ok, 1)
                pool.tensor_tensor(dm[:, b, 0:1], mx[:, 1 - b, G - 1:G], mx[:, b, 0:1], ALU.subtract
                                   ).then_inc(dm_ok, 1)
                arrived(pool, rs_in, g, b)
                pool.wait_ge(dm_ok, g * 2 + 2)
                pool.tensor_tensor(dm[:, b, :], dm[:, b, :], rs[:, b, :], ALU.add).then_inc(dmr_ok, 1)

            def body(t, b, q):
                if live(t + 4):
                    gather_x(t + 4, q)
                if live(t + 3):
                    gather_q(t + 3, (q + 3) % 4)
                if live(t - 1):
                    shift(t - 1, 1 - b)
            for g in range(2):
                gather_x(g, g)
            pool.wait_ge(qtab_out, 16)
            for scanned in (mx, num, den):
                pool.memset(scanned[:, 1, G - 1:G], 0.0).then_inc(zeroed, 1)
            gather_q(0, 0)
            steps(pool, body)

            pool.wait_ge(row_out[0], 16 * (NG // 2))
            pool.wait_ge(row_out[1], 16 * (NG // 2))
            for t in range(NT):
                pool.indirect_dma_start(end_rows[:, t, :], None, nrow_d[:, :],
                                        bass.IndirectOffsetOnAxis(ap=end_i[:, t:t + 1], axis=0)).then_inc(nrow_in[t * P // G], 16)


        ROW_TILES = [(b, list(range(8 * b, min(8 * b + 8, NT)))) for b in range(-(-NT // 8))]

        @block.scalar
        def _(act):
            for dst, src in WEIGHTS:
                act.dma_start(dst[:] if not isinstance(dst, bass.AP) else dst, src).then_inc(loaded, 16)
            act.wait_ge(loaded, ALL_WEIGHTS)
            act.activation(sel[:, :, :].rearrange("k j m -> k (j m)"), sel_f[:, :], ACT.Copy).then_inc(sel_done, 1)

            act.activation(wt_h[:, :, :], wt[:, :, :], ACT.Copy).then_inc(wth_ok, 1)

            act.wait_ge(sh_in, 16)
            for part in range(3):
                if part > 0:
                    act.wait_ge(split_step, part)
                    act.wait_ge(split_out[part - 1], 16)
                act.activation(shp[:, :], shf[:, :], ACT.Copy).then_inc(split_done, 1)
                act.wait_ge(split_done, part + 1)
                act.dma_start(sh3_d[part].rearrange("s (c w) -> (s c) w", c=SC), shp[:, :]
                              ).then_inc(split_out[part], 16)

            def rows_out(c, b):
                if not isinstance(c, int) or c >= 2:
                    arrived(act, chunk_out, c - 2, b)
                for h in range(2):
                    act.wait_ge(chunk_ps, c * 2 + (h + 1))
                    act.activation(row_c[:, b, h * G:(h + 1) * G], bank[2 * b + h][:, :], ACT.Copy
                                   ).then_inc(chunk_row, 1)
            rows_out(0, 0)
            rows_out(1, 1)
            with act.Fori(0, (NC - 3) // 2) as i:
                for r in range(2):
                    rows_out(i * 2 + (2 + r), r)
            rows_out(NC - 1, 0)

            act.wait_ge(b1e_ok, 1)

            def inputs_turned(n, lo, w):
                act.wait_ge(xat_ps, n + 1)
                act.activation(xa_t[:, lo:lo + w], bank[n][:, 0:w], ACT.Copy).then_inc(xat_ok, 1)

            def gate_1(n, lo, w):
                act.wait_ge(h1_ps, n + 1)
                act.activation(sg_t[:, lo:lo + w], bank[n][0:D, 0:w], ACT.Sigmoid, bias=b1e[:, :]).then_inc(h1_sig, 1)

            def gate_2(n, lo, w):
                act.wait_ge(h2_ps, n + 1)
                act.wait_ge(h1_ok, n + 1)
                act.activation(sg_t[:, lo:lo + w], bank[n][0:D, 0:w], ACT.Sigmoid, bias=b2[:, :]).then_inc(h2_sig, 1)
            staggered(inputs_turned, None, gate_1, gate_2)
            act.wait_ge(ln, 5)
            act.activation(rstd[:, :], var[:, :], ACT.Sqrt, scale=1.0 / D, bias=epst[:, :]).then_inc(ln_sqrt, 1)
            for n, (lo, w) in enumerate(NODE_BLOCKS):
                act.wait_ge(x1t_ps, n + 1)
                act.activation(x1_t[:, lo:lo + w], bank[n][0:D, 0:w], ACT.Copy).then_inc(x1t_ok, 1)
            for n, (lo, w) in enumerate(NODE_BLOCKS):
                act.wait_ge(q_ps, n + 1)
                act.activation(q_r[:, lo // P:(lo + w) // P, :].rearrange("p t o -> p (t o)"),
                               bank[n][:, 0:w], ACT.Copy).then_inc(q_ok, 1)
            act.wait_ge(q_ok, len(NODE_BLOCKS))
            act.dma_start(qtab_d.rearrange("(t p) d -> p t d", p=P), q_r).then_inc(qtab_out, 16)

            def front_x(g, b):
                act.wait_ge(xt_ps, g + 1)
                used(act, z_ok, g, NJ)
                act.activation(xt[:, b, :], ps_xw[:, :], ACT.Copy).then_inc(xt_ok, 1)

            def front_h(g, b):
                act.wait_ge(hid_ps, g + 1)
                if not isinstance(g, int) or g >= 1:
                    act.wait_ge(wv_ps, g)
                act.activation(hid[:, :], ps_hw[:, :], ACT.Relu, bias=b1kv[:, :]).then_inc(hid_ok, 1)
                act.activation(hid_h[:, :], ps_hw[:, :], ACT.Relu, bias=b1kv[:, :]).then_inc(hid_ok, 1)

            def outer_high(g, b, j):
                if j == 0:
                    used(act, acc_ps, g)
                act.wait_ge(z_ok, g * NJ + (j + 1))
                act.activation(z_h[:, b, j, :], z[:, j, :], ACT.Copy).then_inc(zh_ok, 1)

            def front_q(g, b):
                act.wait_ge(qt_ps, g + 1)
                used(act, kq_ok, g)
                act.activation(qt[:, b, :], ps_qa[:, :], ACT.Copy).then_inc(qt_ok, 1)

            def weights_v(g, b):
                act.wait_ge(wv_ps, g + 1)
                used(act, val_ok, g)
                act.activation(wv[:, b, :], ps_hw[:, :], ACT.Identity, bias=b2v[:, :]).then_inc(wv_ok, 1)

            def exponents(g, b):
                act.wait_ge(am_ok, g + 1)
                used(act, den_ok, g)
                act.activation(ex[:, b, :], ex[:, b, :], ACT.Exp).then_inc(ex_ok, 1)
                act.wait_ge(dmr_ok, g + 1)
                act.activation(dm[:, b, :], dm[:, b, :], ACT.Exp).then_inc(dec_ok, 1)

            def rows(g, b, h):
                if h == 0 and (not isinstance(g, int) or g >= 2):
                    arrived(act, row_out, g - 2, b)
                act.wait_ge(row_ps, g * 2 + (h + 1))
                act.activation(row[:, b, 2 * h:2 * h + 2, 0:O],
                               ps_r[:, 0:2 * O].rearrange("p (j o) -> p j o", j=2), ACT.Copy).then_inc(row_ok, 1)
                act.activation(row[:, b, 2 * h:2 * h + 2, O:RW],
                               ps_r[:, 2 * O:2 * O + 2 * H].rearrange("p (j h) -> p j h", j=2),
                               ACT.Copy).then_inc(row_ok, 1)

            def body(t, b, q):
                if live(t + 1):
                    front_h(t + 1, 1 - b)
                    outer_high(t + 1, 1 - b, 0)
                if live(t + 2):
                    front_x(t + 2, b)
                if live(t + 1):
                    front_q(t + 1, 1 - b)
                    outer_high(t + 1, 1 - b, 1)
                    weights_v(t + 1, 1 - b)
                    outer_high(t + 1, 1 - b, 2)
                    outer_high(t + 1, 1 - b, 3)
                if live(t - 2):
                    rows(t - 2, b, 0)
                if live(t + 1):
                    outer_high(t + 1, 1 - b, 4)
                if live(t - 2):
                    rows(t - 2, b, 1)
                if live(t - 1):
                    exponents(t - 1, 1 - b)
            steps(act, body)

            for n, (lo, w) in enumerate(NODE_BLOCKS):
                act.wait_ge(upd_ps, n + 1)
                act.activation(xa_t[:, lo:lo + w], bank[n][:, 0:w], ACT.Copy).then_inc(upd_ok, 1)
            act.wait_ge(bn, 5)
            act.activation(bnc[:, 3:4], bnc[:, 2:3], ACT.Sqrt, scale=1.0 / N, bias=epst[0:D, :]).then_inc(bn_sqrt, 1)
            act.wait_ge(ln, LN_STEPS + 5)
            act.activation(rstd[:, :], var[:, :], ACT.Sqrt, scale=1.0 / D, bias=epst[:, :]).then_inc(ln_sqrt, 1)

        @block.tensor
        def _(pe):
            pe.wait_ge(zeroed, 1)
            pe.wait_ge(bad_step, 2)
            pe.matmul(bank[6][0:1, 0:1], bad_col[:, :], ones[:, 0:1], start=True, stop=True).then_inc(bad_ps, 1)
            pe.wait_ge(bad_ok, 1)
            pe.wait_ge(consts_in, ALL_CONSTS)
            unsorted = pe.value_load(bad[0:1, 0:1], min_val=0, max_val=1)
            with pe.If(unsorted == 1):
                with pe.Fori(0, NK) as k:
                    pe.wait_ge(so1, k * 3 + 2)
                    pe.matmul(bank[0][0:NT, 0:P], so_hi, so_lo, start=True, stop=True).then_inc(so1_ps, 1)
                pe.wait_ge(so_off, 2)
                pe.matmul(bank[0][0:NT, 0:1], upper[0:NT, 0:NT], so_cum[:, P - 1:P], start=True, stop=True
                          ).then_inc(so_off_ps, 1)
                pe.wait_ge(so_off, 5)
                with pe.Fori(0, NK) as k:
                    pe.wait_ge(so2, k * SORT2 + 4)
                    pe.transpose(bank[0][0:NT, 0:P], so_hi, ident[:, :])
                    pe.transpose(bank[1][:, 0:P], so_bc, ident[:, :]).then_inc(so2_turned, 1)
                    pe.wait_ge(so2, k * SORT2 + 5)
                    pe.matmul(bank[2][:, 0:P], so_hit, so_cum, start=True, stop=True)
                    pe.matmul(bank[3][0:NT, 0:P], so_hi, so_lo, start=True, stop=True).then_inc(so2_ps, 1)
                with pe.Fori(0, NK) as k:
                    pe.wait_ge(so3_in, k * 16 + 16)
                    pe.transpose(bank[0][0:D + S, 0:P], so_row[:, 0:D + S], ident[:, :]).then_inc(so3_ps, 1)

            pe.wait_ge(zeroed, 4)
            pe.wait_ge(below_ok, 1)
            for k in range(RP):
                pe.wait_ge(below_ok, k + 1)
                for t in range(NT):
                    mm = pe.matmul(bank[7][0:NT, 0:P], one_col[:, NT - 1 - t:2 * NT - 1 - t],
                                   flags[k % 2][:, t * P:(t + 1) * P],
                                   start=k == 0 and t == 0, stop=k == RP - 1 and t == NT - 1)
                mm.then_inc(below_ps, 1)
            pe.wait_ge(loaded, ALL_WEIGHTS)
            pe.matmul(bank[6][0:D, 448:449], w1u[:, :], u0[:, :], start=True, stop=True).then_inc(b1e_ps, 1)
            pe.wait_ge(find_step, 4)
            pe.transpose(bank[7][:, P:P + NT], count[:, :], ident[0:NT, 0:NT]).then_inc(below_ps, 1)

            def chunk_rows(c, b):
                pe.wait_ge(chunk_run, c + 1)
                for h in range(2):
                    used(pe, chunk_row, c, 2)
                    for j in range(8):
                        tr = pe.transpose(bank[2 * b + h][:, j * D:(j + 1) * D],
                                          run_c[:, b, bass.ds(8 * h + j, P, WJ)], ident[0:D, 0:D])
                        if j == 0:
                            carry(tr, consts_in, ALL_CONSTS)
                    tr.then_inc(chunk_ps, 1)

            chunk_rows(0, 0)
            chunk_rows(1, 1)
            with pe.Fori(0, (NC - 3) // 2) as i:
                for r in range(2):
                    chunk_rows(i * 2 + (2 + r), r)
            chunk_rows(NC - 1, 0)

            pe.wait_ge(chunk_row, 2 * NC)

            def turn_inputs(n, lo, w):
                pe.wait_ge(masked, n + 1)
                for t in tiles_of(n):
                    tr = pe.transpose(bank[n][:, t * P - lo:(t + 1) * P - lo], x_r[:, t, :], ident[:, :])
                tr.then_inc(xat_ps, 1)

            def layer_1(n, lo, w):
                pe.wait_ge(xat_ok, n + 1)
                pe.matmul(bank[n][0:D, 0:w], w1[:, :], xa_t[:, lo:lo + w], start=True, stop=True).then_inc(h1_ps, 1)

            def layer_2(n, lo, w):
                pe.wait_ge(h1_ok, n + 1)
                pe.matmul(bank[n][0:D, 0:w], w2[:, :], h_t[:, lo:lo + w], start=True, stop=True).then_inc(h2_ps, 1)
            staggered(turn_inputs, None, layer_1, layer_2)
            pe.wait_ge(res_ok, len(NODE_BLOCKS))
            for b, tiles in ROW_TILES:
                for j, t in enumerate(tiles):
                    tr = pe.transpose(bank[b][:, j * D:(j + 1) * D], h_t[:, t * P:(t + 1) * P], ident[0:D, 0:D])
                tr.then_inc(rr_ps, 1)
            pe.wait_ge(x1_ok, 1)
            for n, (lo, w) in enumerate(NODE_BLOCKS):
                for t in range(lo // P, (lo + w) // P):
                    tr = pe.transpose(bank[n][0:D, t * P - lo:(t + 1) * P - lo], x1_r[:, t, :], ident[:, :])
                tr.then_inc(x1t_ps, 1)
            for n, (lo, w) in enumerate(NODE_BLOCKS):
                pe.wait_ge(x1t_ok, n + 1)
                for t in range(lo // P, (lo + w) // P):
                    mm = pe.matmul(bank[n][:, t * P - lo:(t + 1) * P - lo], x1_t[:, t * P:(t + 1) * P], wq[:, :],
                                   start=True, stop=True)
                mm.then_inc(q_ps, 1)
            pe.wait_ge(q_ok, len(NODE_BLOCKS))
            pe.wait_ge(sel_done, 1)
            pe.wait_ge(wtl_ok, 1)

            def x_turn(g, q):
                arrived(pe, xg_in, g, q, 64)
                used(pe, wkq_ok, g)
                if isinstance(g, int) and g == 1:
                    pe.wait_ge(xt_ok, 1)
                for k in range(4):
                    tr = pe.transpose(ps_xw[:, k * P:(k + 1) * P], xg[:, q, k, :], ident[:, :])
                tr.then_inc(xt_ps, 1)

            def hidden(g, b):
                arrived(pe, ea_in, g, b)
                if not isinstance(g, int) or g >= 1:
                    pe.wait_ge(wv_ok, g)
                pe.matmul(ps_hw[:, :], w1kv[:, :], ea[:, b, :], start=True, stop=True).then_inc(hid_ps, 1)

            def q_turn(g, q):
                arrived(pe, qg_in, g, q, 64)
                if not isinstance(g, int) or g >= 3:
                    pe.wait_ge(am_ok, g - 2)
                elif g >= 1:
                    pe.wait_ge(qt_ok, g)
                for k in range(4):
                    tr = pe.transpose(ps_qa[:, k * P:(k + 1) * P], qg[:, q, k, :], ident[:, :])
                tr.then_inc(qt_ps, 1)

            def split_matmul(ps, w, high, low, start, stop=False, rows=slice(0, P)):
                pe.matmul(ps[:, :], wt_h[rows, w, :], high, start=start, stop=False)
                pe.matmul(ps[:, :], wt_h[rows, w, :], low, start=False, stop=False)
                return pe.matmul(ps[:, :], wt_l[rows, w, :], high, start=False, stop=stop)

            def split_matmul_last(ps, w, both):
                pe.matmul(ps[:, :], wt_h[:, w, :], both, start=False, stop=False)
                return pe.matmul(ps[:, :], wt_l[0:D, w, :], both[0:D, :], start=False, stop=True)

            def weights(g, b):
                pe.wait_ge(hidl_ok, g + 1)
                if not isinstance(g, int) or g + 1 < NG:
                    pe.wait_ge(xt_ok, g + 2)
                else:
                    pe.wait_ge(xt_ok, NG)
                for ps, rows, done in ((ps_xw, slice(0, D), wk_ps), (ps_hw, slice(D, P), wv_ps)):
                    split_matmul(ps, W2KV, hid_h[rows, :], hid_l[rows, :], True, True, rows).then_inc(done, 1)

            def spread(g, b, j):
                if j == 0:
                    arrived(pe, s3_in, g, b)
                if not isinstance(g, int) or g * NJ + j >= 2:
                    pe.wait_ge(z_ok, g * NJ + (j - 1))
                pe.matmul(bank[2 + (NJ * b + j) % 2][:, :], sel[:, j, :], s3[:, b, :], start=True, stop=True
                          ).then_inc(shb_ps, 1)

            def products(g, b, j):
                pe.wait_ge(zl_ok, g * NJ + (j + 1))
                if j == 0 and (not isinstance(g, int) or g >= 1):
                    pe.wait_ge(kq_ok, g)
                    pe.wait_ge(val_ok, g)
                if j < 4:
                    split_matmul(ps_k, CK + j, z_h[:, b, j, :], z_l[:, b, j, :], j == 0)
                    split_matmul(ps_v, CV + j, z_h[:, b, j, :], z_l[:, b, j, :], j == 0)
                else:
                    split_matmul_last(ps_k, CK + j, z_h[:, b, j, :])
                    split_matmul_last(ps_v, CV + j, z_h[:, b, j, :]).then_inc(acc_ps, 1)

            def scores(g, b):
                pe.wait_ge(kq_ok, g + 1)
                pe.wait_ge(qt_ok, g + 3 if not isinstance(g, int) or g + 3 <= NG else NG)
                pe.matmul(ps_qa[:, :], headones[:, :], kq[:, b, :], start=True, stop=True).then_inc(att_ps, 1)

            def row_turn(g, b, h):
                pe.wait_ge(num_ok, g + 1)
                pe.wait_ge(den_ok, g + 1)
                if h == 1 or not isinstance(g, int) or g >= 1:
                    pe.wait_ge(row_ok, g * 4 + 2 * h)
                for i in range(2):
                    j = 2 * h + i
                    pe.transpose(ps_r[:, i * O:(i + 1) * O], num[:, b, bass.ds(j, P, 4)], ident[:, :])
                    mm = pe.matmul(ps_r[:, 2 * O + i * H:2 * O + (i + 1) * H], den[:, b, bass.ds(j, P, 4)],
                                   ident[:, bass.ds(0, H, DH)], start=True, stop=True)
                mm.then_inc(row_ps, 1)

            def body(t, b, q):
                if live(t + 1):
                    spread(t + 1, 1 - b, 0)
                    spread(t + 1, 1 - b, 1)
                if live(t + 2):
                    x_turn(t + 2, (q + 2) % 4)
                if live(t + 1):
                    hidden(t + 1, 1 - b)
                    q_turn(t + 1, (q + 1) % 4)
                for j in range(NJ):
                    if live(t):
                        products(t, b, j)
                    if j + 2 < NJ and live(t + 1):
                        spread(t + 1, 1 - b, j + 2)
                    if j == 1 and live(t + 1):
                        weights(t + 1, 1 - b)
                    if j == 1 and live(t - 1):
                        scores(t - 1, 1 - b)
                    if j == 2 and live(t - 2):
                        row_turn(t - 2, b, 0)
                    if j == 4 and live(t - 2):
                        row_turn(t - 2, b, 1)
            steps(pe, body)

            pe.wait_ge(row_ok, 4 * NG)
            pe.wait_ge(am_ok, NG)
            pe.wait_ge(val_ok, NG)

            def turn_updates(n, lo, w):
                pe.wait_ge(upd_step, 4 * n + 4)
                for t in tiles_of(n):
                    tr = pe.transpose(bank[n][:, t * P - lo:(t + 1) * P - lo], end_rows[:, t, 0:O], ident[:, :])
                tr.then_inc(upd_ps, 1)

            def project(n, lo, w):
                pe.wait_ge(upd_ok, n + 1)
                pe.matmul(bank[n][0:D, 0:w], wself[:, :], x1_t[:, lo:lo + w], start=True, stop=False)
                pe.matmul(bank[n][0:D, 0:w], wout[:, :], xa_t[:, lo:lo + w], start=False, stop=True).then_inc(o_ps, 1)
            staggered(turn_updates, project)
            pe.wait_ge(bn, 8)
            for b, tiles in ROW_TILES:
                for j, t in enumerate(tiles):
                    tr = pe.transpose(bank[b][:, j * D:(j + 1) * D], h_t[:, t * P:(t + 1) * P], ident[0:D, 0:D])
                tr.then_inc(y_ps, 1)

        @block.vector
        def _(dve):
            dve.wait_ge(dlin_in, 32)
            falls = x1_r[:, :, :].rearrange("p t d -> p (t d)")[:, 0:NK]
            dve.tensor_tensor(falls, d_this[:, :], d_prev[:, :], ALU.is_lt).then_inc(bad_step, 1)
            dve.wait_ge(bad_step, 1)
            dve.tensor_reduce(bad_col[:, :], falls, AX_X, ALU.add).then_inc(bad_step, 1)
            dve.wait_ge(bad_ps, 1)
            dve.tensor_scalar(bad[:, :], bank[6][0:1, 0:1], 1.0, None, ALU.min).then_inc(bad_ok, 1)
            dve.wait_ge(bad_ok, 1)
            dve.wait_ge(consts_in, ALL_CONSTS)
            dve.wait_ge(tabs_in, 32)
            unsorted = dve.value_load(bad[0:1, 0:1], min_val=0, max_val=1)
            with dve.If(unsorted == 1):
                dve.tensor_scalar(lo_i[:, :], dst_t[:, :], P - 1, None, ALU.bitwise_and).then_inc(hilo, 1)
                dve.tensor_scalar(hi_i[:, :], dst_t[:, :], 7, None, ALU.logical_shift_right).then_inc(hilo, 1)
                dve.wait_ge(hilo, 2)
                dve.tensor_copy(lo_f[:, :], lo_i[:, :]).then_inc(hilo, 1)
                dve.tensor_copy(hi_f[:, :], hi_i[:, :]).then_inc(hilo, 1)
                dve.wait_ge(hilo, 4)
                dve.memset(so_count, 0.0).then_inc(so_off, 1)
                dve.wait_ge(so_off, 1)
                with dve.Fori(0, NK) as k:
                    dve.tensor_scalar(so_lo, iota_row[:, :], lo_f[:, bass.ds(k, 1)], None, ALU.is_equal
                                      ).then_inc(so1, 1)
                    dve.tensor_scalar(so_hi, iota_row[:, 0:NT], hi_f[:, bass.ds(k, 1)], None, ALU.is_equal
                                      ).then_inc(so1, 1)
                    dve.wait_ge(so1_ps, k + 1)
                    dve.tensor_tensor(so_count, so_count, bank[0][0:NT, 0:P], ALU.add).then_inc(so1, 1)
                    dve.wait_ge(so1, k * 3 + 3)
                dve.tensor_tensor_scan(so_cum, ones[0:NT, :], so_count, 0.0, ALU.mult, ALU.add).then_inc(so_off, 1)
                dve.wait_ge(so_off_ps, 1)
                dve.tensor_copy(so_before, bank[0][0:NT, 0:1]).then_inc(so_off, 1)
                dve.wait_ge(so_off, 3)
                dve.tensor_tensor(so_cum, so_cum, so_count, ALU.subtract).then_inc(so_off, 1)
                dve.wait_ge(so_off, 4)
                dve.tensor_scalar(so_cum, so_cum, so_before, None, ALU.add).then_inc(so_off, 1)
                dve.wait_ge(so_off, 5)
                with dve.Fori(0, NK) as k:
                    dve.tensor_scalar(so_lo, iota_row[:, :], lo_f[:, bass.ds(k, 1)], None, ALU.is_equal
                                      ).then_inc(so2, 1)
                    dve.tensor_scalar(so_hi, iota_row[:, 0:NT], hi_f[:, bass.ds(k, 1)], None, ALU.is_equal
                                      ).then_inc(so2, 1)
                    dve.tensor_copy(so_dst, dst_t[:, bass.ds(k, 1)]).then_inc(so2, 1)
                    dve.wait_ge(so2, k * SORT2 + 3)
                    dve.tensor_scalar(so_bc, ones[:, :], so_dst, None, ALU.mult).then_inc(so2, 1)
                    dve.wait_ge(so2_turned, k + 1)
                    dve.tensor_copy(so_hit, bank[0][0:NT, 0:P]).then_inc(so2, 1)
                    dve.scalar_tensor_tensor(out=so_bc, in0=bank[1][:, 0:P], scalar=so_dst, in1=lower[:, :],
                                             op0=ALU.is_equal, op1=ALU.mult).then_inc(so2, 1)
                    dve.wait_ge(so2, k * SORT2 + 6)
                    dve.tensor_reduce(so_rank, so_bc, AX_X, ALU.add).then_inc(so2, 1)
                    dve.wait_ge(so2_ps, k + 1)
                    dve.tensor_tensor(so_prod, bank[2][:, 0:P], so_lo, ALU.mult).then_inc(so2, 1)
                    dve.wait_ge(so2, k * SORT2 + 8)
                    dve.tensor_reduce(so_base, so_prod, AX_X, ALU.add).then_inc(so2, 1)
                    dve.wait_ge(so2, k * SORT2 + 9)
                    dve.tensor_tensor(so_posf, so_base, so_rank, ALU.add).then_inc(so2, 1)
                    dve.wait_ge(so2, k * SORT2 + 10)
                    dve.tensor_copy(so_pos[:, :], so_posf).then_inc(so2, 1)
                    dve.tensor_tensor(so_cum, so_cum, bank[3][0:NT, 0:P], ALU.add).then_inc(so2, 1)
                    dve.wait_ge(so2, k * SORT2 + SORT2)
                    dve.wait_ge(so_placed, k * 16 + 16)
                with dve.Fori(0, NK) as k:
                    dve.wait_ge(so3_ps, k + 1)
                    dve.tensor_copy(so_turn, bank[0][0:D + S, 0:P]).then_inc(so3, 1)
                    dve.tensor_copy(src_t[:, bass.ds(k, 1)], so_row[:, RS_SRC:RS_SRC + 1].bitcast(I32)
                                    ).then_inc(so3, 1)
                    dve.tensor_copy(dst_t[:, bass.ds(k, 1)], so_row[:, RS_DST:RS_DST + 1].bitcast(I32)
                                    ).then_inc(so3, 1)
                    dve.wait_ge(so3_out, k * 48 + 48)
                dve.wait_ge(so3, 3 * NK)
                dve.wait_ge(resorted, 32)

            dve.tensor_tensor(keep[:, :], d_prev[:, :], d_this[:, :], ALU.is_equal).then_inc(flags_done, 1)
            dve.wait_ge(flags_done, 1)
            dve.tensor_scalar(reset[:, :], keep[:, :], -1.0, FAR, ALU.add, ALU.mult).then_inc(flags_done, 1)

            def across(v, n, axis):
                if axis == 1:
                    return v.rearrange("p (k o) -> p k o", o=1).to_broadcast([P, v.shape[1], n])
                return v.rearrange("p (o k) -> p o k", o=1).to_broadcast([P, n, v.shape[1]])
            dve.tensor_copy(first_f[:, :], d_this[:, bass.ds(0, RP, RL)]).then_inc(find_step, 1)
            dve.tensor_scalar(tile_f[:, :], iota_row[:, 0:NT], float(P), None, ALU.mult).then_inc(find_step, 1)
            dve.wait_ge(find_step, 2)
            dve.tensor_tensor(rel_f[:, :, :], across(first_f[:, :], NT, 1), across(tile_f[:, :], RP, 2), ALU.subtract
                              ).then_inc(find_step, 1)
            dve.wait_ge(find_step, 3)
            for k in range(RP):
                if k >= 2:
                    dve.wait_ge(below_ps, k - 1)
                dve.tensor_tensor(flags[k % 2].rearrange("p (t m) -> p t m", t=NT),
                                  across(rel_f[:, k, :], P, 1), across(iota_row[:, :], NT, 2), ALU.is_le
                                  ).then_inc(below_ok, 1)
            dve.wait_ge(wth_ok, 1)
            dve.tensor_tensor(wt_l[:, :, :], wt[:, :, :], wt_h[:, :, :].bitcast(F32), ALU.subtract).then_inc(wtl_ok, 1)
            dve.wait_ge(b1e_ps, 1)
            dve.tensor_tensor(b1e[:, :], bank[6][0:D, 448:449], b1[:, :], ALU.add).then_inc(b1e_ok, 1)
            dve.wait_ge(below_ps, RP)
            dve.tensor_copy(count[:, :], bank[7][0:NT, 0:P]).then_inc(find_step, 1)
            dve.wait_ge(below_ps, RP + 1)
            dve.tensor_scalar(row_f[:, :], bank[7][:, P:P + NT], -1.0, 0.0, ALU.add, ALU.max).then_inc(find_step, 1)
            dve.wait_ge(find_step, 5)
            dve.tensor_copy(row_i[:, :], row_f[:, :]).then_inc(find_step, 1)

            def sh_remainder(part):
                dve.wait_ge(split_done, part + 1)
                dve.tensor_tensor(shf[:, :], shf[:, :], shp[:, :], ALU.subtract).then_inc(split_step, 1)

            dve.wait_ge(zeroed, 5)

            def run(c0, i=0):
                b, c = c0 % CR, c0 if isinstance(i, int) else i * CR + c0
                turn = (c0 // CR + 1) * 32
                dve.wait_ge(chunk_in[b], turn if isinstance(i, int) else i * 32 + turn)
                if not isinstance(c, int) or c >= 1:
                    dve.wait_ge(chunk_run, c)
                if not isinstance(c, int) or c >= 2:
                    dve.wait_ge(chunk_ps, c * 2 - 2)
                dve.tensor_tensor_scan(run_c[:, b, :], keep_c[:, b, :], ea_c[:, b, :], run_c[:, 1 - b, W - 1:W],
                                       ALU.mult, ALU.add).then_inc(chunk_run, 1)

            run(0)
            sh_remainder(0)
            run(1)
            sh_remainder(1)
            with dve.Fori(0, CL // 2) as i:
                for r in range(CR):
                    run(2 + r, i)

            dve.wait_ge(dst_rows_in, 16 * NT)
            for slot, op in enumerate((ALU.is_le, ALU.is_equal)):
                dve.tensor_tensor(flags[slot][:, 0:NT * RL].rearrange("p (t c) -> p t c", t=NT), dst_rows[:, :, :],
                                  across(node_i[:, :], RL, 1), op).then_inc(find_step, 1)
            dve.wait_ge(find_step, 8)
            rows = [flags[slot][:, 0:NT * RL].rearrange("p (t c) -> p t c", t=NT) for slot in range(2)]
            dve.tensor_reduce(within[:, :], rows[0], AX_X, ALU.add).then_inc(find_step, 1)
            dve.tensor_reduce(has[:, :], rows[1], AX_X, ALU.max).then_inc(ends_ok, 1)
            dve.wait_ge(find_step, 9)
            dve.tensor_scalar(end_f[:, :], row_f[:, :], float(RL), -1.0, ALU.mult, ALU.add).then_inc(find_step, 1)
            dve.wait_ge(find_step, 10)
            dve.tensor_tensor(end_f[:, :], end_f[:, :], within[:, :], ALU.add).then_inc(find_step, 1)
            dve.wait_ge(find_step, 11)
            dve.tensor_scalar(end_f[:, :], end_f[:, :], 0.0, None, ALU.max).then_inc(find_step, 1)
            dve.wait_ge(find_step, 12)
            dve.tensor_copy(end_i[:, :], end_f[:, :]).then_inc(ends_ok, 1)

            with dve.Fori(CL // 2, CL) as i:
                for r in range(CR):
                    run(2 + r, i)
            for c in range(2 + CL * CR, NC):
                run(c)

            dve.wait_ge(x_in, 16)
            dve.wait_ge(ends_ok, 2)
            dve.wait_ge(b1e_ok, 1)

            def mask(n, lo, w):
                tiles = slice(tiles_of(n)[0], tiles_of(n)[-1] + 1)
                dve.wait_ge(agg_in[n], 16 * len(tiles_of(n)))
                dve.tensor_tensor(x_r[:, tiles, D:2 * D], x_r[:, tiles, D:2 * D], across(has[:, tiles], D, 1), ALU.mult
                                  ).then_inc(masked, 1)

            def swish_1(n, lo, w):
                dve.wait_ge(h1_sig, n + 1)
                dve.scalar_tensor_tensor(out=h_t[:, lo:lo + w], in0=bank[n][0:D, 0:w], scalar=b1e[:, :],
                                         in1=sg_t[:, lo:lo + w], op0=ALU.add, op1=ALU.mult).then_inc(h1_ok, 1)

            def swish_2(n, lo, w):
                dve.wait_ge(h2_sig, n + 1)
                dve.scalar_tensor_tensor(out=h_t[:, lo:lo + w], in0=bank[n][0:D, 0:w], scalar=b2[:, :],
                                         in1=sg_t[:, lo:lo + w], op0=ALU.add, op1=ALU.mult).then_inc(h2_ok, 1)

            def residual(n, lo, w):
                dve.wait_ge(h2_ok, n + 1)
                dve.tensor_tensor(h_t[:, lo:lo + w], h_t[:, lo:lo + w], xa_t[0:D, lo:lo + w], ALU.add
                                  ).then_inc(res_ok, 1)
            staggered(mask, None, swish_1, swish_2, residual)
            for b, tiles in ROW_TILES:
                dve.wait_ge(rr_ps, b + 1)
                dve.tensor_copy(r_r[:, tiles[0]:tiles[-1] + 1, :].rearrange("p t d -> p (t d)"),
                                bank[b][:, 0:len(tiles) * D]).then_inc(rr_ok, 1)

            def spread_cols(v):
                return v[:, :].rearrange("p (t o) -> p t o", o=1).to_broadcast([P, NT, D])

            def layer_norm(dst, ok, base):
                dve.tensor_reduce(mean[:, :], r_r[:, :, :], AX_X, ALU.add).then_inc(ln, 1)
                dve.wait_ge(ln, base + 1)
                dve.tensor_scalar(mean[:, :], mean[:, :], 1.0 / D, None, ALU.mult).then_inc(ln, 1)
                dve.wait_ge(ln, base + 2)
                dve.tensor_tensor(r_r[:, :, :], r_r[:, :, :], spread_cols(mean), ALU.subtract).then_inc(ln, 1)
                dve.wait_ge(ln, base + 3)
                dve.tensor_tensor(sq_r, r_r[:, :, :], r_r[:, :, :], ALU.mult).then_inc(ln, 1)
                dve.wait_ge(ln, base + 4)
                dve.tensor_reduce(var[:, :], sq_r, AX_X, ALU.add).then_inc(ln, 1)
                dve.wait_ge(ln_sqrt, base // LN_STEPS + 1)
                dve.reciprocal(rstd[:, :], rstd[:, :]).then_inc(ln, 1)
                dve.wait_ge(ln, base + LN_STEPS)
                dve.tensor_tensor(dst, r_r[:, :, :], spread_cols(rstd), ALU.mult).then_inc(ok, 1)
            dve.wait_ge(rr_ok, len(ROW_TILES))
            layer_norm(x1_r[:, :, :], x1_ok, 0)

            def outer(g, b, j):
                dve.wait_ge(shb_ps, g * NJ + (j + 1))
                if j == 0:
                    dve.wait_ge(xt_ok, g + 1)
                    used(dve, acc_ps, g)
                dve.tensor_tensor(z[:, j, :], bank[2 + (NJ * b + j) % 2][:, :], xt[:, b, :], ALU.mult
                                  ).then_inc(z_ok, 1)

            def outer_low(g, b, j):
                dve.wait_ge(zh_ok, g * NJ + (j + 1))
                rows = slice(0, P) if j < 4 else slice(D, P)
                low = z_l[:, b, j, :] if j < 4 else z_h[rows, b, j, :]
                dve.tensor_tensor(low, z[rows, j, :], z_h[rows, b, j, :].bitcast(F32), ALU.subtract
                                  ).then_inc(zl_ok, 1)

            def hidden_low(g, b):
                dve.wait_ge(hid_ok, g * 2 + 2)
                if not isinstance(g, int) or g >= 1:
                    dve.wait_ge(wv_ps, g)
                dve.tensor_tensor(hid_l[:, :], hid[:, :], hid_h[:, :].bitcast(F32), ALU.subtract
                                  ).then_inc(hidl_ok, 1)

            def key_query(g, b):
                dve.wait_ge(wk_ps, g + 1)
                dve.wait_ge(qt_ok, g + 1)
                used(dve, kq_ok, g)
                dve.scalar_tensor_tensor(out=qt[:, b, :], in0=ps_xw[:, :], scalar=b2k[:, :], in1=qt[:, b, :],
                                         op0=ALU.add, op1=ALU.mult).then_inc(wkq_ok, 1)

            def weigh(g, b):
                dve.wait_ge(acc_ps, g + 1)
                dve.wait_ge(wkq_ok, g + 1)
                used(dve, att_ps, g)
                dve.tensor_tensor(kq[:, b, :], ps_k[:, :], qt[:, b, :], ALU.mult).then_inc(kq_ok, 1)
                dve.wait_ge(wv_ok, g + 1)
                dve.tensor_tensor(val[:, b, :], ps_v[:, :], wv[:, b, :], ALU.mult).then_inc(val_ok, 1)

            def maxima(g, b):
                dve.wait_ge(att_ps, g + 1)
                arrived(dve, rs_in, g, b)
                if not isinstance(g, int) or g >= 1:
                    dve.wait_ge(mx_ok, g)
                    dve.wait_ge(dm_ok, g * 2)
                else:
                    dve.wait_ge(zeroed, 8)
                dve.tensor_tensor_scan(mx[:, b, :], rs[:, b, :], ps_qa[:, :], mx[:, 1 - b, G - 1:G],
                                       ALU.add, ALU.max).then_inc(mx_ok, 1)

            def below(g, b):
                dve.wait_ge(mx_ok, g + 1)
                used(dve, ex_ok, g)
                dve.tensor_tensor(ex[:, b, :], ps_qa[:, :], mx[:, b, :], ALU.subtract).then_inc(am_ok, 1)

            def weigh_values(g, b):
                dve.wait_ge(ex_ok, g + 1)
                dve.wait_ge(val_ok, g + 1)
                dve.tensor_tensor(val[:, b, :], val[:, b, :], ex[:, b, :], ALU.mult).then_inc(ev_ok, 1)

            def sum_values(g, b):
                dve.wait_ge(ev_ok, g + 1)
                dve.wait_ge(dec_ok, g + 1)
                if not isinstance(g, int) or g >= 1:
                    dve.wait_ge(num_ok, g)
                used(dve, row_ps, g, 2)
                dve.tensor_tensor_scan(num[:, b, :], dm[:, b, :], val[:, b, :], num[:, 1 - b, G - 1:G],
                                       ALU.mult, ALU.add).then_inc(num_ok, 1)

            def sum_exponents(g, b):
                if not isinstance(g, int) or g >= 1:
                    dve.wait_ge(den_ok, g)
                dve.tensor_tensor_scan(den[:, b, :], dm[:, b, :], ex[:, b, :], den[:, 1 - b, G - 1:G],
                                       ALU.mult, ALU.add).then_inc(den_ok, 1)

            def body(t, b, q):
                if live(t - 1):
                    weigh(t - 1, 1 - b)
                if live(t + 1):
                    outer(t + 1, 1 - b, 0)
                if live(t - 2):
                    weigh_values(t - 2, b)
                if live(t + 1):
                    outer(t + 1, 1 - b, 1)
                    hidden_low(t + 1, 1 - b)
                    outer_low(t + 1, 1 - b, 0)
                if live(t - 2):
                    sum_values(t - 2, b)
                if live(t + 1):
                    outer_low(t + 1, 1 - b, 1)
                    outer(t + 1, 1 - b, 2)
                    key_query(t + 1, 1 - b)
                if live(t - 2):
                    sum_exponents(t - 2, b)
                if live(t + 1):
                    outer_low(t + 1, 1 - b, 2)
                    outer(t + 1, 1 - b, 3)
                if live(t - 1):
                    maxima(t - 1, 1 - b)
                if live(t + 1):
                    outer(t + 1, 1 - b, 4)
                    outer_low(t + 1, 1 - b, 3)
                if live(t - 1):
                    below(t - 1, 1 - b)
                if live(t + 1):
                    outer_low(t + 1, 1 - b, 4)
            steps(dve, body)

            def divide(n, lo, w):
                tiles, base = slice(tiles_of(n)[0], tiles_of(n)[-1] + 1), 4 * n
                dve.wait_ge(nrow_in[n], 16 * len(tiles_of(n)))
                dve.tensor_tensor(end_rows[:, tiles, :], end_rows[:, tiles, :], across(has[:, tiles], RW, 1), ALU.mult
                                  ).then_inc(upd_step, 1)
                dve.wait_ge(upd_step, base + 1)
                dve.tensor_scalar(rden[:, tiles, :], end_rows[:, tiles, O:RW], 1e-16, None, ALU.add
                                  ).then_inc(upd_step, 1)
                dve.wait_ge(upd_step, base + 2)
                dve.reciprocal(rden[:, tiles, :], rden[:, tiles, :]).then_inc(upd_step, 1)
                dve.wait_ge(upd_step, base + 3)
                heads = end_rows[:, tiles, 0:O].rearrange("p t (h d) -> p t h d", h=H)
                dve.tensor_tensor(heads, heads, rden[:, tiles, :].rearrange("p t (h o) -> p t h o", o=1)
                                  .to_broadcast([P, len(tiles_of(n)), H, DH]), ALU.mult).then_inc(upd_step, 1)

            def layer_out(n, lo, w):
                dve.wait_ge(o_ps, n + 1)
                dve.tensor_copy(h_t[:, lo:lo + w], bank[n][0:D, 0:w]).then_inc(o_ok, 1)
            staggered(divide, None, layer_out)
            dve.wait_ge(o_ok, len(NODE_BLOCKS))
            dve.tensor_reduce(bnc[:, 0:1], h_t[:, 0:N], AX_X, ALU.add).then_inc(bn, 1)
            dve.wait_ge(bn, 1)
            dve.tensor_scalar(bnc[:, 1:2], bnc[:, 0:1], 1.0 / N, None, ALU.mult).then_inc(bn, 1)
            dve.wait_ge(bn, 2)
            dve.tensor_scalar(h_t[:, :], h_t[:, :], bnc[:, 1:2], None, ALU.subtract).then_inc(bn, 1)
            dve.wait_ge(bn, 3)
            dve.tensor_tensor(sg_t[:, :], h_t[:, :], h_t[:, :], ALU.mult).then_inc(bn, 1)
            dve.wait_ge(bn, 4)
            dve.tensor_reduce(bnc[:, 2:3], sg_t[:, 0:N], AX_X, ALU.add).then_inc(bn, 1)
            dve.wait_ge(bn_sqrt, 1)
            dve.reciprocal(bnc[:, 4:5], bnc[:, 3:4]).then_inc(bn, 1)
            dve.wait_ge(bn, 6)
            dve.tensor_tensor(bnc[:, 5:6], bnc[:, 4:5], gamma[:, :], ALU.mult).then_inc(bn, 1)
            dve.wait_ge(bn, 7)
            dve.tensor_scalar(h_t[:, :], h_t[:, :], bnc[:, 5:6], beta[:, :], ALU.mult, ALU.add).then_inc(bn, 1)
            for b, tiles in ROW_TILES:
                dve.wait_ge(y_ps, b + 1)
                dve.tensor_tensor(r_r[:, tiles[0]:tiles[-1] + 1, :],
                                  bank[b][:, 0:len(tiles) * D].rearrange("p (t d) -> p t d", d=D),
                                  x1_r[:, tiles[0]:tiles[-1] + 1, :], ALU.add).then_inc(rr_ok, 1)
            dve.wait_ge(rr_ok, 2 * len(ROW_TILES))
            layer_norm(r_r[:, :, :], out_ok, LN_STEPS)


def kernel(**inputs):
    import numpy as _np
    import concourse.bacc as _bacc
    from concourse import mybir as _mybir
    from concourse.bass_utils import run_bass_kernel_spmd as _run

    v = {k: _np.asarray(x) for k, x in inputs.items()}
    l1 = lambda name: v["L1_gnn_" + name]
    pad = EP - E
    src = _np.pad(v["src"], (0, pad))
    dst = _np.pad(v["dst"], (0, pad), constant_values=N)
    ea = _np.pad(v["edge_attr_64"], ((0, pad), (0, 0)))
    sh = _np.pad(v["edge_attr_9"], ((0, pad), (0, 0)))
    k, m = _np.arange(P)[:, None], _np.arange(P)[None, :]
    s27 = _np.arange(SP3)[:, None] % S
    col = _np.arange(NJ * P)[None, :]
    arrays = {
        "x": _np.pad(v["x"], ((0, NP - N), (0, 0))),
        "src_t": src.reshape(NK, P).T, "dst_t": dst.reshape(NK, P).T,
        "dst_lin": _np.pad(dst, (1, 0), constant_values=-1),
        "ea_rows": ea, "sh_rows": sh, "src_col": src[:, None], "dst_col": dst[:, None],
        "ea_t": ea.T, "sh_t": sh.T,
        "c_k": l1("Cqk").transpose(1, 0, 2).reshape(S * D, O), "c_v": l1("Cv").transpose(1, 0, 2).reshape(S * D, O),
        "k_w1": l1("k_w1"), "v_w1": l1("v_w1"), "k_w2": l1("k_w2"), "v_w2": l1("v_w2"),
        "k_b1": l1("k_b1")[:, None], "v_b1": l1("v_b1")[:, None],
        "k_b2": l1("k_b2")[:, None], "v_b2": l1("v_b2")[:, None],
        "w1": v["L0_gnn_W1"], "b1": v["L0_gnn_b1"][:, None], "u0": v["L0_gnn_u"][0][:, None],
        "w2": v["L0_gnn_W2"], "b2": v["L0_gnn_b2"][:, None],
        "wq": l1("Wq"), "wout": l1("W_out"), "wself": l1("W_self"),
        "gamma": l1("gamma")[:, None], "beta": l1("beta")[:, None],
        "ident": (k == m).astype(_np.float32),
        "headones": (k // DH == m // DH).astype(_np.float32),
        "iota_row": (m + 0 * k).astype(_np.float32),
        "node_id": (k + P * _np.arange(NT)[None, :]).astype(_np.int32),
        "upper": (k < m).astype(_np.float32), "lower": (m < k).astype(_np.float32),
        "sel": (s27 == _np.minimum(2 * (col // P) + col % P // D, S - 1)).astype(_np.float32),
    }
    nc = _bacc.Bacc("TRN2", target_bir_lowering=False, num_devices=1)
    feed, aps = {}, {}
    for name, x in arrays.items():
        x = _np.ascontiguousarray(x)
        feed[f"in_{name}"] = x
        aps[name] = nc.dram_tensor(f"in_{name}", x.shape, _mybir.dt.from_np(x.dtype), kind="ExternalInput").ap()
    out = nc.dram_tensor("out_x", (NP, D), _mybir.dt.float32, kind="ExternalOutput").ap()
    gnn_two_layers(nc, aps, out)
    r = _run(nc, [feed], core_ids=[0])
    return r.results[0]["out_x"][0:N]
```
